# Optimizing a Trainium2 kernel written in Bass

```python
import numpy as np
import jax
import jax.numpy as jnp

def _softmax(x, axis=-1):
    return jax.nn.softmax(x, axis=axis)

def _gelu(x):
    return jax.nn.gelu(x, approximate=True)

def _silu(x):
    return jax.nn.silu(x)

def _sigmoid(x):
    return jax.nn.sigmoid(x)

def _layernorm(x, axis=-1, eps=1e-05):
    m = jnp.mean(x, axis=axis, keepdims=True)
    v = jnp.var(x, axis=axis, keepdims=True)
    return (x - m) / jnp.sqrt(v + eps)

def _scatter_add(tgt, idx, src, axis=0):
    return tgt.at[idx].add(src)

def _segment_sum(src, seg, n):
    return jax.ops.segment_sum(src, seg, n)
kernel_name = 'mk_gnn_ffn_d2_gnn_r32_dd7b93'

def setup_inputs(seed: int=0):
    np.random.seed(seed)
    _w = jnp.asarray

    def _rec_inputs():
        import jax
        import jax.numpy as jnp
        _gk = jax.random.key(seed)
        x = -8.776e-05 + 1 * jax.random.normal(jax.random.fold_in(_gk, 1), (625, 256), jnp.float32)
        _s = jax.random.randint(jax.random.fold_in(_gk, 2), (10000,), 0, 625, jnp.int32)
        _d = jax.random.randint(jax.random.fold_in(_gk, 3), (10000,), 0, 625, jnp.int32)
        _loop = jnp.arange(625, dtype=jnp.int32)
        src = jnp.concatenate([_s, _d, _loop])
        dst = jnp.concatenate([_d, _s, _loop])
        _o = jnp.argsort(dst, stable=True)
        src = src[_o]
        dst = dst[_o]
        edge_type_8 = jax.random.randint(jax.random.fold_in(_gk, 12), (20625,), 0, 8, jnp.int32)
        return (x, src, dst, edge_type_8)
    x, src, dst, edge_type_8 = _rec_inputs()

    def _L0_gnn_setup():
        import jax, jax.numpy as jnp
        import numpy as np
        N_NODES = 625
        N_EDGES = 10000
        D = 256
        R = 8

        def _xavier(key, shape):
            fan_in, fan_out = (shape[-2], shape[-1])
            bound = float(np.sqrt(6.0 / (fan_in + fan_out)))
            return jax.random.uniform(key, shape, jnp.float32, -bound, bound)

        def _rgcn_layer(x, W, self_w, b, src, dst, edge_type, num_nodes):
            xW = jnp.einsum('ni,rio->rno', x, W)
            msg = xW[edge_type, src]
            agg = jax.ops.segment_sum(msg, dst, num_segments=num_nodes)
            return agg + x @ self_w + b
        key = jax.random.key(seed)
        ks = jax.random.split(key, 10)
        x = jax.random.normal(ks[0], (N_NODES, D), jnp.float32)
        edge_index = jax.random.randint(ks[1], (2, N_EDGES), 0, N_NODES)
        edge_type = jax.random.randint(ks[2], (N_EDGES,), 0, R)
        W1 = _xavier(ks[3], (R, D, D))
        self_w1 = _xavier(ks[4], (D, D))
        b1 = jnp.zeros((D,), jnp.float32)
        W2 = _xavier(ks[5], (R, D, D))
        self_w2 = _xavier(ks[6], (D, D))
        b2 = jnp.zeros((D,), jnp.float32)
        return {'x': x, 'W1': W1, 'self_w1': self_w1, 'b1': b1, 'W2': W2, 'self_w2': self_w2, 'b2': b2, 'edge_index': edge_index, 'edge_type': edge_type}
    _L0_gnn_all = _L0_gnn_setup()
    _L0_gnn_in = {k: v for k, v in _L0_gnn_all.items() if k in ('W1', 'self_w1', 'b1', 'W2', 'self_w2', 'b2')}
    del _L0_gnn_all

    def _L0_ffn_setup():
        import jax, jax.numpy as jnp
        import numpy as np
        B, S, D, H, E, K = (8, 256, 256, 1024, 8, 2)
        key = jax.random.key(seed)
        ks = jax.random.split(key, 7)
        s_in = 1.0 / np.sqrt(D)
        s_hid = 1.0 / np.sqrt(H)
        return {'x': jax.random.normal(ks[0], (B, S, D), dtype=jnp.float32), 'Wg': jax.random.uniform(ks[1], (E, D), jnp.float32, -s_in, s_in), 'bg': jax.random.uniform(ks[2], (E,), jnp.float32, -s_in, s_in), 'W1': jax.random.uniform(ks[3], (E, H, D), jnp.float32, -s_in, s_in), 'b1': jax.random.uniform(ks[4], (E, H), jnp.float32, -s_in, s_in), 'W2': jax.random.uniform(ks[5], (E, D, H), jnp.float32, -s_hid, s_hid), 'b2': jax.random.uniform(ks[6], (E, D), jnp.float32, -s_hid, s_hid)}
    _L0_ffn_all = _L0_ffn_setup()
    _L0_ffn_in = {k: v for k, v in _L0_ffn_all.items() if k in ('Wg', 'bg', 'W1', 'b1', 'W2', 'b2')}
    del _L0_ffn_all

    def _L1_gnn_setup():
        import jax, jax.numpy as jnp
        import numpy as np
        N = 50000
        E = 25000
        IN = 256
        HD = 4
        D = 64
        key = jax.random.key(seed)
        k1, k2, k3, k4, k5 = jax.random.split(key, 5)
        h = jax.random.normal(k1, (N, IN), dtype=jnp.float32)
        edge_index = jax.random.randint(k2, (2, E), 0, N)
        W = jax.random.normal(k3, (IN, HD * D), dtype=jnp.float32) * (1.0 / np.sqrt(IN))
        a_src = jax.random.normal(k4, (HD, D), dtype=jnp.float32) * 0.1
        a_dst = jax.random.normal(k5, (HD, D), dtype=jnp.float32) * 0.1
        return {'h': h, 'edge_index': edge_index, 'W': W, 'a_src': a_src, 'a_dst': a_dst}
    _L1_gnn_all = _L1_gnn_setup()
    _L1_gnn_in = {k: v for k, v in _L1_gnn_all.items() if k in ('W', 'a_src', 'a_dst')}
    del _L1_gnn_all

    def _L1_ffn_setup():
        import jax, jax.numpy as jnp
        import numpy as np
        DIM = 256
        H = 8
        D = 64
        G = 64
        INNER = H * D
        SCALE = D ** (-0.5)
        key = jax.random.key(seed)
        ks = jax.random.split(key, 12)
        B, N = (4, 512)
        x = jax.random.normal(ks[0], (B, N, DIM), dtype=jnp.float32)
        s = lambda fan_in: 1.0 / np.sqrt(fan_in)
        W_fx = jax.random.normal(ks[1], (DIM, INNER), dtype=jnp.float32) * s(DIM)
        b_fx = jnp.zeros((INNER,), dtype=jnp.float32)
        W_x = jax.random.normal(ks[2], (DIM, INNER), dtype=jnp.float32) * s(DIM)
        b_x = jnp.zeros((INNER,), dtype=jnp.float32)
        A = jax.random.normal(ks[3], (G, D), dtype=jnp.float32)
        Q, _ = jnp.linalg.qr(A.T)
        W_slice = Q[:, :G].astype(jnp.float32)
        b_slice = jnp.zeros((G,), dtype=jnp.float32)
        W_q = jax.random.normal(ks[4], (D, D), dtype=jnp.float32) * s(D)
        W_k = jax.random.normal(ks[5], (D, D), dtype=jnp.float32) * s(D)
        W_v = jax.random.normal(ks[6], (D, D), dtype=jnp.float32) * s(D)
        W_out = jax.random.normal(ks[7], (INNER, DIM), dtype=jnp.float32) * s(INNER)
        b_out = jnp.zeros((DIM,), dtype=jnp.float32)
        temperature = jnp.ones((1, H, 1, 1), dtype=jnp.float32) * 0.5
        return {'x': x, 'W_fx': W_fx, 'b_fx': b_fx, 'W_x': W_x, 'b_x': b_x, 'W_slice': W_slice, 'b_slice': b_slice, 'W_q': W_q, 'W_k': W_k, 'W_v': W_v, 'W_out': W_out, 'b_out': b_out, 'temperature': temperature}
    _L1_ffn_all = _L1_ffn_setup()
    _L1_ffn_in = {k: v for k, v in _L1_ffn_all.items() if k in ('W_fx', 'b_fx', 'W_x', 'b_x', 'W_slice', 'b_slice', 'W_q', 'W_k', 'W_v', 'W_out', 'b_out', 'temperature')}
    del _L1_ffn_all
    return {'x': x, 'src': src, 'dst': dst, 'edge_type_8': edge_type_8, 'L0_gnn_W1': _L0_gnn_in['W1'], 'L0_gnn_self_w1': _L0_gnn_in['self_w1'], 'L0_gnn_b1': _L0_gnn_in['b1'], 'L0_gnn_W2': _L0_gnn_in['W2'], 'L0_gnn_self_w2': _L0_gnn_in['self_w2'], 'L0_gnn_b2': _L0_gnn_in['b2'], 'L0_ffn_Wg': _L0_ffn_in['Wg'], 'L0_ffn_bg': _L0_ffn_in['bg'], 'L0_ffn_W1': _L0_ffn_in['W1'], 'L0_ffn_b1': _L0_ffn_in['b1'], 'L0_ffn_W2': _L0_ffn_in['W2'], 'L0_ffn_b2': _L0_ffn_in['b2'], 'L1_gnn_W': _L1_gnn_in['W'], 'L1_gnn_a_src': _L1_gnn_in['a_src'], 'L1_gnn_a_dst': _L1_gnn_in['a_dst'], 'L1_ffn_W_fx': _L1_ffn_in['W_fx'], 'L1_ffn_b_fx': _L1_ffn_in['b_fx'], 'L1_ffn_W_x': _L1_ffn_in['W_x'], 'L1_ffn_b_x': _L1_ffn_in['b_x'], 'L1_ffn_W_slice': _L1_ffn_in['W_slice'], 'L1_ffn_b_slice': _L1_ffn_in['b_slice'], 'L1_ffn_W_q': _L1_ffn_in['W_q'], 'L1_ffn_W_k': _L1_ffn_in['W_k'], 'L1_ffn_W_v': _L1_ffn_in['W_v'], 'L1_ffn_W_out': _L1_ffn_in['W_out'], 'L1_ffn_b_out': _L1_ffn_in['b_out'], 'L1_ffn_temperature': _L1_ffn_in['temperature']}

def reference(x, src, dst, edge_type_8, L0_gnn_W1, L0_gnn_self_w1, L0_gnn_b1, L0_gnn_W2, L0_gnn_self_w2, L0_gnn_b2, L0_ffn_Wg, L0_ffn_bg, L0_ffn_W1, L0_ffn_b1, L0_ffn_W2, L0_ffn_b2, L1_gnn_W, L1_gnn_a_src, L1_gnn_a_dst, L1_ffn_W_fx, L1_ffn_b_fx, L1_ffn_W_x, L1_ffn_b_x, L1_ffn_W_slice, L1_ffn_b_slice, L1_ffn_W_q, L1_ffn_W_k, L1_ffn_W_v, L1_ffn_W_out, L1_ffn_b_out, L1_ffn_temperature):
    import jax
    import jax.numpy as jnp

    def _L0_gnn_ref(x, W1, self_w1, b1, W2, self_w2, b2, edge_index, edge_type):
        import jax, jax.numpy as jnp
        import numpy as np
        N_NODES = 625
        N_EDGES = 10000
        D = 256
        R = 8

        def _xavier(key, shape):
            fan_in, fan_out = (shape[-2], shape[-1])
            bound = float(np.sqrt(6.0 / (fan_in + fan_out)))
            return jax.random.uniform(key, shape, jnp.float32, -bound, bound)

        def _rgcn_layer(x, W, self_w, b, src, dst, edge_type, num_nodes):
            xW = jnp.einsum('ni,rio->rno', x, W)
            msg = xW[edge_type, src]
            agg = jax.ops.segment_sum(msg, dst, num_segments=num_nodes)
            return agg + x @ self_w + b
        src, dst = (edge_index[0], edge_index[1])
        h = _rgcn_layer(x, W1, self_w1, b1, src, dst, edge_type, N_NODES)
        h = jax.nn.relu(h)
        out = _rgcn_layer(h, W2, self_w2, b2, src, dst, edge_type, N_NODES)
        return out

    def _L0_ffn_ref(x, Wg, bg, W1, b1, W2, b2):
        import jax, jax.numpy as jnp
        import numpy as np
        B, S, D, H, E, K = (8, 256, 256, 1024, 8, 2)
        gate_scores = jnp.einsum('bsd,ed->bse', x, Wg) + bg
        topk_scores, topk_idx = jax.lax.top_k(gate_scores, K)
        topk_probs = jax.nn.softmax(topk_scores, axis=-1)
        combine = jnp.sum(topk_probs[..., None] * jax.nn.one_hot(topk_idx, E, dtype=x.dtype), axis=-2)
        out = jnp.zeros_like(x)
        for e in range(E):
            h = jax.nn.relu(jnp.einsum('bsd,hd->bsh', x, W1[e]) + b1[e])
            y = jnp.einsum('bsh,dh->bsd', h, W2[e]) + b2[e]
            out = out + combine[..., e:e + 1] * y
        return out

    def _L1_gnn_ref(h, edge_index, W, a_src, a_dst):
        import jax, jax.numpy as jnp
        import numpy as np
        N = 50000
        E = 25000
        IN = 256
        HD = 4
        D = 64
        n = h.shape[0]
        src, dst = (edge_index[0], edge_index[1])
        hp = (h @ W).reshape(n, HD, D)
        e_src = jnp.einsum('ehd,hd->eh', hp[src], a_src)
        e_dst = jnp.einsum('ehd,hd->eh', hp[dst], a_dst)
        e = jax.nn.leaky_relu(e_src + e_dst, negative_slope=0.2)
        e_max = jax.ops.segment_max(e, dst, num_segments=n)
        ex = jnp.exp(e - e_max[dst])
        e_sum = jax.ops.segment_sum(ex, dst, num_segments=n)
        alpha = ex / (e_sum[dst] + 1e-16)
        msg = hp[src] * alpha[..., None]
        out = jax.ops.segment_sum(msg, dst, num_segments=n)
        return out.reshape(n, HD * D)

    def _L1_ffn_ref(x, W_fx, b_fx, W_x, b_x, W_slice, b_slice, W_q, W_k, W_v, W_out, b_out, temperature):
        import jax, jax.numpy as jnp
        import numpy as np
        DIM = 256
        H = 8
        D = 64
        G = 64
        INNER = H * D
        SCALE = D ** (-0.5)
        B, N, _ = x.shape
        fx_mid = (x @ W_fx + b_fx).reshape(B, N, H, D).transpose(0, 2, 1, 3)
        x_mid = (x @ W_x + b_x).reshape(B, N, H, D).transpose(0, 2, 1, 3)
        temp = jnp.clip(temperature, 0.1, 5.0)
        slice_weights = jax.nn.softmax((x_mid @ W_slice + b_slice) / temp, axis=-1)
        slice_norm = slice_weights.sum(axis=2)
        slice_token = jnp.einsum('bhnc,bhng->bhgc', fx_mid, slice_weights)
        slice_token = slice_token / (slice_norm[..., None] + 1e-05)
        q = slice_token @ W_q
        k = slice_token @ W_k
        v = slice_token @ W_v
        attn = jax.nn.softmax(jnp.einsum('bhgc,bhkc->bhgk', q, k) * SCALE, axis=-1)
        out_slice = jnp.einsum('bhgk,bhkc->bhgc', attn, v)
        out_x = jnp.einsum('bhgc,bhng->bhnc', out_slice, slice_weights)
        out_x = out_x.transpose(0, 2, 1, 3).reshape(B, N, INNER)
        return out_x @ W_out + b_out
    edge_index = jnp.stack([src, dst])
    x = x + _L0_gnn_ref(_layernorm(x, axis=-1), L0_gnn_W1, L0_gnn_self_w1, L0_gnn_b1, L0_gnn_W2, L0_gnn_self_w2, L0_gnn_b2, edge_index, edge_type_8)
    x = x + _L0_ffn_ref(_layernorm(x, axis=-1)[None], L0_ffn_Wg, L0_ffn_bg, L0_ffn_W1, L0_ffn_b1, L0_ffn_W2, L0_ffn_b2)[0]
    x = x + _L1_gnn_ref(_layernorm(x, axis=-1), edge_index, L1_gnn_W, L1_gnn_a_src, L1_gnn_a_dst)
    x = x + _L1_ffn_ref(_layernorm(x, axis=-1)[None], L1_ffn_W_fx, L1_ffn_b_fx, L1_ffn_W_x, L1_ffn_b_x, L1_ffn_W_slice, L1_ffn_b_slice, L1_ffn_W_q, L1_ffn_W_k, L1_ffn_W_v, L1_ffn_W_out, L1_ffn_b_out, L1_ffn_temperature)[0]
    return x

_drawn_inputs = setup_inputs


def setup_inputs(seed=0):
    import zlib

    import numpy as np

    out = dict(_drawn_inputs(seed))
    spreads = {'L0_gnn_b1': (0.0, 0.4),
     'L0_gnn_b2': (0.0, 0.8),
     'L1_ffn_b_fx': (0.0, 0.8),
     'L1_ffn_b_x': (0.0, 0.8),
     'L1_ffn_b_slice': (0.0, 0.8),
     'L1_ffn_b_out': (0.0, 2.0),
     'L1_ffn_temperature': (0.5, 0.6)}
    factors = {'L0_ffn_Wg': 8.0,
     'L0_ffn_bg': 8.0,
     'L0_ffn_W1': 8.0,
     'L0_ffn_b1': 8.0,
     'L0_ffn_W2': 8.0,
     'L0_ffn_b2': 8.0,
     'L1_gnn_W': 2.716,
     'L1_gnn_a_src': 8.0,
     'L1_gnn_a_dst': 8.0,
     'L1_ffn_W_fx': 3.028,
     'L1_ffn_W_x': 8.0,
     'L1_ffn_W_slice': 8.0,
     'L1_ffn_W_q': 8.0,
     'L1_ffn_W_k': 8.0,
     'L1_ffn_W_v': 2.771,
     'L1_ffn_W_out': 2.808}
    for name, (base, spread) in spreads.items():
        noise = np.random.default_rng([zlib.crc32(name.encode()), seed]).standard_normal(out[name].shape)
        drawn = base * np.exp(spread * noise) if base else spread * noise
        out[name] = jnp.asarray(drawn.astype(out[name].dtype))
    for name, factor in factors.items():
        out[name] = (out[name] * factor).astype(out[name].dtype)
    return out
```

```python
from collections import namedtuple
from contextlib import ExitStack

import concourse.bass as bass
from concourse import mybir

P = 128
F32 = mybir.dt.float32
F32R = mybir.dt.float32r
F16 = mybir.dt.float16
BF16 = mybir.dt.bfloat16
I32 = mybir.dt.int32
U32 = mybir.dt.uint32
ALU = mybir.AluOpType
ACT = mybir.ActivationFunctionType
AX = mybir.AxisListType

NODES, DIM, EDGES, TYPES = 625, 256, 20625, 8
CH = -(-NODES // P)
NP = CH * P
LAST = NODES - (CH - 1) * P
KD = DIM // P
HALF = NP // 2

TILES = 3
GE = TILES * P
GROUPS = -(-EDGES // GE)
FULL_ROWS = EDGES // GE
REST = EDGES - FULL_ROWS * GE
WIN = 16
KEYS = TYPES * WIN
WINDOWS = NP // WIN
OUTSIDE = 5000

EXPERTS, HID = 8, 1024
HB = HID // P
HRING = 4
HEADS1, HD1 = 4, 64
HEADS2, HD2, SLICES = 8, 64, 64
INNER = HEADS2 * HD2
IB = INNER // P
LN_EPS = 1e-5
NEG = -1e30


class Place:
    pass


def layout(nc):
    at = Place()
    at.pos = -(-nc.sbuf_base // 64) * 64
    size = {F32: 4, F32R: 4, F16: 2, BF16: 2, I32: 4, U32: 4}

    def put(name, shape, dt):
        n = size[dt]
        for s in shape[1:]:
            n *= s
        t = nc.alloc_sbuf_tensor_at(name, shape, dt, offset=at.pos)
        at.pos += -(-n // 64) * 64
        return t

    T = Place()
    T.X = put("X", [P, CH, DIM], F32)
    T.xn = put("xn", [P, CH, DIM], F32)
    T.xTh = put("xTh", [P, KD, NP], F32R)
    T.xTl = put("xTl", [P, KD, NP], F32R)
    T.stats = put("stats", [P, CH, 6], F32)
    T.mv = put("mv", [P, CH, 2], F32)
    T.std = put("std", [P, CH], F32)
    T.rstd = put("rstd", [P, CH], F32)
    T.eps = put("eps", [P, 1], F32)
    T.ident = put("ident", [P, P], F32)
    shared = at.pos

    T.A = put("A", [P, CH, TYPES, NP], F16)
    T.wh0 = put("wh0", [P, TYPES + 1, KD, DIM], F32R)
    T.wl0 = put("wl0", [P, TYPES + 1, KD, DIM], F32R)
    after_w0 = at.pos
    T.wh1 = put("wh1", [P, TYPES + 1, KD, DIM], F32R)
    T.wl1 = put("wl1", [P, TYPES + 1, KD, DIM], F32R)
    T.raw = put("raw", [P, TYPES + 1, KD, DIM], F32)
    T.xp = put("xp", [P, 3, CH, DIM], BF16)
    T.xr = put("xr", [P, CH, DIM], F32)
    T.b_bc = put("b_bc", [P, 2, DIM], F32)
    over = at.pos
    T.ei = put("ei", [GROUPS, 3, GE], I32)
    T.ef = put("ef", [GROUPS, 4, GE], F32)
    T.dvalid = T.ef[:, 3, :]
    T.dlim = put("dlim", [GROUPS, 4], F32)
    T.eT = put("eT", [P, 4, TILES, GROUPS], F32)
    T.oh = put("oh", [P, 2, TILES, NP], F16)
    T.ko = put("ko", [P, 2, TILES, KEYS], F16)
    T.iota = put("iota", [P, NP], F16)
    T.kiota = put("kiota", [P, KEYS], F16)
    T.add = put("add", [P, 2, CH * KEYS], F16)
    T.kgen = put("kgen", [P, 4, TILES * GROUPS], F32)
    T.w16 = put("w16", [P, 1], F32)
    T.lims = put("lims", [1, 2, GROUPS], F32)
    T.spanmax = put("spanmax", [1, 2], F32)
    T.bases = put("bases", [1, 64], I32)
    T.fits = put("fits", [1, 1], I32)
    end1 = at.pos
    at.pos = over
    T.yh = put("yh", [P, 2, NP], F32R)
    T.yl = put("yl", [P, 2, NP], F32R)
    T.C = put("C", [P, CH, NP], F32)
    end1 = max(end1, at.pos)
    assert end1 <= nc.sbuf_usable_end, end1
    c_pos = over + 2 * 2 * NP * 4

    at.pos = shared
    T.ewh0 = put("ewh0", [P, 2 * HID + HB * DIM], F32R)
    assert at.pos <= after_w0
    at.pos = shared + 2 * CH * TYPES * NP
    T.stg = put("stg", [P, 2, 2 * HID + HB * DIM], F32)
    assert at.pos <= after_w0
    T.ewl0 = put("ewl0", [P, 2 * HID + HB * DIM], F32R)
    T.ewh1 = put("ewh1", [P, 2 * HID + HB * DIM], F32R)
    T.ewl1 = put("ewl1", [P, 2 * HID + HB * DIM], F32R)
    assert at.pos <= over
    at.pos = shared + 16384
    T.ht = put("ht", [P, HRING, NP], F32)
    T.hh = put("hh", [P, HRING, NP], F32R)
    T.hl = put("hl", [P, HRING, NP], F32R)
    T.b1 = put("b1", [P, EXPERTS * HB], F32)
    T.b2 = put("b2", [EXPERTS, DIM], F32)
    assert at.pos <= shared + 2 * CH * TYPES * NP
    at.pos = c_pos + CH * NP * 4
    T.wg = put("wg", [P, 1, KD, EXPERTS], F32)
    T.bg = put("bg", [P, EXPERTS], F32)
    T.gate = put("gate", [P, CH, EXPERTS], F32)
    T.top = put("top", [P, CH, 8], F32)
    T.topi = put("topi", [P, CH, 8], U32)
    T.topf = put("topf", [P, CH, 8], F32)
    T.gp = put("gp", [P, 5, CH], F32)
    T.ctmp = put("ctmp", [P, CH, EXPERTS], F32)
    T.comb = put("comb", [P, CH, EXPERTS], F32)
    T.iota8 = put("iota8", [P, EXPERTS], F32)
    T.combT = put("combT", [EXPERTS, NP], F32)
    assert at.pos <= nc.sbuf_usable_end, at.pos

    at.pos = shared
    T.w3 = put("w3", [P, KD, DIM], F32)
    T.w3h = put("w3h", [P, KD, DIM], F32R)
    T.w3l = put("w3l", [P, KD, DIM], F32R)
    T.hp = put("hp", [P, CH, HEADS1, HD1 + 1], F32)
    T.hpT = put("hpT", [P, KD, NP], F32)
    T.asrc = put("asrc", [P, KD], F32)
    T.asrc_bc = put("asrc_bc", [P, KD, P], F32)
    T.adst = put("adst", [P, DIM], F32)
    T.edm = put("edm", [P, CH, DIM], F32)
    T.ed = put("ed", [P, CH, HEADS1], F32)
    T.es = put("es", [P, HEADS1, NP], F32)
    T.CT = put("CT", [P, CH, NP], F32)
    T.negm = put("negm", [P, CH, NP], F32)
    T.mtmp = put("mtmp", [P, 2, NP], F32)
    T.mes = put("mes", [P, CH, HEADS1], F32)
    T.tm = put("tm", [P, CH, HEADS1], F32)
    T.nm = put("nm", [P, CH, HEADS1], F32)
    T.t = put("t", [P, 2, NP], F32)
    T.lk = put("lk", [P, 2, NP], F32)
    T.ex = put("ex", [P, 2, NP], F32)
    T.pr = put("pr", [P, 2, NP], F32)
    T.pT = put("pT", [P, 2, NP], F32)
    T.den = put("den", [P, 2, CH], F32)
    T.o3 = put("o3", [P, CH, HD1], F32)
    assert at.pos <= c_pos, (at.pos, c_pos)

    T.wfx = put("wfx", [P, KD, INNER], F32)
    T.wfxh = put("wfxh", [P, KD, INNER], F32R)
    T.wfxl = put("wfxl", [P, KD, INNER], F32R)
    T.wx = put("wx", [P, KD, INNER], F32)
    T.wxh = put("wxh", [P, KD, INNER], F32R)
    T.wxl = put("wxl", [P, KD, INNER], F32R)
    T.wo = put("wo", [HD2, HEADS2, DIM], F32)
    T.wsl = put("wsl", [P, P], F32)
    T.wqkv = put("wqkv", [HD2, 3, HD2], F32)
    T.bfx = put("bfx", [P, INNER], F32)
    T.bx = put("bx", [P, IB], F32)
    T.bsl = put("bsl", [P, SLICES], F32)
    T.bout = put("bout", [P, DIM], F32)
    T.temp = put("temp", [P, 2, HEADS2], F32)
    T.ones = put("ones", [P, HD2], F32)
    assert at.pos <= c_pos, (at.pos, c_pos)
    at.pos = shared
    T.fx = put("fx", [P, CH, INNER], F32)
    T.xm = put("xm", [P, IB, NP], F32)
    T.lg = put("lg", [P, CH, INNER], F32)
    T.sm = put("sm", [P, 4, CH * HEADS2], F32)
    T.sw = put("sw", [P, CH, INNER], F32)
    T.swT = put("swT", [P, IB, NP], F32)
    T.nrm = put("nrm", [HD2, 2, INNER], F32)
    T.tok = put("tok", [HD2, INNER], F32)
    T.qk = put("qk", [HD2, 2, INNER], F32)
    T.v = put("v", [SLICES, INNER], F32)
    T.at = put("at", [SLICES, 3, INNER], F32)
    T.ats = put("ats", [SLICES, 3, HEADS2], F32)
    T.atT = put("atT", [SLICES, INNER], F32)
    T.osT = put("osT", [HD2, INNER], F32)
    T.M = put("M", [P, IB, DIM], F32)
    T.bounds = (at.pos,)
    return T


SEMAPHORES = """
x_zero x_in ei_set e_in b_in raw_in raw_free w_ready const_ready a_zero
ln_stats ln_aggr ln_std ln_rstd ln_out
tr_done xTh_ready xTl_ready
ef_ready ef_step eT_done eT_ready base_done base_step base_ready
oh_ready counts_done staged added key_step w16_step A_built
xp_step xr_step xp_ready y_done yh_ready yl_ready out_done acc_read layer_step c_step C_built
stg0_in stg1_in ewh_ready ewl_ready experts_done
gate_in gate_const gate_mm gate_step gate_exp comb_ready combT_done combT_ready b2_done b2_added eb_in
h_done ht_ready hh_ready hl_ready h_used yacc_done yacc_added
w3_in w3_ready asrc_ready hp_done hp_ready hpT_done hpT_ready es_done es_ready ed_step
ct_done ct_ready negm_ready mes_step m_ready t_ready lk_ready ex_ready pr_ready pT_done pT_ready agg_done
o3_step x3_ready
w4_in wfx_ready wx_ready w4_const fx_done fx_ready xm_done xm_ready temp_step lg_done lg_step sm_exp sw_ready
swT_done swT_ready tok_done tok_step tok_ready qkv_done qkv_ready al_done al_step al_exp at_ready
atT_done atT_ready osT_done osT_ready M_done M_ready out4_done y_ready stored
""".split()


def program(nc, D, out):
    T = layout(nc)
    with ExitStack() as ctx:
        S = namedtuple("Semaphores", SEMAPHORES)(*[ctx.enter_context(nc.semaphore(n)) for n in SEMAPHORES])
        PS = ctx.enter_context(nc.psum_tensor("PS", [P, 8, 512], F32))
        block = ctx.enter_context(nc.Block())
        R = Place()
        R.banks = PS
        R.flat = PS[:, :, :].rearrange("p b n -> p (b n)")

        @block.sync
        def _(sp):
            load_everything(sp, nc, S, T, D, out)

        @block.gpsimd
        def _(pool):
            pool_program(pool, nc, S, T)

        @block.scalar
        def _(act):
            act_program(act, nc, S, T, R)

        @block.tensor
        def _(pe):
            pe_program(pe, nc, S, T, R)

        @block.vector
        def _(dve):
            dve_program(dve, nc, S, T, R)


def chunks(t, c):
    return P if c < CH - 1 else LAST


def load_everything(sp, nc, S, T, D, out):
    full = (CH - 1) * P
    sp.wait_ge(S.x_zero, 1)
    sp.dma_start(T.X[:, 0:CH - 1, :], D.x[0:full, :].rearrange("(c p) d -> p c d", p=P)).then_inc(S.x_in, 16)
    sp.dma_start(T.X[0:LAST, CH - 1, :], D.x[full:NODES, :]).then_inc(S.x_in, 16)
    sp.wait_ge(S.ei_set, 1)
    for n, e in enumerate((D.dst, D.edge_type_8, D.src)):
        sp.dma_start(T.ei[0:FULL_ROWS, n, :], e[0:FULL_ROWS * GE].rearrange("(g e) -> g e", e=GE)).then_inc(S.e_in, 16)
        sp.dma_start(T.ei[FULL_ROWS:FULL_ROWS + 1, n, 0:REST],
                     e[FULL_ROWS * GE:EDGES].rearrange("(g e) -> g e", g=1)).then_inc(S.e_in, 16)
    for n, (w, self_w, b) in enumerate(((D.L0_gnn_W1, D.L0_gnn_self_w1, D.L0_gnn_b1),
                                        (D.L0_gnn_W2, D.L0_gnn_self_w2, D.L0_gnn_b2))):
        if n:
            sp.wait_ge(S.raw_free, 1)
        for k in range(KD):
            sp.dma_start(T.raw[:, 0:TYPES, k, :],
                         w[:, k * P:(k + 1) * P, :].rearrange("r p o -> p r o")).then_inc(S.raw_in, 16)
        sp.dma_start(T.raw[:, TYPES, :, :], self_w.rearrange("(k p) o -> p k o", p=P)).then_inc(S.raw_in, 16)
        sp.dma_start(T.b_bc[:, n, :], b.partition_broadcast(P)).then_inc(S.b_in, 16)
    sp.wait_ge(S.A_built, 1)
    sp.dma_start(T.wg[:, 0, :, :], D.wgT.rearrange("(k p) e -> p k e", p=P)).then_inc(S.gate_in, 16)
    sp.dma_start(T.bg[:, :], D.L0_ffn_bg.partition_broadcast(P)).then_inc(S.gate_in, 16)

    def expert(e):
        s = e % 2
        arrived = (S.stg0_in, S.stg1_in)[s]
        sp.dma_start(T.stg[:, s, 0:2 * HID].rearrange("p (k h) -> p k h", k=KD),
                     D.w1T[e].rearrange("(k p) h -> p k h", p=P)).then_inc(arrived, 16)
        sp.dma_start(T.stg[:, s, 2 * HID:].rearrange("p (b o) -> p b o", b=HB),
                     D.w2T[e].rearrange("(b p) o -> p b o", p=P)).then_inc(arrived, 16)

    sp.wait_ge(S.out_done, 2 + 2 * TYPES)
    expert(0)
    expert(1)
    sp.wait_ge(S.y_done, 4 * TYPES)
    sp.wait_ge(S.C_built, 1)
    sp.dma_start(T.b1[:, :], D.b1T).then_inc(S.eb_in, 16)
    sp.dma_start(T.b2[:, :], D.L0_ffn_b2).then_inc(S.eb_in, 16)
    for e in range(2, EXPERTS):
        sp.wait_ge(S.ewl_ready, e - 1)
        expert(e)
    sp.wait_ge(S.experts_done, 1)
    sp.dma_start(T.w3[:, :, :], D.L1_gnn_W.rearrange("(k p) o -> p k o", p=P)).then_inc(S.w3_in, 16)
    sp.dma_start(T.adst[:, :], D.adst.partition_broadcast(P)).then_inc(S.w3_in, 16)
    sp.dma_start(T.asrc[:, :], D.asrcT).then_inc(S.w3_in, 16)
    sp.dma_start(T.wfx[:, :, :], D.L1_ffn_W_fx.rearrange("(k p) o -> p k o", p=P)).then_inc(S.w4_in, 16)
    sp.dma_start(T.wx[:, :, :], D.L1_ffn_W_x.rearrange("(k p) o -> p k o", p=P)).then_inc(S.w4_in, 16)
    sp.dma_start(T.wo[:, :, :], D.L1_ffn_W_out.rearrange("(h c) o -> c h o", c=HD2)).then_inc(S.w4_in, 16)
    for n, w in enumerate((D.L1_ffn_W_q, D.L1_ffn_W_k, D.L1_ffn_W_v)):
        sp.dma_start(T.wqkv[:, n, :], w).then_inc(S.w4_in, 16)
    sp.dma_start(T.bfx[:, :], D.L1_ffn_b_fx.partition_broadcast(P)).then_inc(S.w4_in, 16)
    sp.dma_start(T.bx[:, :], D.bxT).then_inc(S.w4_in, 16)
    sp.dma_start(T.bsl[:, :], D.L1_ffn_b_slice.partition_broadcast(P)).then_inc(S.w4_in, 16)
    sp.dma_start(T.bout[:, :], D.L1_ffn_b_out.partition_broadcast(P)).then_inc(S.w4_in, 16)
    sp.dma_start(T.temp[:, 0, :], D.temp.partition_broadcast(P)).then_inc(S.w4_in, 16)
    sp.wait_ge(S.w4_const, 1)
    for n in range(2):
        sp.dma_start(T.wsl[n * HD2:(n + 1) * HD2, n * HD2:(n + 1) * HD2], D.L1_ffn_W_slice).then_inc(S.w4_in, 16)
    sp.wait_ge(S.y_ready, CH)
    sp.dma_start(out[0:full, :].rearrange("(c p) d -> p c d", p=P), T.X[:, 0:CH - 1, :]).then_inc(S.stored, 16)
    sp.dma_start(out[full:NODES, :], T.X[0:LAST, CH - 1, :]).then_inc(S.stored, 16)
    sp.wait_ge(S.stored, 32)


W4_LOADS = 16 * 13


def pool_program(pool, nc, S, T):
    nc.gpsimd.memset(T.X[:, CH - 1, :], 0.0).then_inc(S.x_zero, 1)
    nc.gpsimd.memset(T.ei[:, 1:3, :], 0)
    nc.gpsimd.memset(T.ei[:, 0, :], OUTSIDE).then_inc(S.ei_set, 1)
    nc.gpsimd.memset(T.eps[:, :], LN_EPS).then_inc(S.const_ready, 1)
    nc.gpsimd.memset(T.ident[:, :], 0.0).then_inc(S.const_ready, 1)
    nc.gpsimd.iota(T.iota[:, :], pattern=[[1, NP]], base=0, channel_multiplier=0,
                   allow_small_or_imprecise_dtypes=True).then_inc(S.const_ready, 1)
    nc.gpsimd.iota(T.kiota[:, :], pattern=[[1, KEYS]], base=0, channel_multiplier=0,
                   allow_small_or_imprecise_dtypes=True).then_inc(S.const_ready, 1)
    pool.wait_ge(S.const_ready, 4)
    nc.gpsimd.affine_select(out=T.ident[:, :], in_=T.ident[:, :], compare_op=ALU.not_equal, fill=1.0,
                            base=0, pattern=[[-1, P]], channel_multiplier=1).then_inc(S.const_ready, 1)
    nc.gpsimd.memset(T.A[:, :, :, :].rearrange("p c r n -> p (c r n)").bitcast(F32), 0.0).then_inc(S.a_zero, 1)
    for n, (wh, wl) in enumerate(((T.wh0, T.wl0), (T.wh1, T.wl1))):
        pool.wait_ge(S.raw_in, 48 * (n + 1))
        nc.gpsimd.tensor_copy(wh[:, :, :, :], T.raw[:, :, :, :]).then_inc(S.w_ready, 1)
        pool.wait_ge(S.w_ready, 2 * n + 1)
        nc.gpsimd.tensor_tensor(wl[:, :, :, :], T.raw[:, :, :, :], wh[:, :, :, :].bitcast(F32),
                                ALU.subtract).then_inc(S.w_ready, 1)
        if n == 0:
            pool.wait_ge(S.w_ready, 2)
            nc.gpsimd.engine_nop().then_inc(S.raw_free, 1)
    pool.wait_ge(S.A_built, 1)
    nc.gpsimd.iota(T.iota8[:, :], pattern=[[1, EXPERTS]], base=0, channel_multiplier=0,
                   allow_small_or_imprecise_dtypes=True).then_inc(S.gate_const, 1)
    nc.gpsimd.tensor_tensor(T.C[:, :, :], T.A[:, :, 0, :], T.A[:, :, 1, :], ALU.add).then_inc(S.c_step, 1)
    for r in range(2, TYPES):
        pool.wait_ge(S.c_step, r - 1)
        nc.gpsimd.tensor_tensor(T.C[:, :, :], T.C[:, :, :], T.A[:, :, r, :], ALU.add).then_inc(S.c_step, 1)
    pool.wait_ge(S.c_step, TYPES - 1)
    nc.gpsimd.engine_nop().then_inc(S.C_built, 1)
    pool.wait_ge(S.experts_done, 1)
    nc.gpsimd.memset(T.hp[:, :, :, HD1:HD1 + 1], 1.0).then_inc(S.w3_ready, 1)
    nc.gpsimd.memset(T.wsl[:, :], 0.0).then_inc(S.w4_const, 1)
    nc.gpsimd.memset(T.ones[:, :], 1.0).then_inc(S.w4_const, 1)
    pool.wait_ge(S.w3_in, 48)
    nc.gpsimd.tensor_copy(T.w3h[:, :, :], T.w3[:, :, :]).then_inc(S.w3_ready, 1)
    pool.wait_ge(S.w3_ready, 2)
    nc.gpsimd.tensor_tensor(T.w3l[:, :, :], T.w3[:, :, :], T.w3h[:, :, :].bitcast(F32),
                            ALU.subtract).then_inc(S.w3_ready, 1)
    pool.wait_ge(S.w4_in, W4_LOADS)
    for raw, hi, lo, ready in ((T.wfx, T.wfxh, T.wfxl, S.wfx_ready), (T.wx, T.wxh, T.wxl, S.wx_ready)):
        nc.gpsimd.tensor_copy(hi[:, :, :], raw[:, :, :]).then_inc(ready, 1)
        pool.wait_ge(ready, 1)
        nc.gpsimd.tensor_tensor(lo[:, :, :], raw[:, :, :], hi[:, :, :].bitcast(F32),
                                ALU.subtract).then_inc(ready, 1)


def act_program(act, nc, S, T, R):
    A = nc.scalar

    def ln(n):
        if n == 0:
            act.wait_ge(S.const_ready, 1)
        act.wait_ge(S.ln_aggr, CH * (n + 1))
        A.activation(T.std[:, :], T.mv[:, :, 1], ACT.Sqrt, bias=T.eps[:, 0:1]).then_inc(S.ln_std, 1)

    def xT(n):
        act.wait_ge(S.tr_done, n + 1)
        A.activation(T.xTh[:, :, :].rearrange("p k n -> p (k n)"), R.flat[:, 0:KD * NP], ACT.Copy).then_inc(S.xTh_ready, 1)

    def split3(n):
        for part in range(3):
            if part == 0:
                act.wait_ge(S.ln_out if n == 0 else S.layer_step, CH if n == 0 else 2)
                src = T.xn
            else:
                act.wait_ge(S.xr_step, 2 * n + part)
                src = T.xr
            A.activation(T.xp[:, part, :, :], src[:, :, :], ACT.Copy).then_inc(S.xp_step, 1)

    def stage_counts(g0):
        with act.Fori(0, GROUPS // 2) as i:
            for b in range(2):
                act.wait_ge(S.counts_done, g0 + i * 2 + b + 3)
                act.wait_ge(S.added, g0 + i * 2 + b + 1)
                A.activation(T.add[:, b, :], R.flat[:, 1024 * b:1024 * b + CH * KEYS], ACT.Copy).then_inc(S.staged, 1)

    def layer(n):
        j0 = 2 * TYPES * n
        with act.Fori(0, TYPES) as r:
            for k in range(KD):
                act.wait_ge(S.y_done, r * 2 + (j0 + k + 1))
                act.wait_ge(S.out_done, r * 2 + (j0 + k + 1))
                A.activation(T.yh[:, k, :].rearrange("p (h n) -> p h n", h=2),
                             R.banks[:, 2 * k:2 * k + 2, 0:HALF], ACT.Copy).then_inc(S.yh_ready, 1)

    ln(0)
    xT(0)
    split3(0)
    act.wait_ge(S.base_ready, 1)
    fits = act.value_load(T.fits[0:1, 0:1], min_val=0, max_val=1)
    A.sem_inc(S.staged, 2)
    with act.If(fits == 1):
        stage_counts(0)
    with act.Else():
        with act.Fori(0, WINDOWS) as w:
            stage_counts(w * GROUPS)
    layer(0)
    xT(1)
    split3(1)
    layer(1)

    ln(1)
    xT(2)
    act.wait_ge(S.gate_step, CH + 2)
    A.activation(T.gp[:, 1, :], T.gp[:, 0, :], ACT.Exp).then_inc(S.gate_exp, 1)
    act.wait_ge(S.combT_done, 1)
    A.activation(T.combT[:, :], R.flat[0:EXPERTS, 1536:1536 + NP], ACT.Copy).then_inc(S.combT_ready, 1)
    act.wait_ge(S.y_done, 4 * TYPES)
    act.wait_ge(S.out_done, 2 + 4 * TYPES)
    act.wait_ge(S.C_built, 1)
    act.wait_ge(S.eb_in, 32)
    A.sem_inc(S.ht_ready, 2)
    with act.Fori(0, EXPERTS // 2) as i:
        for s, wh in enumerate((T.ewh0, T.ewh1)):
            act.wait_ge((S.stg0_in, S.stg1_in)[s], i * 32 + 32)
            act.wait_ge(S.h_used, (i * 2 + s) * HB)
            A.activation(wh[:, :], T.stg[:, s, :], ACT.Copy).then_inc(S.ewh_ready, 1)
            for hb in range(HB):
                b = hb % 2
                act.wait_ge(S.h_done, (i * 2 + s) * HB + hb + 1)
                act.wait_ge(S.hl_ready, (i * 2 + s) * HB + hb + 1)
                A.activation(T.ht[:, hb % HRING, :].rearrange("p (h n) -> p h n", h=2),
                             R.banks[:, 2 * b:2 * b + 2, 0:HALF], ACT.Relu,
                             bias=T.b1[:, bass.ds((i * 2 + s) * HB + hb, 1)]).then_inc(S.ht_ready, 1)

    ln(2)
    xT(3)
    act.wait_ge(S.hpT_done, 1)
    for k in range(KD):
        A.activation(T.hpT[:, k, :].rearrange("p (h n) -> p h n", h=2),
                     R.banks[:, 2 * k:2 * k + 2, 0:HALF], ACT.Copy).then_inc(S.hpT_ready, 1)
    for h in range(HEADS1):
        b = h % 2
        act.wait_ge(S.es_done, h + 1)
        A.activation(T.es[:, h, :].rearrange("p (h n) -> p h n", h=2),
                     R.banks[:, 2 * b:2 * b + 2, 0:HALF], ACT.Copy).then_inc(S.es_ready, 1)
    for c in range(CH):
        act.wait_ge(S.ct_done, c + 1)
        A.activation(T.CT[:, c, :], R.flat[:, 2048 + 1024 * (c % 2):2048 + 1024 * (c % 2) + NP],
                     ACT.Copy).then_inc(S.ct_ready, 1)

    def probs_T(j):
        act.wait_ge(S.pT_done, j + 1)
        if j >= 2:
            act.wait_ge(S.agg_done, j - 1)
        A.activation(T.pT[:, j % 2, :], R.flat[:, 1024 * (j % 2):1024 * (j % 2) + NP], ACT.Copy).then_inc(S.pT_ready, 1)

    act.wait_ge(S.m_ready, 1)
    for j in range(HEADS1 * CH):
        h, c = divmod(j, CH)
        act.wait_ge(S.lk_ready, j + 1)
        if j >= 2:
            act.wait_ge(S.pr_ready, j - 1)
        A.activation(T.ex[:, j % 2, :], T.lk[:, j % 2, :], ACT.Exp, bias=T.nm[:, c, h:h + 1]).then_inc(S.ex_ready, 1)
        if j >= 2:
            probs_T(j - 2)
    probs_T(HEADS1 * CH - 2)
    probs_T(HEADS1 * CH - 1)

    ln(3)
    xT(4)
    act.wait_ge(S.w4_in, W4_LOADS)
    for b in range(IB):
        act.wait_ge(S.xm_done, b + 1)
        A.activation(T.xm[:, b, :].rearrange("p (h n) -> p h n", h=2),
                     R.banks[:, 2 * (b % 2):2 * (b % 2) + 2, 0:HALF], ACT.Identity,
                     bias=T.bx[:, b:b + 1]).then_inc(S.xm_ready, 1)
    for c in range(CH):
        act.wait_ge(S.lg_step, 4 * c + 4)
        A.activation(T.sw[:, c, :], T.lg[:, c, :], ACT.Exp).then_inc(S.sm_exp, 1)
    act.wait_ge(S.qkv_done, 1)
    A.activation(T.qk[:, :, :].rearrange("p a n -> p (a n)"), R.flat[0:HD2, 1024:2048], ACT.Copy).then_inc(S.qkv_ready, 1)
    A.activation(T.v[:, :], R.flat[0:SLICES, 2048:2560], ACT.Copy).then_inc(S.qkv_ready, 1)
    act.wait_ge(S.al_step, 2)
    A.activation(T.at[:, 1, :], T.at[:, 0, :], ACT.Exp, scale=float(HD2) ** -0.5).then_inc(S.al_exp, 1)
    act.wait_ge(S.atT_done, 1)
    A.activation(T.atT[:, :], R.flat[0:SLICES, 0:INNER], ACT.Copy).then_inc(S.atT_ready, 1)
    act.wait_ge(S.osT_done, 1)
    A.activation(T.osT[:, :], R.flat[0:HD2, 512:512 + INNER], ACT.Copy).then_inc(S.osT_ready, 1)
    act.wait_ge(S.swT_done, 1)
    A.activation(T.swT[:, :, :].rearrange("p b n -> p (b n)"), R.flat[:, 1024:1024 + IB * NP], ACT.Copy).then_inc(S.swT_ready, 1)
    act.wait_ge(S.M_done, 1)
    A.activation(T.M[:, :, :].rearrange("p b n -> p (b n)"), R.flat[:, 0:IB * DIM], ACT.Copy).then_inc(S.M_ready, 1)


def pe_program(pe, nc, S, T, R):
    def mm3(o, lh, ll, rh, rl, start, stop, **kw):
        nc.tensor.matmul(o, lh, rh, start=start, stop=False, **kw)
        nc.tensor.matmul(o, lh, rl, start=False, stop=False, **kw)
        return nc.tensor.matmul(o, ll, rh, start=False, stop=stop, **kw)

    def transpose_x(n):
        if n == 0:
            pe.wait_ge(S.const_ready, 5)
        if n == 1:
            pe.wait_ge(S.layer_step, 2)
            pe.wait_ge(S.yl_ready, 2 + 2 * TYPES)
        elif n:
            pe.wait_ge(S.ln_out, CH * n)
        else:
            pe.wait_ge(S.ln_out, CH)
        for k in range(KD):
            for c in range(CH):
                o = (k * CH + c) * P
                mm = nc.tensor.transpose(R.flat[:, o:o + P], T.xn[:, c, k * P:(k + 1) * P], T.ident[:, :])
        mm.then_inc(S.tr_done, 1)

    def edges():
        pe.wait_ge(S.ef_ready, 1)
        for n in range(4):
            for j in range(TILES):
                o = 2048 + (0 if n < 3 else 512) + ((n % 3) * TILES + j) * GROUPS
                mm = nc.tensor.transpose(R.flat[:, o:o + GROUPS], T.ef[:, n, j * P:(j + 1) * P],
                                         T.ident[0:GROUPS, 0:GROUPS])
        mm.then_inc(S.eT_done, 1)
        for n in range(2):
            o = 3072 + n * GROUPS
            mm = nc.tensor.transpose(R.flat[0:1, o:o + GROUPS], T.dlim[:, n:n + 1], T.ident[0:GROUPS, 0:GROUPS])
        mm.then_inc(S.base_done, 1)

    def counts(g0):
        with pe.Fori(0, GROUPS // 2) as i:
            for b in range(2):
                pe.wait_ge(S.oh_ready, g0 + i * 2 + b + 1)
                pe.wait_ge(S.staged, g0 + i * 2 + b + 1)
                for c in range(CH):
                    for j in range(TILES):
                        o = 1024 * b + c * KEYS
                        mm = nc.tensor.matmul(R.flat[:, o:o + KEYS], T.oh[:, b, j, c * P:(c + 1) * P],
                                              T.ko[:, b, j, :], start=(j == 0), stop=(j == TILES - 1))
                mm.then_inc(S.counts_done, 1)

    def layer(n):
        wh, wl = ((T.wh0, T.wl0), (T.wh1, T.wl1))[n]
        j0 = 2 * TYPES * n

        def acc(c):
            return R.flat[:, 2048 + c * DIM:2048 + (c + 1) * DIM]

        pe.wait_ge(S.w_ready, 2 * n + 2)
        pe.wait_ge(S.xTl_ready, n + 1)
        pe.wait_ge(S.xTh_ready, n + 1)
        for c in range(CH):
            for k in range(KD):
                x = slice(c * P, (c + 1) * P)
                mm3(acc(c), T.xTh[:, k, x], T.xTl[:, k, x], wh[:, TYPES, k, :], wl[:, TYPES, k, :],
                    start=(k == 0 and c % 2 == 0), stop=False, skip_group_check=True)
        pe.wait_ge(S.xp_step, 3 * (n + 1))

        def aggregate(r, k, j):
            pe.wait_ge(S.yl_ready, j + 1)
            for half in range(2):
                for c in range(CH):
                    for part in range(3):
                        mm = nc.tensor.matmul(
                            R.banks[:, 2 * k + half, 0:HALF], T.xp[:, part, c, k * P:(k + 1) * P],
                            (T.A[:, c, r, half * HALF:(half + 1) * HALF] if type(r) is int else
                             T.A[:, c, bass.ds(r, 1), half * HALF:(half + 1) * HALF].rearrange("p a n -> p (a n)")),
                            start=(c == 0 and part == 0), stop=(c == CH - 1 and part == 2))
            mm.then_inc(S.y_done, 1)

        def product(r, k, j, last=False):
            pe.wait_ge(S.yl_ready, j + 3)
            for c in range(CH):
                x = slice(c * P, (c + 1) * P)
                if type(r) is int:
                    h, l = wh[:, r, k, :], wl[:, r, k, :]
                else:
                    h = wh[:, bass.ds(r, 1), k, :].rearrange("p a n -> p (a n)")
                    l = wl[:, bass.ds(r, 1), k, :].rearrange("p a n -> p (a n)")
                mm = mm3(acc(c), T.yh[:, k, x], T.yl[:, k, x], h, l, start=False, stop=last, skip_group_check=True)
            mm.then_inc(S.out_done, 1)

        aggregate(0, 0, j0)
        with pe.Fori(0, TYPES - 1) as r:
            aggregate(r, 1, r * 2 + (j0 + 1))
            product(r, 0, r * 2 + j0)
            aggregate(r + 1, 0, r * 2 + (j0 + 2))
            product(r, 1, r * 2 + (j0 + 1))
        j = j0 + 2 * TYPES - 2
        aggregate(TYPES - 1, 1, j + 1)
        product(TYPES - 1, 0, j)
        product(TYPES - 1, 1, j + 1, last=True)

    transpose_x(0)
    edges()
    pe.wait_ge(S.base_ready, 1)
    fits = pe.value_load(T.fits[0:1, 0:1], min_val=0, max_val=1)
    nc.tensor.sem_inc(S.counts_done, 2)
    with pe.If(fits == 1):
        counts(0)
    with pe.Else():
        with pe.Fori(0, WINDOWS) as w:
            counts(w * GROUPS)
    nc.tensor.sem_inc(S.out_done, 2)
    pe.wait_ge(S.A_built, 1)
    layer(0)
    transpose_x(1)
    layer(1)

    transpose_x(2)
    pe.wait_ge(S.xTh_ready, 3)
    pe.wait_ge(S.xTl_ready, 3)
    pe.wait_ge(S.gate_in, 32)
    pe.wait_ge(S.acc_read, 2 * CH)
    for c in range(CH):
        for k in range(KD):
            x = slice(c * P, (c + 1) * P)
            for a in (T.xTh, T.xTl):
                mm = nc.tensor.matmul(R.flat[:, 2048 + c * EXPERTS:2048 + (c + 1) * EXPERTS],
                                      a[:, k, x].bitcast(F32), T.wg[:, 0, k, :],
                                      start=(k == 0 and a is T.xTh), stop=(k == KD - 1 and a is T.xTl))
    mm.then_inc(S.gate_mm, 1)
    pe.wait_ge(S.comb_ready, 1)
    for c in range(CH):
        mm = nc.tensor.transpose(R.flat[0:EXPERTS, 1536 + c * P:1536 + (c + 1) * P], T.comb[:, c, :], T.ident[:, :])
    mm.then_inc(S.combT_done, 1)
    pe.wait_ge(S.combT_ready, 1)
    pe.wait_ge(S.eb_in, 32)

    def yacc(c):
        return R.flat[:, 2048 + c * DIM:2048 + (c + 1) * DIM]

    for c in range(CH):
        mm = nc.tensor.matmul(yacc(c), T.combT[:, c * P:(c + 1) * P], T.b2[:, :], start=True, stop=True)
    mm.then_inc(S.b2_done, 1)
    pe.wait_ge(S.b2_added, 1)
    nc.tensor.sem_inc(S.h_used, HB)

    def hidden(wh, wl, hb, j):
        b = hb % 2
        pe.wait_ge(S.ht_ready, j + 1)
        for half in range(2):
            for k in range(KD):
                w = slice(k * HID + hb * P, k * HID + (hb + 1) * P)
                n = slice(half * HALF, (half + 1) * HALF)
                mm = mm3(R.banks[:, 2 * b + half, 0:HALF], wh[:, w], wl[:, w], T.xTh[:, k, n], T.xTl[:, k, n],
                         start=(k == 0), stop=(k == KD - 1))
        mm.then_inc(S.h_done, 1)

    def outputs(wh, wl, hb, j, e):
        pe.wait_ge(S.hl_ready, j + HRING + 1)
        if hb == 0:
            pe.wait_ge(S.yacc_added, e + 1)
        w = slice(2 * HID + hb * DIM, 2 * HID + (hb + 1) * DIM)
        for c in range(CH):
            x = slice(c * P, (c + 1) * P)
            mm = mm3(yacc(c), T.hh[:, hb % HRING, x], T.hl[:, hb % HRING, x], wh[:, w], wl[:, w],
                     start=(hb == 0 and c % 2 == 0), stop=(hb == HB - 1), skip_group_check=True)
        mm.then_inc(S.h_used, 1)

    LAG = 2
    sets = ((T.ewh0, T.ewl0), (T.ewh1, T.ewl1))

    def experts(i, first):
        for n in range(2 * HB):
            s, hb = divmod(n, HB)
            if hb == 0:
                pe.wait_ge(S.ewl_ready, i * 2 + s + 1)
            hidden(*sets[s], hb, i * (2 * HB) + n)
            if n >= LAG or not first:
                m = n - LAG
                s2, hb2 = divmod(m % (2 * HB), HB)
                outputs(*sets[s2], hb2, i * (2 * HB) + m, i * 2 + (s2 if m >= 0 else s2 - 2))

    pe.wait_ge(S.xTl_ready, 3)
    experts(0, True)
    with pe.Fori(1, EXPERTS // 2) as i:
        experts(i, False)
    for m in range(EXPERTS * HB - LAG, EXPERTS * HB):
        outputs(*sets[1], m % HB, m, EXPERTS - 1)

    transpose_x(3)
    pe.wait_ge(S.xTh_ready, 4)
    pe.wait_ge(S.xTl_ready, 4)
    pe.wait_ge(S.w3_ready, 3)
    for f in range(KD):
        for half in range(2):
            n = slice(half * HALF, (half + 1) * HALF)
            for k in range(KD):
                w = slice(f * P, (f + 1) * P)
                mm = mm3(R.banks[:, 2 * f + half, 0:HALF], T.w3h[:, k, w], T.w3l[:, k, w],
                         T.xTh[:, k, n], T.xTl[:, k, n], start=(k == 0), stop=(k == KD - 1))
    mm.then_inc(S.hpT_done, 1)
    for c in range(CH):
        x = slice(c * P, (c + 1) * P)
        for k in range(KD):
            mm = mm3(R.flat[:, 2048 + c * DIM:2048 + (c + 1) * DIM], T.xTh[:, k, x], T.xTl[:, k, x],
                     T.w3h[:, k, :], T.w3l[:, k, :], start=(k == 0), stop=(k == KD - 1))
    mm.then_inc(S.hp_done, 1)
    pe.wait_ge(S.asrc_ready, 1)
    pe.wait_ge(S.hpT_ready, 2)
    for h in range(HEADS1):
        k, o = divmod(h * HD1, P)
        b = h % 2
        if h >= 2:
            pe.wait_ge(S.es_ready, h - 1)
        for half in range(2):
            mm = nc.tensor.matmul(R.banks[:, 2 * b + half, 0:HALF], T.asrc_bc[o:o + HD1, k, :],
                                  T.hpT[o:o + HD1, k, half * HALF:(half + 1) * HALF], start=True, stop=True)
        mm.then_inc(S.es_done, 1)
    pe.wait_ge(S.hp_ready, 1)
    for c in range(CH):
        if c >= 2:
            pe.wait_ge(S.ct_ready, c - 1)
        for s in range(CH):
            o = 2048 + 1024 * (c % 2) + s * P
            mm = nc.tensor.transpose(R.flat[:, o:o + P], T.C[:, s, c * P:(c + 1) * P], T.ident[:, :])
        mm.then_inc(S.ct_done, 1)

    def turn(j):
        pe.wait_ge(S.pr_ready, j + 1)
        if j >= 2:
            pe.wait_ge(S.pT_ready, j - 1)
        for s in range(CH):
            o = 1024 * (j % 2) + s * P
            mm = nc.tensor.transpose(R.flat[:, o:o + P], T.pr[:, j % 2, s * P:(s + 1) * P], T.ident[:, :])
        mm.then_inc(S.pT_done, 1)

    def gather(j):
        h, c = divmod(j, CH)
        pe.wait_ge(S.pT_ready, j + 1)
        if c == 0 and h >= 2:
            pe.wait_ge(S.x3_ready, h - 1)
        o = 2048 + 512 * (h % 2) + c * (HD1 + 1)
        for s in range(CH):
            mm = nc.tensor.matmul(R.flat[:, o:o + HD1 + 1], T.pT[:, j % 2, s * P:(s + 1) * P], T.hp[:, s, h, :],
                                  start=(s == 0), stop=(s == CH - 1))
        mm.then_inc(S.agg_done, 1)

    pe.wait_ge(S.es_ready, HEADS1)
    pe.wait_ge(S.ct_ready, CH)
    for j in range(HEADS1 * CH):
        turn(j)
        if j >= 1:
            gather(j - 1)
    gather(HEADS1 * CH - 1)

    transpose_x(4)
    pe.wait_ge(S.xTh_ready, 5)
    pe.wait_ge(S.xTl_ready, 5)
    pe.wait_ge(S.wx_ready, 2)
    pe.wait_ge(S.w4_in, W4_LOADS)
    for b in range(IB):
        if b >= 2:
            pe.wait_ge(S.xm_ready, b - 1)
        for half in range(2):
            n = slice(half * HALF, (half + 1) * HALF)
            for k in range(KD):
                w = slice(b * P, (b + 1) * P)
                mm = mm3(R.banks[:, 2 * (b % 2) + half, 0:HALF], T.wxh[:, k, w], T.wxl[:, k, w],
                         T.xTh[:, k, n], T.xTl[:, k, n], start=(k == 0), stop=(k == KD - 1))
        mm.then_inc(S.xm_done, 1)
    pe.wait_ge(S.wfx_ready, 2)
    for c in range(CH):
        if c >= 2:
            pe.wait_ge(S.fx_ready, c - 1)
        x = slice(c * P, (c + 1) * P)
        for k in range(KD):
            mm = mm3(R.banks[:, 4 + c % 2, :], T.xTh[:, k, x], T.xTl[:, k, x], T.wfxh[:, k, :], T.wfxl[:, k, :],
                     start=(k == 0), stop=(k == KD - 1))
        mm.then_inc(S.fx_done, 1)
    pe.wait_ge(S.xm_ready, IB)
    for c in range(CH):
        if c >= 2:
            pe.wait_ge(S.lg_step, 4 * (c - 2) + 1)
        for b in range(IB):
            mm = nc.tensor.matmul(R.banks[:, 6 + c % 2, b * P:(b + 1) * P], T.xm[:, b, c * P:(c + 1) * P],
                                  T.wsl[:, :], start=True, stop=True)
        mm.then_inc(S.lg_done, 1)
    pe.wait_ge(S.sw_ready, CH)
    pe.wait_ge(S.fx_ready, CH)
    pe.wait_ge(S.w4_const, 2)
    for c in range(CH):
        k = chunks(T, c)
        nc.tensor.matmul(R.flat[0:HD2, 512:1024], T.ones[0:k, :], T.sw[0:k, c, :], start=(c == 0), stop=(c == CH - 1))
    for h in range(HEADS2):
        w = slice(h * HD2, (h + 1) * HD2)
        for c in range(CH):
            k = chunks(T, c)
            mm = nc.tensor.matmul(R.flat[0:HD2, w], T.fx[0:k, c, w], T.sw[0:k, c, w], start=(c == 0), stop=(c == CH - 1))
    mm.then_inc(S.tok_done, 1)
    pe.wait_ge(S.tok_ready, 1)
    for n in range(2):
        nc.tensor.matmul(R.flat[0:HD2, 1024 + 512 * n:1536 + 512 * n], T.wqkv[:, n, :], T.tok[:, :], start=True, stop=True)
    for h in range(HEADS2):
        w = slice(h * HD2, (h + 1) * HD2)
        mm = nc.tensor.matmul(R.flat[0:SLICES, 2048 + h * HD2:2048 + (h + 1) * HD2], T.tok[:, w], T.wqkv[:, 2, :],
                              start=True, stop=True)
    mm.then_inc(S.qkv_done, 1)
    pe.wait_ge(S.qkv_ready, 2)
    for h in range(HEADS2):
        w = slice(h * SLICES, (h + 1) * SLICES)
        mm = nc.tensor.matmul(R.flat[0:SLICES, 2560 + h * SLICES:2560 + (h + 1) * SLICES], T.qk[:, 0, w], T.qk[:, 1, w],
                              start=True, stop=True)
    mm.then_inc(S.al_done, 1)
    pe.wait_ge(S.at_ready, 1)
    for h in range(HEADS2):
        w = slice(h * SLICES, (h + 1) * SLICES)
        mm = nc.tensor.transpose(R.flat[0:SLICES, w], T.at[:, 2, w], T.ident[0:SLICES, 0:SLICES])
    mm.then_inc(S.atT_done, 1)
    pe.wait_ge(S.atT_ready, 1)
    for h in range(HEADS2):
        w = slice(h * HD2, (h + 1) * HD2)
        mm = nc.tensor.matmul(R.flat[0:HD2, 512 + h * SLICES:512 + (h + 1) * SLICES], T.v[:, w], T.atT[:, w],
                              start=True, stop=True)
    mm.then_inc(S.osT_done, 1)
    for b in range(IB):
        for c in range(CH):
            o = 1024 + (b * CH + c) * P
            mm = nc.tensor.transpose(R.flat[:, o:o + P], T.sw[:, c, b * P:(b + 1) * P], T.ident[:, :])
    mm.then_inc(S.swT_done, 1)
    pe.wait_ge(S.osT_ready, 1)
    for h in range(HEADS2):
        b, o = divmod(h * SLICES, P)
        mm = nc.tensor.matmul(R.flat[o:o + SLICES, b * DIM:(b + 1) * DIM], T.osT[:, h * SLICES:(h + 1) * SLICES],
                              T.wo[:, h, :], start=True, stop=True)
    mm.then_inc(S.M_done, 1)
    pe.wait_ge(S.M_ready, 1)
    pe.wait_ge(S.swT_ready, 1)
    for c in range(CH):
        for b in range(IB):
            mm = nc.tensor.matmul(R.banks[:, 2 + c, 0:DIM], T.swT[:, b, c * P:(c + 1) * P],
                                  T.M[:, b, :], start=(b == 0), stop=(b == IB - 1))
        mm.then_inc(S.out4_done, 1)


def dve_program(dve, nc, S, T, R):
    V = nc.vector

    def ln(n):
        for c in range(CH):
            V.bn_stats(T.stats[:, c, :], T.X[:, c, :]).then_inc(S.ln_stats, 1)
        for c in range(CH):
            dve.wait_ge(S.ln_stats, CH * n + c + 1)
            V.bn_aggr(T.mv[:, c, :], T.stats[:, c, :]).then_inc(S.ln_aggr, 1)
        dve.wait_ge(S.ln_std, n + 1)
        V.reciprocal(T.rstd[:, :], T.std[:, :]).then_inc(S.ln_rstd, 1)
        dve.wait_ge(S.ln_rstd, n + 1)
        for c in range(CH):
            V.tensor_scalar(T.xn[:, c, :], T.X[:, c, :], T.mv[:, c, 0:1], T.rstd[:, c:c + 1],
                            ALU.subtract, ALU.mult).then_inc(S.ln_out, 1)

    def xT(n):
        dve.wait_ge(S.xTh_ready, n + 1)
        V.tensor_tensor(T.xTl[:, :, :].rearrange("p k n -> p (k n)"), R.flat[:, 0:KD * NP],
                        T.xTh[:, :, :].rearrange("p k n -> p (k n)").bitcast(F32), ALU.subtract).then_inc(S.xTl_ready, 1)

    def split3(n):
        dve.wait_ge(S.xp_step, 3 * n + 1)
        V.tensor_tensor(T.xr[:, :, :], T.xn[:, :, :], T.xp[:, 0, :, :], ALU.subtract).then_inc(S.xr_step, 1)
        dve.wait_ge(S.xp_step, 3 * n + 2)
        dve.wait_ge(S.xr_step, 2 * n + 1)
        V.tensor_tensor(T.xr[:, :, :], T.xr[:, :, :], T.xp[:, 1, :, :], ALU.subtract).then_inc(S.xr_step, 1)

    def edges():
        dve.wait_ge(S.e_in, 96)
        V.tensor_copy(T.ef[:, 0:3, :], T.ei[:, :, :]).then_inc(S.ef_step, 1)
        dve.wait_ge(S.ef_step, 1)
        V.tensor_reduce(T.dlim[:, 0:1], T.ef[:, 0, :], AX.X, ALU.min).then_inc(S.ef_step, 1)
        V.scalar_tensor_tensor(T.ef[:, 3, :], T.ef[:, 0, :], float(OUTSIDE), T.ef[:, 0, :],
                               ALU.is_lt, ALU.mult).then_inc(S.ef_step, 1)
        dve.wait_ge(S.ef_step, 3)
        V.tensor_reduce(T.dlim[:, 2:3], T.ef[:, 3, :], AX.X, ALU.max).then_inc(S.ef_step, 1)
        dve.wait_ge(S.ef_step, 4)
        V.tensor_tensor(T.dlim[:, 1:2], T.dlim[:, 2:3], T.dlim[:, 0:1], ALU.subtract).then_inc(S.ef_step, 1)
        V.scalar_tensor_tensor(T.ef[:, 3, :], T.ef[:, 1, :], float(WIN), T.ef[:, 0, :],
                               ALU.mult, ALU.add).then_inc(S.ef_step, 1)
        dve.wait_ge(S.ef_step, 6)
        V.tensor_scalar(T.ef[:, 3, :], T.ef[:, 3, :], T.dlim[:, 0:1], None, ALU.subtract).then_inc(S.ef_ready, 1)
        n = 3 * TILES * GROUPS
        flat = T.eT[:, :, :, :].rearrange("p a t g -> p (a t g)")
        dve.wait_ge(S.eT_done, 1)
        V.tensor_copy(flat[:, 0:n], R.flat[:, 2048:2048 + n]).then_inc(S.eT_ready, 1)
        V.tensor_copy(flat[:, n:n + TILES * GROUPS], R.flat[:, 2560:2560 + TILES * GROUPS]).then_inc(S.eT_ready, 1)
        dve.wait_ge(S.base_done, 1)
        V.tensor_copy(T.bases[:, 0:GROUPS], R.flat[0:1, 3072:3072 + GROUPS]).then_inc(S.base_step, 1)
        V.tensor_reduce(T.spanmax[:, 0:1], R.flat[0:1, 3072 + GROUPS:3072 + 2 * GROUPS], AX.X, ALU.max).then_inc(S.base_step, 1)
        dve.wait_ge(S.base_step, 2)
        V.tensor_scalar(T.spanmax[:, 1:2], T.spanmax[:, 0:1], float(FIT_BELOW), None, ALU.is_lt).then_inc(S.base_step, 1)
        dve.wait_ge(S.base_step, 3)
        V.tensor_copy(T.fits[:, :], T.spanmax[:, 1:2]).then_inc(S.base_ready, 1)

    def counts(key, g0, base_of):
        def one_hot(g, b):
            dve.wait_ge(S.counts_done, g + g0 + 1)
            for j in range(TILES):
                V.tensor_scalar(T.oh[:, b, j, :], T.iota[:, :],
                                T.eT[:, 2, j, bass.ds(g, 1)], None, ALU.is_equal)
            for j in range(TILES):
                ins = V.tensor_scalar(T.ko[:, b, j, :], T.kiota[:, :], key[:, j, bass.ds(g, 1)], None, ALU.is_equal)
            ins.then_inc(S.oh_ready, 1)

        def add(g, b, base):
            dve.wait_ge(S.staged, g + g0 + 3)
            dve.wait_ge(S.added, g + g0 + 2)
            at = T.A[:, :, :, bass.ds(base, WIN)]
            V.tensor_tensor(at, at, T.add[:, b, :].rearrange("p (c r d) -> p c r d", c=CH, r=TYPES),
                            ALU.add).then_inc(S.added, 1)

        one_hot(0, 0)
        with dve.Fori(0, GROUPS // 2 - 1) as i:
            bases = [base_of(i * 2 + b) for b in range(2)]
            one_hot(i * 2 + 1, 1)
            add(i * 2, 0, bases[0])
            one_hot(i * 2 + 2, 0)
            add(i * 2 + 1, 1, bases[1])
        bases = [base_of(GROUPS - 2 + b) for b in range(2)]
        one_hot(GROUPS - 1, 1)
        add(GROUPS - 2, 0, bases[0])
        add(GROUPS - 1, 1, bases[1])

    def window_keys(w):
        flat = T.eT[:, :, :, :].rearrange("p a t g -> p a (t g)")
        d, t = flat[:, 0, :], flat[:, 1, :]
        rel, low, high, key = (T.kgen[:, n, :] for n in range(4))
        dve.wait_ge(S.added, w * GROUPS + 2)
        dve.wait_ge(S.w16_step, w + 1)
        V.tensor_scalar(rel, d, T.w16[:, 0:1], None, ALU.subtract).then_inc(S.key_step, 1)
        dve.wait_ge(S.key_step, w * 6 + 1)
        V.tensor_scalar(low, rel, 0.0, float(OUTSIDE), ALU.is_lt, ALU.mult).then_inc(S.key_step, 1)
        V.tensor_scalar(high, rel, float(WIN), float(OUTSIDE), ALU.is_ge, ALU.mult).then_inc(S.key_step, 1)
        V.scalar_tensor_tensor(key, t, float(WIN), rel, ALU.mult, ALU.add).then_inc(S.key_step, 1)
        dve.wait_ge(S.key_step, w * 6 + 4)
        V.tensor_tensor(key, key, low, ALU.add).then_inc(S.key_step, 1)
        dve.wait_ge(S.key_step, w * 6 + 5)
        V.tensor_tensor(key, key, high, ALU.add).then_inc(S.key_step, 1)
        dve.wait_ge(S.key_step, w * 6 + 6)
        V.tensor_scalar(T.w16[:, :], T.w16[:, :], float(WIN), None, ALU.add).then_inc(S.w16_step, 1)

    def layer(n):
        j0 = 2 * TYPES * n
        with dve.Fori(0, TYPES) as r:
            for k in range(KD):
                dve.wait_ge(S.yh_ready, r * 2 + (j0 + k + 1))
                dve.wait_ge(S.out_done, r * 2 + (j0 + k + 1))
                V.tensor_tensor(T.yl[:, k, :].rearrange("p (h n) -> p h n", h=2), R.banks[:, 2 * k:2 * k + 2, 0:HALF],
                                T.yh[:, k, :].rearrange("p (h n) -> p h n", h=2).bitcast(F32),
                                ALU.subtract).then_inc(S.yl_ready, 1)
        dve.wait_ge(S.out_done, 2 + 2 * TYPES * (n + 1))
        to = T.xn if n == 0 else T.xr
        dve.wait_ge(S.b_in, 32)
        for c in range(CH):
            V.tensor_tensor(to[:, c, :], R.flat[:, 2048 + c * DIM:2048 + (c + 1) * DIM], T.b_bc[:, n, :],
                            ALU.add).then_inc(S.acc_read, 1)
        dve.wait_ge(S.acc_read, CH * (n + 1))
        if n == 0:
            V.sem_inc(S.layer_step, 1)
            V.tensor_scalar(T.xn[:, :, :], T.xn[:, :, :], 0.0, None, ALU.max).then_inc(S.layer_step, 1)
        else:
            V.tensor_tensor(T.X[:, :, :], T.X[:, :, :], T.xr[:, :, :], ALU.add).then_inc(S.layer_step, 1)
            dve.wait_ge(S.layer_step, 3)

    dve.wait_ge(S.x_in, 32)
    ln(0)
    edges()
    xT(0)
    split3(0)
    fits = dve.value_load(T.fits[0:1, 0:1], min_val=0, max_val=1)
    V.sem_inc(S.added, 2)
    dve.wait_ge(S.base_ready, 1)
    dve.wait_ge(S.const_ready, 5)
    dve.wait_ge(S.eT_ready, 2)
    dve.wait_ge(S.a_zero, 1)
    with dve.If(fits == 1):
        counts(T.eT[:, 3, :, :], 0,
               lambda g: dve.value_load(T.bases[0:1, bass.ds(g, 1)], min_val=0, max_val=NODES - 1))
        dve.wait_ge(S.added, GROUPS + 2)
    with dve.Else():
        V.memset(T.w16[:, :], 0.0).then_inc(S.w16_step, 1)
        with dve.Fori(0, WINDOWS) as w:
            window_keys(w)
            counts(T.kgen[:, 3, :].rearrange("p (t g) -> p t g", t=TILES), w * GROUPS, lambda g: w * WIN)
        dve.wait_ge(S.added, GROUPS * WINDOWS + 2)
    V.sem_inc(S.A_built, 1)
    V.sem_inc(S.yl_ready, 2)
    layer(0)
    xT(1)
    split3(1)
    layer(1)

    ln(1)
    xT(2)
    dve.wait_ge(S.gate_mm, 1)
    dve.wait_ge(S.gate_in, 32)
    dve.wait_ge(S.gate_const, 1)
    V.tensor_tensor(T.gate[:, :, :], R.flat[:, 2048:2048 + CH * EXPERTS].rearrange("p (c e) -> p c e", c=CH),
                    T.bg[:, :].unsqueeze(1).to_broadcast([P, CH, EXPERTS]), ALU.add).then_inc(S.gate_step, 1)
    dve.wait_ge(S.gate_step, 1)
    for c in range(CH):
        V.max(T.top[:, c, :], T.gate[:, c, :]).then_inc(S.gate_step, 1)
    dve.wait_ge(S.gate_step, CH + 1)
    V.tensor_tensor(T.gp[:, 0, :], T.top[:, :, 1], T.top[:, :, 0], ALU.subtract).then_inc(S.gate_step, 1)
    for c in range(CH):
        V.max_index(T.topi[:, c, :], T.top[:, c, :], T.gate[:, c, :]).then_inc(S.gate_step, 1)
    dve.wait_ge(S.gate_step, 2 * CH + 2)
    V.tensor_copy(T.topf[:, :, :], T.topi[:, :, :]).then_inc(S.gate_step, 1)
    dve.wait_ge(S.gate_exp, 1)
    V.tensor_scalar(T.gp[:, 2, :], T.gp[:, 1, :], 1.0, None, ALU.add).then_inc(S.gate_step, 1)
    dve.wait_ge(S.gate_step, 2 * CH + 4)
    V.reciprocal(T.gp[:, 3, :], T.gp[:, 2, :]).then_inc(S.gate_step, 1)
    dve.wait_ge(S.gate_step, 2 * CH + 5)
    V.tensor_tensor(T.gp[:, 4, :], T.gp[:, 1, :], T.gp[:, 3, :], ALU.mult).then_inc(S.gate_step, 1)
    dve.wait_ge(S.gate_step, 2 * CH + 6)
    for c in range(CH):
        for n, to in enumerate((T.comb, T.ctmp)):
            V.tensor_scalar(to[:, c, :], T.iota8[:, :], T.topf[:, c, n:n + 1], T.gp[:, 3 + n, c:c + 1],
                            ALU.is_equal, ALU.mult).then_inc(S.gate_step, 1)
    dve.wait_ge(S.gate_step, 4 * CH + 6)
    V.tensor_tensor(T.comb[:, :, :], T.comb[:, :, :], T.ctmp[:, :, :], ALU.add).then_inc(S.comb_ready, 1)
    dve.wait_ge(S.b2_done, 1)
    V.tensor_tensor(T.X[:, :, :].rearrange("p c d -> p (c d)"), T.X[:, :, :].rearrange("p c d -> p (c d)"),
                    R.flat[:, 2048:2048 + CH * DIM], ALU.add).then_inc(S.b2_added, 1)
    dve.wait_ge(S.b2_added, 1)
    dve.wait_ge(S.comb_ready, 1)
    V.sem_inc(S.yacc_added, 1)
    V.sem_inc(S.hl_ready, HRING)

    def take_sums(e):
        dve.wait_ge(S.h_used, e * HB + 2 * HB)
        for c in range(CH):
            ins = V.scalar_tensor_tensor(T.X[:, c, :], R.flat[:, 2048 + c * DIM:2048 + (c + 1) * DIM],
                                         T.comb[:, c, bass.ds(e, 1)], T.X[:, c, :], ALU.mult, ALU.add)
        ins.then_inc(S.yacc_added, 1)

    LAG = 2

    def experts(i, first):
        for s, (wh, wl) in enumerate(((T.ewh0, T.ewl0), (T.ewh1, T.ewl1))):
            e = i * 2 + s
            dve.wait_ge(S.ewh_ready, e + 1)
            V.tensor_tensor(wl[:, :], T.stg[:, s, :], wh[:, :].bitcast(F32), ALU.subtract).then_inc(S.ewl_ready, 1)
            for hb in range(HB):
                j = e * HB + hb
                b = hb % HRING
                dve.wait_ge(S.ht_ready, j + 3)
                dve.wait_ge(S.h_used, j + (HB - HRING + 1))
                V.tensor_copy(T.hh[:, b, :], T.ht[:, b, :]).then_inc(S.hh_ready, 1)
                dve.wait_ge(S.hh_ready, j + 1)
                V.tensor_tensor(T.hl[:, b, :], T.ht[:, b, :], T.hh[:, b, :].bitcast(F32),
                                ALU.subtract).then_inc(S.hl_ready, 1)
                if hb == LAG and not (first and s == 0):
                    dve.wait_ge(S.yacc_added, e)
                    take_sums(e - 1)

    experts(0, True)
    with dve.Fori(1, EXPERTS // 2) as i:
        experts(i, False)
    dve.wait_ge(S.yacc_added, EXPERTS)
    take_sums(EXPERTS - 1)
    dve.wait_ge(S.yacc_added, EXPERTS + 1)
    V.sem_inc(S.experts_done, 1)

    ln(2)
    xT(3)
    dve.wait_ge(S.w3_in, 48)
    dve.wait_ge(S.w3_ready, 1)
    for k in range(KD):
        ins = V.tensor_scalar(T.asrc_bc[:, k, :], T.ident[:, :], 0.0, T.asrc[:, k:k + 1], ALU.mult, ALU.add)
    ins.then_inc(S.asrc_ready, 1)
    dve.wait_ge(S.hp_done, 1)
    for c in range(CH):
        ins = V.tensor_copy(T.hp[:, c, :, 0:HD1],
                            R.flat[:, 2048 + c * DIM:2048 + (c + 1) * DIM].rearrange("p (h d) -> p h d", h=HEADS1))
    ins.then_inc(S.hp_ready, 1)
    dve.wait_ge(S.hp_ready, 1)
    for c in range(CH):
        V.tensor_tensor(T.edm[:, c, :].rearrange("p (h d) -> p h d", h=HEADS1), T.hp[:, c, :, 0:HD1],
                        T.adst[:, :].rearrange("p (h d) -> p h d", h=HEADS1), ALU.mult).then_inc(S.ed_step, 1)
    dve.wait_ge(S.ed_step, CH)
    V.tensor_reduce(T.ed[:, :, :].rearrange("p c h -> p (c h)"),
                    T.edm[:, :, :].rearrange("p c (h d) -> p (c h) d", h=HEADS1), AX.X, ALU.add).then_inc(S.ed_step, 1)
    for c in range(CH):
        dve.wait_ge(S.ct_ready, c + 1)
        V.tensor_scalar(T.negm[:, c, :], T.CT[:, c, :], 0.0, NEG,
                        ALU.is_equal, ALU.mult).then_inc(S.negm_ready, 1)
    n = 0
    for h in range(HEADS1):
        dve.wait_ge(S.es_ready, h + 1)
        for c in range(CH):
            dve.wait_ge(S.negm_ready, c + 1)
            if n >= 2:
                dve.wait_ge(S.mes_step, n - 1)
            V.tensor_tensor_reduce(T.mtmp[:, n % 2, :], T.es[:, h, :], T.negm[:, c, :], 1.0, NEG, ALU.add, ALU.max,
                                   T.mes[:, c, h:h + 1]).then_inc(S.mes_step, 1)
            n += 1
    dve.wait_ge(S.mes_step, n)
    dve.wait_ge(S.ed_step, CH + 1)
    V.tensor_tensor(T.tm[:, :, :], T.mes[:, :, :], T.ed[:, :, :], ALU.add).then_inc(S.mes_step, 1)
    dve.wait_ge(S.mes_step, n + 1)
    V.scalar_tensor_tensor(T.nm[:, :, :], T.tm[:, :, :], 0.2, T.tm[:, :, :], ALU.mult, ALU.max).then_inc(S.mes_step, 1)
    dve.wait_ge(S.mes_step, n + 2)
    V.tensor_scalar(T.nm[:, :, :], T.nm[:, :, :], -1.0, None, ALU.mult).then_inc(S.m_ready, 1)

    def scores(j):
        h, c = divmod(j, CH)
        b = j % 2
        if j >= 2:
            dve.wait_ge(S.lk_ready, j - 1)
        V.tensor_scalar(T.t[:, b, :], T.es[:, h, :], T.mes[:, c, h:h + 1], T.ed[:, c, h:h + 1],
                        ALU.min, ALU.add).then_inc(S.t_ready, 1)
        dve.wait_ge(S.t_ready, j + 1)
        if j >= 2:
            dve.wait_ge(S.ex_ready, j - 1)
        V.scalar_tensor_tensor(T.lk[:, b, :], T.t[:, b, :], 0.2, T.t[:, b, :], ALU.mult, ALU.max).then_inc(S.lk_ready, 1)

    def weights(j):
        h, c = divmod(j, CH)
        dve.wait_ge(S.ex_ready, j + 1)
        if j >= 2:
            dve.wait_ge(S.pT_done, j - 1)
        V.tensor_tensor(T.pr[:, j % 2, :], T.ex[:, j % 2, :], T.CT[:, c, :], ALU.mult).then_inc(S.pr_ready, 1)

    def normalise(h):
        o = 2048 + 512 * (h % 2)
        sums = R.flat[:, o:o + CH * (HD1 + 1)].rearrange("p (c d) -> p c d", c=CH)
        dve.wait_ge(S.agg_done, CH * (h + 1))
        V.tensor_scalar(T.den[:, 0, :], sums[:, :, HD1], 1e-16, None, ALU.add).then_inc(S.o3_step, 1)
        dve.wait_ge(S.o3_step, 3 * h + 1)
        V.reciprocal(T.den[:, 1, :], T.den[:, 0, :]).then_inc(S.o3_step, 1)
        dve.wait_ge(S.o3_step, 3 * h + 2)
        V.tensor_tensor(T.o3[:, :, :], sums[:, :, 0:HD1], T.den[:, 1, :].unsqueeze(2).to_broadcast([P, CH, HD1]),
                        ALU.mult).then_inc(S.o3_step, 1)
        dve.wait_ge(S.o3_step, 3 * h + 3)
        V.tensor_tensor(T.X[:, :, h * HD1:(h + 1) * HD1], T.X[:, :, h * HD1:(h + 1) * HD1], T.o3[:, :, :],
                        ALU.add).then_inc(S.x3_ready, 1)

    dve.wait_ge(S.m_ready, 1)
    dve.wait_ge(S.ct_ready, CH)
    for j in range(HEADS1 * CH):
        scores(j)
        if j >= 1:
            weights(j - 1)
        if j >= 2 * CH and j % CH == 2:
            normalise(j // CH - 2)
    weights(HEADS1 * CH - 1)
    for h in range(2, HEADS1):
        normalise(h)
    dve.wait_ge(S.x3_ready, HEADS1)

    ln(3)
    xT(4)
    dve.wait_ge(S.w4_in, W4_LOADS)
    V.tensor_scalar(T.temp[:, 1, :], T.temp[:, 0, :], 0.1, 5.0, ALU.max, ALU.min).then_inc(S.temp_step, 1)
    dve.wait_ge(S.temp_step, 1)
    V.reciprocal(T.temp[:, 0, :], T.temp[:, 1, :]).then_inc(S.temp_step, 1)
    dve.wait_ge(S.temp_step, 2)
    for c in range(CH):
        dve.wait_ge(S.fx_done, c + 1)
        V.tensor_tensor(T.fx[:, c, :], R.banks[:, 4 + c % 2, :], T.bfx[:, :], ALU.add).then_inc(S.fx_ready, 1)

    def per_head(t):
        return t.rearrange("p (h g) -> p h g", h=HEADS2)

    def over_slices(t, rows=P):
        return t.unsqueeze(2).to_broadcast([rows, HEADS2, SLICES])

    for c in range(CH):
        lg = per_head(T.lg[:, c, :])
        hs = slice(c * HEADS2, (c + 1) * HEADS2)
        dve.wait_ge(S.lg_done, c + 1)
        V.tensor_tensor(lg, per_head(R.banks[:, 6 + c % 2, :]),
                        T.bsl[:, :].unsqueeze(1).to_broadcast([P, HEADS2, SLICES]), ALU.add).then_inc(S.lg_step, 1)
        dve.wait_ge(S.lg_step, 4 * c + 1)
        V.tensor_tensor(lg, lg, over_slices(T.temp[:, 0, :]), ALU.mult).then_inc(S.lg_step, 1)
        dve.wait_ge(S.lg_step, 4 * c + 2)
        V.tensor_reduce(T.sm[:, 0, hs], lg, AX.X, ALU.max).then_inc(S.lg_step, 1)
        dve.wait_ge(S.lg_step, 4 * c + 3)
        V.tensor_tensor(lg, lg, over_slices(T.sm[:, 0, hs]), ALU.subtract).then_inc(S.lg_step, 1)
    for c in range(CH):
        sw = per_head(T.sw[:, c, :])
        hs = slice(c * HEADS2, (c + 1) * HEADS2)
        dve.wait_ge(S.sm_exp, c + 1)
        V.tensor_reduce(T.sm[:, 1, hs], sw, AX.X, ALU.add).then_inc(S.tok_step, 1)
        dve.wait_ge(S.tok_step, 2 * c + 1)
        V.reciprocal(T.sm[:, 2, hs], T.sm[:, 1, hs]).then_inc(S.tok_step, 1)
        dve.wait_ge(S.tok_step, 2 * c + 2)
        V.tensor_tensor(sw, sw, over_slices(T.sm[:, 2, hs]), ALU.mult).then_inc(S.sw_ready, 1)
    n = 2 * CH
    dve.wait_ge(S.tok_done, 1)
    V.tensor_scalar(T.nrm[:, 0, :], R.flat[0:HD2, 512:1024], 1e-5, None, ALU.add).then_inc(S.tok_step, 1)
    dve.wait_ge(S.tok_step, n + 1)
    V.reciprocal(T.nrm[:, 1, :], T.nrm[:, 0, :]).then_inc(S.tok_step, 1)
    dve.wait_ge(S.tok_step, n + 2)
    V.tensor_tensor(T.tok[:, :], R.flat[0:HD2, 0:512], T.nrm[:, 1, :], ALU.mult).then_inc(S.tok_ready, 1)
    dve.wait_ge(S.al_done, 1)
    al = per_head(R.flat[0:SLICES, 2560:2560 + INNER])
    V.tensor_reduce(T.ats[:, 0, :], al, AX.X, ALU.max).then_inc(S.al_step, 1)
    dve.wait_ge(S.al_step, 1)
    V.tensor_tensor(per_head(T.at[:, 0, :]), al, over_slices(T.ats[:, 0, :], SLICES), ALU.subtract).then_inc(S.al_step, 1)
    dve.wait_ge(S.al_exp, 1)
    V.tensor_reduce(T.ats[:, 1, :], per_head(T.at[:, 1, :]), AX.X, ALU.add).then_inc(S.al_step, 1)
    dve.wait_ge(S.al_step, 3)
    V.reciprocal(T.ats[:, 2, :], T.ats[:, 1, :]).then_inc(S.al_step, 1)
    dve.wait_ge(S.al_step, 4)
    V.tensor_tensor(per_head(T.at[:, 2, :]), per_head(T.at[:, 1, :]), over_slices(T.ats[:, 2, :], SLICES),
                    ALU.mult).then_inc(S.at_ready, 1)
    for c in range(CH):
        V.tensor_tensor(T.X[:, c, :], T.X[:, c, :], T.bout[:, :], ALU.add).then_inc(S.o3_step, 1)
    dve.wait_ge(S.o3_step, 3 * HEADS1 + CH)
    for c in range(CH):
        dve.wait_ge(S.out4_done, c + 1)
        V.tensor_tensor(T.X[:, c, :], T.X[:, c, :], R.banks[:, 2 + c, 0:DIM],
                        ALU.add).then_inc(S.y_ready, 1)


FIT_BELOW = WIN


NAMES = ["x", "src", "dst", "edge_type_8", "L0_gnn_W1", "L0_gnn_self_w1", "L0_gnn_b1", "L0_gnn_W2", "L0_gnn_self_w2",
         "L0_gnn_b2", "L0_ffn_bg", "L0_ffn_b2", "L1_gnn_W", "L1_ffn_W_fx", "L1_ffn_b_fx", "L1_ffn_W_x",
         "L1_ffn_W_slice", "L1_ffn_b_slice", "L1_ffn_W_q", "L1_ffn_W_k", "L1_ffn_W_v", "L1_ffn_W_out", "L1_ffn_b_out"]


def laid_out(inputs):
    import numpy as np

    a = {n: np.asarray(inputs[n]) for n in NAMES}
    a["wgT"] = np.asarray(inputs["L0_ffn_Wg"]).T
    a["w1T"] = np.asarray(inputs["L0_ffn_W1"]).transpose(0, 2, 1)
    a["w2T"] = np.asarray(inputs["L0_ffn_W2"]).transpose(0, 2, 1)
    a["b1T"] = np.asarray(inputs["L0_ffn_b1"]).reshape(EXPERTS * HB, P).T
    a["asrcT"] = np.asarray(inputs["L1_gnn_a_src"]).reshape(KD, P).T
    a["adst"] = np.asarray(inputs["L1_gnn_a_dst"]).reshape(-1)
    a["bxT"] = np.asarray(inputs["L1_ffn_b_x"]).reshape(IB, P).T
    a["temp"] = np.asarray(inputs["L1_ffn_temperature"]).reshape(-1)
    return {n: np.ascontiguousarray(v) for n, v in a.items()}


def kernel(**inputs):
    import concourse.bacc as bacc
    from concourse.bass_utils import run_bass_kernel_spmd

    arrays = laid_out(inputs)
    nc = bacc.Bacc("TRN2", target_bir_lowering=False, num_devices=1)
    D = namedtuple("Inputs", arrays)(*[
        nc.dram_tensor(f"in_{n}", v.shape, mybir.dt.from_np(v.dtype), kind="ExternalInput").ap()
        for n, v in arrays.items()])
    out = nc.dram_tensor("out_0", (NODES, DIM), F32, kind="ExternalOutput").ap()
    program(nc, D, out)
    r = run_bass_kernel_spmd(nc, [{f"in_{n}": v for n, v in arrays.items()}], core_ids=[0])
    return r.results[0]["out_0"]
```

```python
from collections import namedtuple
from contextlib import ExitStack

import concourse.bass as bass
from concourse import mybir

P = 128
F32 = mybir.dt.float32
F32R = mybir.dt.float32r
F16 = mybir.dt.float16
BF16 = mybir.dt.bfloat16
I32 = mybir.dt.int32
U32 = mybir.dt.uint32
ALU = mybir.AluOpType
ACT = mybir.ActivationFunctionType
AX = mybir.AxisListType

NODES, DIM, EDGES, TYPES = 625, 256, 20625, 8
CH = -(-NODES // P)
NP = CH * P
LAST = NODES - (CH - 1) * P
KD = DIM // P
HALF = NP // 2

TILES = 3
GE = TILES * P
GROUPS = -(-EDGES // GE)
FULL_ROWS = EDGES // GE
REST = EDGES - FULL_ROWS * GE
RING = 3
BATCH = 6
WIN = 16
KEYS = TYPES * WIN
WINDOWS = NP // WIN
OUTSIDE = 5000

EXPERTS, HID = 8, 1024
HB = HID // P
HRING = 4
PIECES = 4
FIRST_PIECE = HB - PIECES - 1
PIECE = (2 * HID + HB * DIM) // PIECES
HEADS1, HD1 = 4, 64
HEADS2, HD2, SLICES = 8, 64, 64
INNER = HEADS2 * HD2
IB = INNER // P
LN_EPS = 1e-5
NEG = -1e30


class Place:
    pass


def layout(nc):
    at = Place()
    at.pos = -(-nc.sbuf_base // 64) * 64
    size = {F32: 4, F32R: 4, F16: 2, BF16: 2, I32: 4, U32: 4}

    def put(name, shape, dt):
        n = size[dt]
        for s in shape[1:]:
            n *= s
        t = nc.alloc_sbuf_tensor_at(name, shape, dt, offset=at.pos)
        at.pos += -(-n // 64) * 64
        return t

    T = Place()
    T.X = put("X", [P, CH, DIM], F32)
    T.xn = put("xn", [P, CH, DIM], F32)
    T.xTh = put("xTh", [P, KD, NP], F32R)
    T.xTl = put("xTl", [P, KD, NP], F32R)
    T.stats = put("stats", [P, CH, 6], F32)
    T.mv = put("mv", [P, CH, 2], F32)
    T.std = put("std", [P, CH], F32)
    T.rstd = put("rstd", [P, CH], F32)
    T.eps = put("eps", [P, 1], F32)
    T.ident = put("ident", [P, P], F32)
    shared = at.pos

    T.A = put("A", [P, CH, TYPES, NP], F16)
    T.wh0 = put("wh0", [P, TYPES + 1, KD, DIM], F32R)
    T.wl0 = put("wl0", [P, TYPES + 1, KD, DIM], F32R)
    after_w0 = at.pos
    at.pos = after_w0 - (TYPES + 1) * KD * DIM * 4
    T.oh = put("oh", [P, GROUPS, TILES, P], F16)
    after_oh = at.pos
    at.pos = after_w0
    T.wh1 = put("wh1", [P, TYPES + 1, KD, DIM], F32R)
    T.wl1 = put("wl1", [P, TYPES + 1, KD, DIM], F32R)
    assert after_oh <= at.pos
    T.raw = put("raw", [P, TYPES + 1, KD, DIM], F32)
    T.xp = put("xp", [P, 3, CH, DIM], BF16)
    T.xr = put("xr", [P, CH, DIM], F32)
    T.b_bc = put("b_bc", [P, 2, DIM], F32)
    over = at.pos
    T.ei = put("ei", [GROUPS, 4, GE], I32)
    T.ef = put("ef", [GROUPS, 5, GE], F32)
    behind = at.pos
    at.pos = over
    T.ko = put("ko", [P, RING, TILES, CH * KEYS], F16)
    at.pos = max(at.pos, behind)
    T.dlim = put("dlim", [GROUPS, 4], F32)
    T.eT = put("eT", [P, 5, TILES, GROUPS], F32)
    T.iota = put("iota", [P, CH * KEYS], F16)
    T.src = put("src", [P, GROUPS, TILES], F16)
    T.add = put("add", [P, RING, CH * KEYS], F16)
    T.kgen = put("kgen", [P, 4, TILES * GROUPS], F32)
    T.w16 = put("w16", [P, 1], F32)
    T.lims = put("lims", [1, 2, GROUPS], F32)
    T.spanmax = put("spanmax", [1, 2], F32)
    T.bases = put("bases", [1, 64], I32)
    T.fits = put("fits", [1, 1], I32)
    end1 = at.pos
    at.pos = over
    T.yh = put("yh", [P, 2, NP], F32R)
    T.yl = put("yl", [P, 2, NP], F32R)
    T.C = put("C", [P, CH, NP], F32)
    end1 = max(end1, at.pos)
    assert end1 <= nc.sbuf_usable_end, end1
    c_pos = over + 2 * 2 * NP * 4

    at.pos = shared
    T.ewh0 = put("ewh0", [P, 2 * HID + HB * DIM], F32R)
    assert at.pos <= after_w0
    at.pos = shared + 2 * CH * TYPES * NP
    T.stg = put("stg", [P, 2, 2 * HID + HB * DIM], F32)
    assert at.pos <= after_w0
    T.ewl0 = put("ewl0", [P, 2 * HID + HB * DIM], F32R)
    T.ewh1 = put("ewh1", [P, 2 * HID + HB * DIM], F32R)
    T.ewl1 = put("ewl1", [P, 2 * HID + HB * DIM], F32R)
    assert at.pos <= over
    at.pos = shared + 16384
    T.ht = put("ht", [P, HRING, NP], F32)
    T.hh = put("hh", [P, HRING, NP], F32R)
    T.hl = put("hl", [P, HRING, NP], F32R)
    T.b1 = put("b1", [P, EXPERTS * HB], F32)
    T.b2 = put("b2", [EXPERTS, DIM], F32)
    assert at.pos <= shared + 2 * CH * TYPES * NP
    at.pos = c_pos + CH * NP * 4
    T.wg = put("wg", [P, 1, KD, EXPERTS], F32)
    T.bg = put("bg", [P, EXPERTS], F32)
    T.gate = put("gate", [P, CH, EXPERTS], F32)
    T.top = put("top", [P, CH, 8], F32)
    T.topi = put("topi", [P, CH, 8], U32)
    T.topf = put("topf", [P, CH, 8], F32)
    T.gp = put("gp", [P, 5, CH], F32)
    T.ctmp = put("ctmp", [P, CH, EXPERTS], F32)
    T.comb = put("comb", [P, CH, EXPERTS], F32)
    T.iota8 = put("iota8", [P, EXPERTS], F32)
    T.combT = put("combT", [EXPERTS, NP], F32)
    assert at.pos <= nc.sbuf_usable_end, at.pos

    at.pos = shared
    T.w3 = put("w3", [P, KD, DIM], F32)
    T.w3h = put("w3h", [P, KD, DIM], F32R)
    T.w3l = put("w3l", [P, KD, DIM], F32R)
    T.hp = put("hp", [P, CH, HEADS1, HD1 + 1], F32)
    T.hpT = put("hpT", [P, KD, NP], F32)
    T.asrc = put("asrc", [P, KD], F32)
    T.asrc_bc = put("asrc_bc", [P, KD, P], F32)
    T.adst = put("adst", [P, DIM], F32)
    T.edm = put("edm", [P, CH, DIM], F32)
    T.ed = put("ed", [P, CH, HEADS1], F32)
    T.es = put("es", [P, HEADS1, NP], F32)
    T.CT = put("CT", [P, CH, NP], F32)
    T.negm = put("negm", [P, CH, NP], F32)
    T.mtmp = put("mtmp", [P, 2, NP], F32)
    T.mes = put("mes", [P, CH, HEADS1], F32)
    T.tm = put("tm", [P, CH, HEADS1], F32)
    T.nm = put("nm", [P, CH, HEADS1], F32)
    T.t = put("t", [P, 2, NP], F32)
    T.lk = put("lk", [P, 2, NP], F32)
    T.ex = put("ex", [P, 2, NP], F32)
    T.pr = put("pr", [P, 2, NP], F32)
    T.pT = put("pT", [P, 2, NP], F32)
    T.den = put("den", [P, 2, CH], F32)
    T.o3 = put("o3", [P, CH, HD1], F32)
    assert at.pos <= c_pos, (at.pos, c_pos)

    T.wfx = put("wfx", [P, KD, INNER], F32)
    T.wfxh = put("wfxh", [P, KD, INNER], F32R)
    T.wfxl = put("wfxl", [P, KD, INNER], F32R)
    T.wx = put("wx", [P, KD, INNER], F32)
    T.wxh = put("wxh", [P, KD, INNER], F32R)
    T.wxl = put("wxl", [P, KD, INNER], F32R)
    T.wo = put("wo", [HD2, HEADS2, DIM], F32)
    T.wsl = put("wsl", [P, P], F32)
    T.wqkv = put("wqkv", [HD2, 3, HD2], F32)
    T.bfx = put("bfx", [P, INNER], F32)
    T.bx = put("bx", [P, IB], F32)
    T.bsl = put("bsl", [P, SLICES], F32)
    T.bout = put("bout", [P, DIM], F32)
    T.temp = put("temp", [P, 2, HEADS2], F32)
    T.ones = put("ones", [P, HD2], F32)
    assert at.pos <= c_pos, (at.pos, c_pos)
    at.pos = shared
    T.fx = put("fx", [P, CH, INNER], F32)
    T.xm = put("xm", [P, IB, NP], F32)
    T.lg = put("lg", [P, CH, INNER], F32)
    T.sm = put("sm", [P, 4, CH * HEADS2], F32)
    T.sw = put("sw", [P, CH, INNER], F32)
    T.swT = put("swT", [P, IB, NP], F32)
    T.nrm = put("nrm", [HD2, 2, INNER], F32)
    T.tok = put("tok", [HD2, INNER], F32)
    T.qk = put("qk", [HD2, 2, INNER], F32)
    T.v = put("v", [SLICES, INNER], F32)
    T.at = put("at", [SLICES, 3, INNER], F32)
    T.ats = put("ats", [SLICES, 3, HEADS2], F32)
    T.atT = put("atT", [SLICES, INNER], F32)
    T.osT = put("osT", [HD2, INNER], F32)
    T.M = put("M", [P, IB, DIM], F32)
    T.bounds = (at.pos,)
    return T


SEMAPHORES = """
x_zero x_in ei_set e_in b_in raw_in wh_ready wl_ready const_ready a_zero
ln_stats ln_aggr ln_std ln_rstd ln_out
tr_done xTh_ready xTl_ready
ef_ready ef_step eT_done eT_ready base_done base_step base_ready
src_ready oh_ready ko_ready counts_done staged added key_step w16_step A_built
xp_step xr_step xp_ready y_done yh_ready yl_ready out_done acc_read layer_step c_step C_built
stg0_in stg1_in ewh_ready ewl_ready experts_done
gate_in gate_const gate_mm gate_step gate_exp comb_ready combT_done combT_ready b2_done b2_added eb_in
h_done ht_ready hh_ready hl_ready h_used yacc_done yacc_added
w3_in w3_ready asrc_ready hp_done hp_ready hpT_done hpT_ready es_done es_ready ed_step
ct_done ct_ready negm_ready mes_step m_ready t_ready lk_ready ex_ready pr_ready pT_done pT_ready agg_done
o3_step x3_ready
w4_in wfx_ready wx_ready w4_const fx_done fx_ready xm_done xm_ready temp_step lg_done lg_step sm_exp sw_ready
swT_done swT_ready tok_done tok_step tok_ready qkv_done qkv_ready al_done al_step al_exp at_ready
atT_done atT_ready osT_done osT_ready M_done M_ready out4_done y_ready stored
""".split()


def program(nc, D, out):
    T = layout(nc)
    with ExitStack() as ctx:
        S = namedtuple("Semaphores", SEMAPHORES)(*[ctx.enter_context(nc.semaphore(n)) for n in SEMAPHORES])
        PS = ctx.enter_context(nc.psum_tensor("PS", [P, 8, 512], F32))
        block = ctx.enter_context(nc.Block())
        R = Place()
        R.banks = PS
        R.flat = PS[:, :, :].rearrange("p b n -> p (b n)")

        @block.sync
        def _(sp):
            load_everything(sp, nc, S, T, D, out)

        @block.gpsimd
        def _(pool):
            pool_program(pool, nc, S, T)

        @block.scalar
        def _(act):
            act_program(act, nc, S, T, R)

        @block.tensor
        def _(pe):
            pe_program(pe, nc, S, T, R)

        @block.vector
        def _(dve):
            dve_program(dve, nc, S, T, R)


def chunks(t, c):
    return P if c < CH - 1 else LAST


def load_everything(sp, nc, S, T, D, out):
    full = (CH - 1) * P
    sp.wait_ge(S.ei_set, 1)
    for n, e in enumerate((D.dst, D.edge_type_8, D.src)):
        sp.dma_start(T.ei[0:FULL_ROWS, n, :], e[0:FULL_ROWS * GE].rearrange("(g e) -> g e", e=GE)).then_inc(S.e_in, 16)
        sp.dma_start(T.ei[FULL_ROWS:FULL_ROWS + 1, n, 0:REST],
                     e[FULL_ROWS * GE:EDGES].rearrange("(g e) -> g e", g=1)).then_inc(S.e_in, 16)
    sp.wait_ge(S.x_zero, 1)
    sp.dma_start(T.X[:, 0:CH - 1, :], D.x[0:full, :].rearrange("(c p) d -> p c d", p=P)).then_inc(S.x_in, 16)
    sp.dma_start(T.X[0:LAST, CH - 1, :], D.x[full:NODES, :]).then_inc(S.x_in, 16)
    for n, (w, self_w, b) in enumerate(((D.L0_gnn_W1, D.L0_gnn_self_w1, D.L0_gnn_b1),
                                        (D.L0_gnn_W2, D.L0_gnn_self_w2, D.L0_gnn_b2))):
        if n:
            sp.wait_ge(S.wl_ready, 1)
        for k in range(KD):
            sp.dma_start(T.raw[:, 0:TYPES, k, :],
                         w[:, k * P:(k + 1) * P, :].rearrange("r p o -> p r o")).then_inc(S.raw_in, 16)
        sp.dma_start(T.raw[:, TYPES, :, :], self_w.rearrange("(k p) o -> p k o", p=P)).then_inc(S.raw_in, 16)
        sp.dma_start(T.b_bc[:, n, :], b.partition_broadcast(P)).then_inc(S.b_in, 16)
    sp.wait_ge(S.A_built, 1)
    sp.dma_start(T.wg[:, 0, :, :], D.wgT.rearrange("(k p) e -> p k e", p=P)).then_inc(S.gate_in, 16)
    sp.dma_start(T.bg[:, :], D.L0_ffn_bg.partition_broadcast(P)).then_inc(S.gate_in, 16)

    def expert(e):
        s = e % 2
        arrived = (S.stg0_in, S.stg1_in)[s]
        sp.dma_start(T.stg[:, s, 0:2 * HID].rearrange("p (k h) -> p k h", k=KD),
                     D.w1T[e].rearrange("(k p) h -> p k h", p=P)).then_inc(arrived, 16)
        sp.dma_start(T.stg[:, s, 2 * HID:].rearrange("p (b o) -> p b o", b=HB),
                     D.w2T[e].rearrange("(b p) o -> p b o", p=P)).then_inc(arrived, 16)

    sp.wait_ge(S.out_done, 2 + 2 * TYPES)
    expert(0)
    expert(1)
    sp.wait_ge(S.y_done, 4 * TYPES)
    sp.wait_ge(S.C_built, 1)
    sp.dma_start(T.b1[:, :], D.b1T).then_inc(S.eb_in, 16)
    sp.dma_start(T.b2[:, :], D.L0_ffn_b2).then_inc(S.eb_in, 16)
    for e in range(2, EXPERTS):
        sp.wait_ge(S.ewl_ready, (e - 1) * PIECES)
        expert(e)
    sp.wait_ge(S.experts_done, 1)
    sp.dma_start(T.w3[:, :, :], D.L1_gnn_W.rearrange("(k p) o -> p k o", p=P)).then_inc(S.w3_in, 16)
    sp.dma_start(T.adst[:, :], D.adst.partition_broadcast(P)).then_inc(S.w3_in, 16)
    sp.dma_start(T.asrc[:, :], D.asrcT).then_inc(S.w3_in, 16)
    sp.dma_start(T.wfx[:, :, :], D.L1_ffn_W_fx.rearrange("(k p) o -> p k o", p=P)).then_inc(S.w4_in, 16)
    sp.dma_start(T.wx[:, :, :], D.L1_ffn_W_x.rearrange("(k p) o -> p k o", p=P)).then_inc(S.w4_in, 16)
    sp.dma_start(T.wo[:, :, :], D.L1_ffn_W_out.rearrange("(h c) o -> c h o", c=HD2)).then_inc(S.w4_in, 16)
    for n, w in enumerate((D.L1_ffn_W_q, D.L1_ffn_W_k, D.L1_ffn_W_v)):
        sp.dma_start(T.wqkv[:, n, :], w).then_inc(S.w4_in, 16)
    sp.dma_start(T.bfx[:, :], D.L1_ffn_b_fx.partition_broadcast(P)).then_inc(S.w4_in, 16)
    sp.dma_start(T.bx[:, :], D.bxT).then_inc(S.w4_in, 16)
    sp.dma_start(T.bsl[:, :], D.L1_ffn_b_slice.partition_broadcast(P)).then_inc(S.w4_in, 16)
    sp.dma_start(T.bout[:, :], D.L1_ffn_b_out.partition_broadcast(P)).then_inc(S.w4_in, 16)
    sp.dma_start(T.temp[:, 0, :], D.temp.partition_broadcast(P)).then_inc(S.w4_in, 16)
    sp.wait_ge(S.w4_const, 1)
    for n in range(2):
        sp.dma_start(T.wsl[n * HD2:(n + 1) * HD2, n * HD2:(n + 1) * HD2], D.L1_ffn_W_slice).then_inc(S.w4_in, 16)
    sp.wait_ge(S.y_ready, CH)
    sp.dma_start(out[0:full, :].rearrange("(c p) d -> p c d", p=P), T.X[:, 0:CH - 1, :]).then_inc(S.stored, 16)
    sp.dma_start(out[full:NODES, :], T.X[0:LAST, CH - 1, :]).then_inc(S.stored, 16)
    sp.wait_ge(S.stored, 32)


W4_LOADS = 16 * 13
A_BY_DVE = 2


def pool_program(pool, nc, S, T):
    nc.gpsimd.memset(T.ei[:, 1:3, :], 0)
    nc.gpsimd.memset(T.ei[:, 0, :], OUTSIDE).then_inc(S.ei_set, 1)
    nc.gpsimd.memset(T.X[:, CH - 1, :], 0.0).then_inc(S.x_zero, 1)
    nc.gpsimd.memset(T.eps[:, :], LN_EPS).then_inc(S.const_ready, 1)
    nc.gpsimd.memset(T.ident[:, :], 0.0).then_inc(S.const_ready, 1)
    nc.gpsimd.iota(T.iota[:, :], pattern=[[1, CH * KEYS]], base=0, channel_multiplier=0,
                   allow_small_or_imprecise_dtypes=True).then_inc(S.const_ready, 1)
    pool.wait_ge(S.const_ready, 3)
    nc.gpsimd.affine_select(out=T.ident[:, :], in_=T.ident[:, :], compare_op=ALU.not_equal, fill=1.0,
                            base=0, pattern=[[-1, P]], channel_multiplier=1).then_inc(S.const_ready, 1)
    nc.gpsimd.memset(T.A[:, A_BY_DVE:CH, :, :].rearrange("p c r n -> p (c r n)").bitcast(F32), 0.0).then_inc(S.a_zero, 1)

    pool.wait_ge(S.A_built, 1)
    pool.wait_ge(S.raw_in, 96)
    nc.gpsimd.tensor_copy(T.wh1[:, :, :, :], T.raw[:, :, :, :]).then_inc(S.wh_ready, 1)
    pool.wait_ge(S.wh_ready, 2)
    nc.gpsimd.tensor_tensor(T.wl1[:, :, :, :], T.raw[:, :, :, :], T.wh1[:, :, :, :].bitcast(F32),
                            ALU.subtract).then_inc(S.wl_ready, 1)
    nc.gpsimd.iota(T.iota8[:, :], pattern=[[1, EXPERTS]], base=0, channel_multiplier=0,
                   allow_small_or_imprecise_dtypes=True).then_inc(S.gate_const, 1)
    nc.gpsimd.tensor_tensor(T.C[:, :, :], T.A[:, :, 0, :], T.A[:, :, 1, :], ALU.add).then_inc(S.c_step, 1)
    for r in range(2, TYPES):
        pool.wait_ge(S.c_step, r - 1)
        nc.gpsimd.tensor_tensor(T.C[:, :, :], T.C[:, :, :], T.A[:, :, r, :], ALU.add).then_inc(S.c_step, 1)
    pool.wait_ge(S.c_step, TYPES - 1)
    nc.gpsimd.engine_nop().then_inc(S.C_built, 1)
    pool.wait_ge(S.experts_done, 1)
    nc.gpsimd.memset(T.hp[:, :, :, HD1:HD1 + 1], 1.0).then_inc(S.w3_ready, 1)
    nc.gpsimd.memset(T.wsl[:, :], 0.0).then_inc(S.w4_const, 1)
    nc.gpsimd.memset(T.ones[:, :], 1.0).then_inc(S.w4_const, 1)
    pool.wait_ge(S.w3_in, 48)
    nc.gpsimd.tensor_copy(T.w3h[:, :, :], T.w3[:, :, :]).then_inc(S.w3_ready, 1)
    pool.wait_ge(S.w3_ready, 2)
    nc.gpsimd.tensor_tensor(T.w3l[:, :, :], T.w3[:, :, :], T.w3h[:, :, :].bitcast(F32),
                            ALU.subtract).then_inc(S.w3_ready, 1)
    pool.wait_ge(S.w4_in, W4_LOADS)
    for raw, hi, lo, ready in ((T.wfx, T.wfxh, T.wfxl, S.wfx_ready), (T.wx, T.wxh, T.wxl, S.wx_ready)):
        nc.gpsimd.tensor_copy(hi[:, :, :], raw[:, :, :]).then_inc(ready, 1)
        pool.wait_ge(ready, 1)
        nc.gpsimd.tensor_tensor(lo[:, :, :], raw[:, :, :], hi[:, :, :].bitcast(F32),
                                ALU.subtract).then_inc(ready, 1)


def act_program(act, nc, S, T, R):
    A = nc.scalar

    def ln(n):
        if n == 0:
            act.wait_ge(S.const_ready, 1)
        act.wait_ge(S.ln_aggr, CH * (n + 1))
        A.activation(T.std[:, :], T.mv[:, :, 1], ACT.Sqrt, bias=T.eps[:, 0:1]).then_inc(S.ln_std, 1)

    def xT(n):
        act.wait_ge(S.tr_done, n + 1)
        A.activation(T.xTh[:, :, :].rearrange("p k n -> p (k n)"), R.flat[:, 0:KD * NP], ACT.Copy).then_inc(S.xTh_ready, 1)

    def split3(n):
        for part in range(3):
            if part == 0:
                act.wait_ge(S.ln_out if n == 0 else S.layer_step, CH if n == 0 else 2)
                src = T.xn
            else:
                act.wait_ge(S.xr_step, 2 * n + part)
                src = T.xr
            A.activation(T.xp[:, part, :, :], src[:, :, :], ACT.Copy).then_inc(S.xp_step, 1)

    def stage_counts(g0):
        with act.Fori(0, GROUPS // RING) as i:
            for b in range(RING):
                act.wait_ge(S.counts_done, g0 + i * RING + b + RING + 1)
                act.wait_ge(S.added, g0 + i * RING + b + 1)
                A.activation(T.add[:, b, :], R.flat[:, 1024 * b:1024 * b + CH * KEYS], ACT.Copy).then_inc(S.staged, 1)

    def layer(n):
        j0 = 2 * TYPES * n
        with act.Fori(0, TYPES) as r:
            for k in range(KD):
                act.wait_ge(S.y_done, r * 2 + (j0 + k + 1))
                act.wait_ge(S.out_done, r * 2 + (j0 + k + 1))
                A.activation(T.yh[:, k, :].rearrange("p (h n) -> p h n", h=2),
                             R.banks[:, 2 * k:2 * k + 2, 0:HALF], ACT.Copy).then_inc(S.yh_ready, 1)

    ln(0)
    xT(0)
    split3(0)
    act.wait_ge(S.raw_in, 48)
    A.activation(T.wh0[:, :, :, :], T.raw[:, :, :, :], ACT.Copy).then_inc(S.wh_ready, 1)
    act.wait_ge(S.base_ready, 1)
    fits = act.value_load(T.fits[0:1, 0:1], min_val=0, max_val=1)
    A.sem_inc(S.staged, RING)
    with act.If(fits == 1):
        stage_counts(0)
    with act.Else():
        with act.Fori(0, WINDOWS) as w:
            stage_counts(w * GROUPS)
    layer(0)
    xT(1)
    split3(1)
    layer(1)

    ln(1)
    xT(2)
    act.wait_ge(S.y_done, 4 * TYPES)
    act.wait_ge(S.out_done, 2 + 4 * TYPES)
    act.wait_ge(S.C_built, 1)

    def high(piece, s, n):
        act.wait_ge((S.stg0_in, S.stg1_in)[s], n * 32 + 32)
        w = slice(piece * PIECE, (piece + 1) * PIECE)
        A.activation((T.ewh0, T.ewh1)[s][:, w], T.stg[:, s, w], ACT.Copy).then_inc(S.ewh_ready, 1)

    for piece in range(PIECES):
        high(piece, 0, 0)
    act.wait_ge(S.gate_step, CH + 2)
    A.activation(T.gp[:, 1, :], T.gp[:, 0, :], ACT.Exp).then_inc(S.gate_exp, 1)
    act.wait_ge(S.combT_done, 1)
    A.activation(T.combT[:, :], R.flat[0:EXPERTS, 1536:1536 + NP], ACT.Copy).then_inc(S.combT_ready, 1)
    act.wait_ge(S.eb_in, 32)
    A.sem_inc(S.ht_ready, 2)

    def experts(i, last):
        for s in range(2):
            for hb in range(HB):
                b = hb % 2
                act.wait_ge(S.h_done, (i * 2 + s) * HB + hb + 1)
                act.wait_ge(S.hl_ready, (i * 2 + s) * HB + hb + 1)
                A.activation(T.ht[:, hb % HRING, :].rearrange("p (h n) -> p h n", h=2),
                             R.banks[:, 2 * b:2 * b + 2, 0:HALF], ACT.Relu,
                             bias=T.b1[:, bass.ds((i * 2 + s) * HB + hb, 1)]).then_inc(S.ht_ready, 1)
                if FIRST_PIECE <= hb < FIRST_PIECE + PIECES and not (last and s == 1):
                    act.wait_ge(S.h_used, (i * 2 + s) * HB + HB)
                    high(hb - FIRST_PIECE, 1 - s, i + s)

    with act.Fori(0, EXPERTS // 2 - 1) as i:
        experts(i, False)
    experts(EXPERTS // 2 - 1, True)

    ln(2)
    xT(3)
    act.wait_ge(S.hpT_done, 1)
    for k in range(KD):
        A.activation(T.hpT[:, k, :].rearrange("p (h n) -> p h n", h=2),
                     R.banks[:, 2 * k:2 * k + 2, 0:HALF], ACT.Copy).then_inc(S.hpT_ready, 1)
    for h in range(HEADS1):
        b = h % 2
        act.wait_ge(S.es_done, h + 1)
        A.activation(T.es[:, h, :].rearrange("p (h n) -> p h n", h=2),
                     R.banks[:, 2 * b:2 * b + 2, 0:HALF], ACT.Copy).then_inc(S.es_ready, 1)
    for c in range(CH):
        act.wait_ge(S.ct_done, c + 1)
        A.activation(T.CT[:, c, :], R.flat[:, 2048 + 1024 * (c % 2):2048 + 1024 * (c % 2) + NP],
                     ACT.Copy).then_inc(S.ct_ready, 1)

    def probs_T(j):
        act.wait_ge(S.pT_done, j + 1)
        if j >= 2:
            act.wait_ge(S.agg_done, j - 1)
        A.activation(T.pT[:, j % 2, :], R.flat[:, 1024 * (j % 2):1024 * (j % 2) + NP], ACT.Copy).then_inc(S.pT_ready, 1)

    act.wait_ge(S.m_ready, 1)
    for j in range(HEADS1 * CH):
        h, c = divmod(j, CH)
        act.wait_ge(S.lk_ready, j + 1)
        if j >= 2:
            act.wait_ge(S.pr_ready, j - 1)
        A.activation(T.ex[:, j % 2, :], T.lk[:, j % 2, :], ACT.Exp, bias=T.nm[:, c, h:h + 1]).then_inc(S.ex_ready, 1)
        if j >= 2:
            probs_T(j - 2)
    probs_T(HEADS1 * CH - 2)
    probs_T(HEADS1 * CH - 1)

    ln(3)
    xT(4)
    act.wait_ge(S.w4_in, W4_LOADS)
    for b in range(IB):
        act.wait_ge(S.xm_done, b + 1)
        A.activation(T.xm[:, b, :].rearrange("p (h n) -> p h n", h=2),
                     R.banks[:, 2 * (b % 2):2 * (b % 2) + 2, 0:HALF], ACT.Identity,
                     bias=T.bx[:, b:b + 1]).then_inc(S.xm_ready, 1)
    for c in range(CH):
        act.wait_ge(S.lg_step, 4 * c + 4)
        A.activation(T.sw[:, c, :], T.lg[:, c, :], ACT.Exp).then_inc(S.sm_exp, 1)
    act.wait_ge(S.qkv_done, 1)
    A.activation(T.qk[:, :, :].rearrange("p a n -> p (a n)"), R.flat[0:HD2, 1024:2048], ACT.Copy).then_inc(S.qkv_ready, 1)
    A.activation(T.v[:, :], R.flat[0:SLICES, 2048:2560], ACT.Copy).then_inc(S.qkv_ready, 1)
    act.wait_ge(S.al_step, 2)
    A.activation(T.at[:, 1, :], T.at[:, 0, :], ACT.Exp, scale=float(HD2) ** -0.5).then_inc(S.al_exp, 1)
    act.wait_ge(S.atT_done, 1)
    A.activation(T.atT[:, :], R.flat[0:SLICES, 0:INNER], ACT.Copy).then_inc(S.atT_ready, 1)
    act.wait_ge(S.osT_done, 1)
    A.activation(T.osT[:, :], R.flat[0:HD2, 512:512 + INNER], ACT.Copy).then_inc(S.osT_ready, 1)
    act.wait_ge(S.swT_done, 1)
    A.activation(T.swT[:, :, :].rearrange("p b n -> p (b n)"), R.flat[:, 1024:1024 + IB * NP], ACT.Copy).then_inc(S.swT_ready, 1)
    act.wait_ge(S.M_done, 1)
    A.activation(T.M[:, :, :].rearrange("p b n -> p (b n)"), R.flat[:, 0:IB * DIM], ACT.Copy).then_inc(S.M_ready, 1)


def pe_program(pe, nc, S, T, R):
    def mm3(o, lh, ll, rh, rl, start, stop, **kw):
        nc.tensor.matmul(o, lh, rh, start=start, stop=False, **kw)
        nc.tensor.matmul(o, lh, rl, start=False, stop=False, **kw)
        return nc.tensor.matmul(o, ll, rh, start=False, stop=stop, **kw)

    def transpose_x(n):
        if n == 1:
            pe.wait_ge(S.layer_step, 2)
            pe.wait_ge(S.yl_ready, 2 + 2 * TYPES)
        elif n:
            pe.wait_ge(S.ln_out, CH * n)
        else:
            pe.wait_ge(S.ln_out, CH)
        for k in range(KD):
            for c in range(CH):
                o = (k * CH + c) * P
                mm = nc.tensor.transpose(R.flat[:, o:o + P], T.xn[:, c, k * P:(k + 1) * P], T.ident[:, :])
        mm.then_inc(S.tr_done, 1)

    def edges():
        pe.wait_ge(S.const_ready, 4)
        pe.wait_ge(S.ef_ready, 1)
        for n in range(5):
            for j in range(TILES):
                o = 2048 + (0 if n < 3 else 512) + ((n % 3) * TILES + j) * GROUPS
                mm = nc.tensor.transpose(R.flat[:, o:o + GROUPS], T.ef[:, n, j * P:(j + 1) * P],
                                         T.ident[0:GROUPS, 0:GROUPS])
        mm.then_inc(S.eT_done, 1)
        for n in range(2):
            o = 3072 + n * GROUPS
            mm = nc.tensor.transpose(R.flat[0:1, o:o + GROUPS], T.dlim[:, n:n + 1], T.ident[0:GROUPS, 0:GROUPS])
        mm.then_inc(S.base_done, 1)

    def counts(g0):
        with pe.Fori(0, GROUPS // RING) as i:
            for b in range(RING):
                pe.wait_ge(S.oh_ready, i * RING + b + 1)
                pe.wait_ge(S.ko_ready, g0 + i * RING + b + 1)
                pe.wait_ge(S.staged, g0 + i * RING + b + 1)
                for o, end in ((0, 512), (512, CH * KEYS)):
                    for j in range(TILES):
                        mm = nc.tensor.matmul(R.flat[:, 1024 * b + o:1024 * b + end], T.oh[:, bass.ds(i * RING + b, 1), j, :].rearrange("p a n -> p (a n)"),
                                              T.ko[:, b, j, o:end], start=(j == 0), stop=(j == TILES - 1))
                mm.then_inc(S.counts_done, 1)

    def layer(n):
        wh, wl = ((T.wh0, T.wl0), (T.wh1, T.wl1))[n]
        j0 = 2 * TYPES * n

        def acc(c):
            return R.flat[:, 2048 + c * DIM:2048 + (c + 1) * DIM]

        def own_rows():
            pe.wait_ge(S.wh_ready, n + 1)
            pe.wait_ge(S.wl_ready, n + 1)
            pe.wait_ge(S.xTl_ready, n + 1)
            pe.wait_ge(S.xTh_ready, n + 1)
            for c in range(CH):
                for k in range(KD):
                    x = slice(c * P, (c + 1) * P)
                    mm3(acc(c), T.xTh[:, k, x], T.xTl[:, k, x], wh[:, TYPES, k, :], wl[:, TYPES, k, :],
                        start=(k == 0 and c % 2 == 0), stop=False, skip_group_check=True)

        pe.wait_ge(S.xp_step, 3 * (n + 1))

        def aggregate(r, k, j):
            pe.wait_ge(S.yl_ready, j + 1)
            for half in range(2):
                for c in range(CH):
                    for part in range(3):
                        mm = nc.tensor.matmul(
                            R.banks[:, 2 * k + half, 0:HALF], T.xp[:, part, c, k * P:(k + 1) * P],
                            (T.A[:, c, r, half * HALF:(half + 1) * HALF] if type(r) is int else
                             T.A[:, c, bass.ds(r, 1), half * HALF:(half + 1) * HALF].rearrange("p a n -> p (a n)")),
                            start=(c == 0 and part == 0), stop=(c == CH - 1 and part == 2))
            mm.then_inc(S.y_done, 1)

        def product(r, k, j, last=False):
            pe.wait_ge(S.yl_ready, j + 3)
            for c in range(CH):
                x = slice(c * P, (c + 1) * P)
                if type(r) is int:
                    h, l = wh[:, r, k, :], wl[:, r, k, :]
                else:
                    h = wh[:, bass.ds(r, 1), k, :].rearrange("p a n -> p (a n)")
                    l = wl[:, bass.ds(r, 1), k, :].rearrange("p a n -> p (a n)")
                mm = mm3(acc(c), T.yh[:, k, x], T.yl[:, k, x], h, l, start=False, stop=last, skip_group_check=True)
            mm.then_inc(S.out_done, 1)

        aggregate(0, 0, j0)
        own_rows()
        with pe.Fori(0, TYPES - 1) as r:
            aggregate(r, 1, r * 2 + (j0 + 1))
            product(r, 0, r * 2 + j0)
            aggregate(r + 1, 0, r * 2 + (j0 + 2))
            product(r, 1, r * 2 + (j0 + 1))
        j = j0 + 2 * TYPES - 2
        aggregate(TYPES - 1, 1, j + 1)
        product(TYPES - 1, 0, j)
        product(TYPES - 1, 1, j + 1, last=True)

    edges()
    transpose_x(0)
    pe.wait_ge(S.base_ready, 1)
    fits = pe.value_load(T.fits[0:1, 0:1], min_val=0, max_val=1)
    nc.tensor.sem_inc(S.counts_done, RING)
    with pe.If(fits == 1):
        counts(0)
    with pe.Else():
        with pe.Fori(0, WINDOWS) as w:
            counts(w * GROUPS)
    nc.tensor.sem_inc(S.out_done, 2)
    pe.wait_ge(S.A_built, 1)
    layer(0)
    transpose_x(1)
    layer(1)

    transpose_x(2)
    pe.wait_ge(S.xTh_ready, 3)
    pe.wait_ge(S.xTl_ready, 3)
    pe.wait_ge(S.gate_in, 32)
    pe.wait_ge(S.acc_read, 2 * CH)
    for c in range(CH):
        for k in range(KD):
            x = slice(c * P, (c + 1) * P)
            for a in (T.xTh, T.xTl):
                mm = nc.tensor.matmul(R.flat[:, 2048 + c * EXPERTS:2048 + (c + 1) * EXPERTS],
                                      a[:, k, x].bitcast(F32), T.wg[:, 0, k, :],
                                      start=(k == 0 and a is T.xTh), stop=(k == KD - 1 and a is T.xTl))
    mm.then_inc(S.gate_mm, 1)
    pe.wait_ge(S.comb_ready, 1)
    for c in range(CH):
        mm = nc.tensor.transpose(R.flat[0:EXPERTS, 1536 + c * P:1536 + (c + 1) * P], T.comb[:, c, :], T.ident[:, :])
    mm.then_inc(S.combT_done, 1)
    pe.wait_ge(S.combT_ready, 1)
    pe.wait_ge(S.eb_in, 32)

    def yacc(c):
        return R.flat[:, 2048 + c * DIM:2048 + (c + 1) * DIM]

    for c in range(CH):
        mm = nc.tensor.matmul(yacc(c), T.combT[:, c * P:(c + 1) * P], T.b2[:, :], start=True, stop=True)
    mm.then_inc(S.b2_done, 1)
    pe.wait_ge(S.b2_added, 1)
    nc.tensor.sem_inc(S.h_used, HB)

    def hidden(wh, wl, hb, j):
        b = hb % 2
        pe.wait_ge(S.ht_ready, j + 1)
        for half in range(2):
            for k in range(KD):
                w = slice(k * HID + hb * P, k * HID + (hb + 1) * P)
                n = slice(half * HALF, (half + 1) * HALF)
                mm = mm3(R.banks[:, 2 * b + half, 0:HALF], wh[:, w], wl[:, w], T.xTh[:, k, n], T.xTl[:, k, n],
                         start=(k == 0), stop=(k == KD - 1))
        mm.then_inc(S.h_done, 1)

    def outputs(wh, wl, hb, j, e):
        pe.wait_ge(S.hl_ready, j + HRING + 1)
        w = slice(2 * HID + hb * DIM, 2 * HID + (hb + 1) * DIM)
        for c in range(CH):
            if hb == 0 and c % 2 == 0:
                pe.wait_ge(S.yacc_added, e * CH + min(c + 2, CH))
            x = slice(c * P, (c + 1) * P)
            mm = mm3(yacc(c), T.hh[:, hb % HRING, x], T.hl[:, hb % HRING, x], wh[:, w], wl[:, w],
                     start=(hb == 0 and c % 2 == 0), stop=(hb == HB - 1), skip_group_check=True)
        mm.then_inc(S.h_used, 1)

    LAG = 2
    sets = ((T.ewh0, T.ewl0), (T.ewh1, T.ewl1))

    def experts(i, first):
        for n in range(2 * HB):
            s, hb = divmod(n, HB)
            if hb == 0:
                pe.wait_ge(S.ewl_ready, (i * 2 + s + 1) * PIECES)
            hidden(*sets[s], hb, i * (2 * HB) + n)
            if n >= LAG or not first:
                m = n - LAG
                s2, hb2 = divmod(m % (2 * HB), HB)
                outputs(*sets[s2], hb2, i * (2 * HB) + m, i * 2 + (s2 if m >= 0 else s2 - 2))

    pe.wait_ge(S.xTl_ready, 3)
    experts(0, True)
    with pe.Fori(1, EXPERTS // 2) as i:
        experts(i, False)
    for m in range(EXPERTS * HB - LAG, EXPERTS * HB):
        outputs(*sets[1], m % HB, m, EXPERTS - 1)

    transpose_x(3)
    pe.wait_ge(S.xTh_ready, 4)
    pe.wait_ge(S.xTl_ready, 4)
    pe.wait_ge(S.w3_ready, 3)
    for f in range(KD):
        for half in range(2):
            n = slice(half * HALF, (half + 1) * HALF)
            for k in range(KD):
                w = slice(f * P, (f + 1) * P)
                mm = mm3(R.banks[:, 2 * f + half, 0:HALF], T.w3h[:, k, w], T.w3l[:, k, w],
                         T.xTh[:, k, n], T.xTl[:, k, n], start=(k == 0), stop=(k == KD - 1))
    mm.then_inc(S.hpT_done, 1)
    for c in range(CH):
        x = slice(c * P, (c + 1) * P)
        for k in range(KD):
            mm = mm3(R.flat[:, 2048 + c * DIM:2048 + (c + 1) * DIM], T.xTh[:, k, x], T.xTl[:, k, x],
                     T.w3h[:, k, :], T.w3l[:, k, :], start=(k == 0), stop=(k == KD - 1))
    mm.then_inc(S.hp_done, 1)
    pe.wait_ge(S.asrc_ready, 1)
    pe.wait_ge(S.hpT_ready, 2)
    for h in range(HEADS1):
        k, o = divmod(h * HD1, P)
        b = h % 2
        if h >= 2:
            pe.wait_ge(S.es_ready, h - 1)
        for half in range(2):
            mm = nc.tensor.matmul(R.banks[:, 2 * b + half, 0:HALF], T.asrc_bc[o:o + HD1, k, :],
                                  T.hpT[o:o + HD1, k, half * HALF:(half + 1) * HALF], start=True, stop=True)
        mm.then_inc(S.es_done, 1)
    pe.wait_ge(S.hp_ready, 1)
    for c in range(CH):
        if c >= 2:
            pe.wait_ge(S.ct_ready, c - 1)
        for s in range(CH):
            o = 2048 + 1024 * (c % 2) + s * P
            mm = nc.tensor.transpose(R.flat[:, o:o + P], T.C[:, s, c * P:(c + 1) * P], T.ident[:, :])
        mm.then_inc(S.ct_done, 1)

    def turn(j):
        pe.wait_ge(S.pr_ready, j + 1)
        if j >= 2:
            pe.wait_ge(S.pT_ready, j - 1)
        for s in range(CH):
            o = 1024 * (j % 2) + s * P
            mm = nc.tensor.transpose(R.flat[:, o:o + P], T.pr[:, j % 2, s * P:(s + 1) * P], T.ident[:, :])
        mm.then_inc(S.pT_done, 1)

    def gather(j):
        h, c = divmod(j, CH)
        pe.wait_ge(S.pT_ready, j + 1)
        if c == 0 and h >= 2:
            pe.wait_ge(S.x3_ready, h - 1)
        o = 2048 + 512 * (h % 2) + c * (HD1 + 1)
        for s in range(CH):
            mm = nc.tensor.matmul(R.flat[:, o:o + HD1 + 1], T.pT[:, j % 2, s * P:(s + 1) * P], T.hp[:, s, h, :],
                                  start=(s == 0), stop=(s == CH - 1))
        mm.then_inc(S.agg_done, 1)

    pe.wait_ge(S.es_ready, HEADS1)
    pe.wait_ge(S.ct_ready, CH)
    for j in range(HEADS1 * CH):
        turn(j)
        if j >= 1:
            gather(j - 1)
    gather(HEADS1 * CH - 1)

    transpose_x(4)
    pe.wait_ge(S.xTh_ready, 5)
    pe.wait_ge(S.xTl_ready, 5)
    pe.wait_ge(S.wx_ready, 2)
    pe.wait_ge(S.w4_in, W4_LOADS)
    for b in range(IB):
        if b >= 2:
            pe.wait_ge(S.xm_ready, b - 1)
        for half in range(2):
            n = slice(half * HALF, (half + 1) * HALF)
            for k in range(KD):
                w = slice(b * P, (b + 1) * P)
                mm = mm3(R.banks[:, 2 * (b % 2) + half, 0:HALF], T.wxh[:, k, w], T.wxl[:, k, w],
                         T.xTh[:, k, n], T.xTl[:, k, n], start=(k == 0), stop=(k == KD - 1))
        mm.then_inc(S.xm_done, 1)
    pe.wait_ge(S.wfx_ready, 2)
    for c in range(CH):
        if c >= 2:
            pe.wait_ge(S.fx_ready, c - 1)
        x = slice(c * P, (c + 1) * P)
        for k in range(KD):
            mm = mm3(R.banks[:, 4 + c % 2, :], T.xTh[:, k, x], T.xTl[:, k, x], T.wfxh[:, k, :], T.wfxl[:, k, :],
                     start=(k == 0), stop=(k == KD - 1))
        mm.then_inc(S.fx_done, 1)
    pe.wait_ge(S.xm_ready, IB)
    for c in range(CH):
        if c >= 2:
            pe.wait_ge(S.lg_step, 4 * (c - 2) + 1)
        for b in range(IB):
            mm = nc.tensor.matmul(R.banks[:, 6 + c % 2, b * P:(b + 1) * P], T.xm[:, b, c * P:(c + 1) * P],
                                  T.wsl[:, :], start=True, stop=True)
        mm.then_inc(S.lg_done, 1)
    pe.wait_ge(S.sw_ready, CH)
    pe.wait_ge(S.fx_ready, CH)
    pe.wait_ge(S.w4_const, 2)
    for c in range(CH):
        k = chunks(T, c)
        nc.tensor.matmul(R.flat[0:HD2, 512:1024], T.ones[0:k, :], T.sw[0:k, c, :], start=(c == 0), stop=(c == CH - 1))
    for h in range(HEADS2):
        w = slice(h * HD2, (h + 1) * HD2)
        for c in range(CH):
            k = chunks(T, c)
            mm = nc.tensor.matmul(R.flat[0:HD2, w], T.fx[0:k, c, w], T.sw[0:k, c, w], start=(c == 0), stop=(c == CH - 1))
    mm.then_inc(S.tok_done, 1)
    pe.wait_ge(S.tok_ready, 1)
    for n in range(2):
        nc.tensor.matmul(R.flat[0:HD2, 1024 + 512 * n:1536 + 512 * n], T.wqkv[:, n, :], T.tok[:, :], start=True, stop=True)
    for h in range(HEADS2):
        w = slice(h * HD2, (h + 1) * HD2)
        mm = nc.tensor.matmul(R.flat[0:SLICES, 2048 + h * HD2:2048 + (h + 1) * HD2], T.tok[:, w], T.wqkv[:, 2, :],
                              start=True, stop=True)
    mm.then_inc(S.qkv_done, 1)
    pe.wait_ge(S.qkv_ready, 2)
    for h in range(HEADS2):
        w = slice(h * SLICES, (h + 1) * SLICES)
        mm = nc.tensor.matmul(R.flat[0:SLICES, 2560 + h * SLICES:2560 + (h + 1) * SLICES], T.qk[:, 0, w], T.qk[:, 1, w],
                              start=True, stop=True)
    mm.then_inc(S.al_done, 1)
    pe.wait_ge(S.at_ready, 1)
    for h in range(HEADS2):
        w = slice(h * SLICES, (h + 1) * SLICES)
        mm = nc.tensor.transpose(R.flat[0:SLICES, w], T.at[:, 2, w], T.ident[0:SLICES, 0:SLICES])
    mm.then_inc(S.atT_done, 1)
    pe.wait_ge(S.atT_ready, 1)
    for h in range(HEADS2):
        w = slice(h * HD2, (h + 1) * HD2)
        mm = nc.tensor.matmul(R.flat[0:HD2, 512 + h * SLICES:512 + (h + 1) * SLICES], T.v[:, w], T.atT[:, w],
                              start=True, stop=True)
    mm.then_inc(S.osT_done, 1)
    for b in range(IB):
        for c in range(CH):
            o = 1024 + (b * CH + c) * P
            mm = nc.tensor.transpose(R.flat[:, o:o + P], T.sw[:, c, b * P:(b + 1) * P], T.ident[:, :])
    mm.then_inc(S.swT_done, 1)
    pe.wait_ge(S.osT_ready, 1)
    for h in range(HEADS2):
        b, o = divmod(h * SLICES, P)
        mm = nc.tensor.matmul(R.flat[o:o + SLICES, b * DIM:(b + 1) * DIM], T.osT[:, h * SLICES:(h + 1) * SLICES],
                              T.wo[:, h, :], start=True, stop=True)
    mm.then_inc(S.M_done, 1)
    pe.wait_ge(S.M_ready, 1)
    pe.wait_ge(S.swT_ready, 1)
    for c in range(CH):
        for b in range(IB):
            mm = nc.tensor.matmul(R.banks[:, 2 + c, 0:DIM], T.swT[:, b, c * P:(c + 1) * P],
                                  T.M[:, b, :], start=(b == 0), stop=(b == IB - 1))
        mm.then_inc(S.out4_done, 1)


def dve_program(dve, nc, S, T, R):
    V = nc.vector

    def ln(n):
        for c in range(CH):
            V.bn_stats(T.stats[:, c, :], T.X[:, c, :]).then_inc(S.ln_stats, 1)
        for c in range(CH):
            dve.wait_ge(S.ln_stats, CH * n + c + 1)
            V.bn_aggr(T.mv[:, c, :], T.stats[:, c, :]).then_inc(S.ln_aggr, 1)
        dve.wait_ge(S.ln_std, n + 1)
        V.reciprocal(T.rstd[:, :], T.std[:, :]).then_inc(S.ln_rstd, 1)
        dve.wait_ge(S.ln_rstd, n + 1)
        for c in range(CH):
            V.tensor_scalar(T.xn[:, c, :], T.X[:, c, :], T.mv[:, c, 0:1], T.rstd[:, c:c + 1],
                            ALU.subtract, ALU.mult).then_inc(S.ln_out, 1)

    def xT(n):
        dve.wait_ge(S.xTh_ready, n + 1)
        V.tensor_tensor(T.xTl[:, :, :].rearrange("p k n -> p (k n)"), R.flat[:, 0:KD * NP],
                        T.xTh[:, :, :].rearrange("p k n -> p (k n)").bitcast(F32), ALU.subtract).then_inc(S.xTl_ready, 1)

    def split3(n):
        dve.wait_ge(S.xp_step, 3 * n + 1)
        V.tensor_tensor(T.xr[:, :, :], T.xn[:, :, :], T.xp[:, 0, :, :], ALU.subtract).then_inc(S.xr_step, 1)
        dve.wait_ge(S.xp_step, 3 * n + 2)
        dve.wait_ge(S.xr_step, 2 * n + 1)
        V.tensor_tensor(T.xr[:, :, :], T.xr[:, :, :], T.xp[:, 1, :, :], ALU.subtract).then_inc(S.xr_step, 1)

    def edges():
        dve.wait_ge(S.e_in, 96)
        V.tensor_scalar(T.ei[:, 3, :], T.ei[:, 2, :], -P, None, ALU.bitwise_and).then_inc(S.src_ready, 1)
        V.tensor_copy(T.ef[:, 0:2, :], T.ei[:, 0:2, :]).then_inc(S.ef_step, 1)
        dve.wait_ge(S.src_ready, 1)
        V.tensor_copy(T.ef[:, 3, :], T.ei[:, 3, :]).then_inc(S.src_ready, 1)
        V.tensor_tensor(T.ef[:, 2, :], T.ei[:, 2, :], T.ei[:, 3, :], ALU.subtract).then_inc(S.src_ready, 1)
        dve.wait_ge(S.ef_step, 1)
        V.tensor_reduce(T.dlim[:, 0:1], T.ef[:, 0, :], AX.X, ALU.min).then_inc(S.ef_step, 1)
        V.scalar_tensor_tensor(T.ef[:, 4, :], T.ef[:, 0, :], float(OUTSIDE), T.ef[:, 0, :],
                               ALU.is_lt, ALU.mult).then_inc(S.ef_step, 1)
        dve.wait_ge(S.ef_step, 3)
        V.tensor_reduce(T.dlim[:, 2:3], T.ef[:, 4, :], AX.X, ALU.max).then_inc(S.ef_step, 1)
        dve.wait_ge(S.ef_step, 4)
        V.tensor_tensor(T.dlim[:, 1:2], T.dlim[:, 2:3], T.dlim[:, 0:1], ALU.subtract).then_inc(S.ef_step, 1)
        V.scalar_tensor_tensor(T.ef[:, 4, :], T.ef[:, 1, :], float(WIN), T.ef[:, 0, :],
                               ALU.mult, ALU.add).then_inc(S.ef_step, 1)
        dve.wait_ge(S.ef_step, 6)
        dve.wait_ge(S.src_ready, 3)
        V.scalar_tensor_tensor(T.ef[:, 4, :], T.ef[:, 4, :], T.dlim[:, 0:1], T.ef[:, 3, :],
                               ALU.subtract, ALU.add).then_inc(S.ef_ready, 1)

    def edge_columns():
        n = 3 * TILES * GROUPS
        flat = T.eT[:, :, :, :].rearrange("p a t g -> p (a t g)")
        dve.wait_ge(S.eT_done, 1)
        V.tensor_copy(flat[:, 0:n], R.flat[:, 2048:2048 + n]).then_inc(S.eT_ready, 1)
        V.tensor_copy(flat[:, n:n + 2 * TILES * GROUPS], R.flat[:, 2560:2560 + 2 * TILES * GROUPS]).then_inc(S.eT_ready, 1)
        dve.wait_ge(S.base_done, 1)
        V.tensor_copy(T.bases[:, 0:GROUPS], R.flat[0:1, 3072:3072 + GROUPS]).then_inc(S.base_step, 1)
        V.tensor_reduce(T.spanmax[:, 0:1], R.flat[0:1, 3072 + GROUPS:3072 + 2 * GROUPS], AX.X, ALU.max).then_inc(S.base_step, 1)
        dve.wait_ge(S.base_step, 2)
        V.tensor_scalar(T.spanmax[:, 1:2], T.spanmax[:, 0:1], float(FIT_BELOW), None, ALU.is_lt).then_inc(S.base_step, 1)
        dve.wait_ge(S.base_step, 3)
        V.tensor_copy(T.fits[:, :], T.spanmax[:, 1:2]).then_inc(S.base_ready, 1)

    def counts(key, g0, base_of):
        def one_hot(g, b):
            dve.wait_ge(S.counts_done, g + g0 + 1)
            for j in range(TILES):
                ins = V.tensor_scalar(T.ko[:, b, j, :], T.iota[:, :], key[:, j, bass.ds(g, 1)], None, ALU.is_equal)
            ins.then_inc(S.ko_ready, 1)

        def add(g, b):
            base = base_of(g)
            dve.wait_ge(S.staged, g + g0 + RING + 1)
            dve.wait_ge(S.added, g + g0 + RING)
            at = T.A[:, :, :, bass.ds(base, WIN)]
            V.tensor_tensor(at, at, T.add[:, b, :].rearrange("p (c r d) -> p c r d", c=CH, r=TYPES),
                            ALU.add).then_inc(S.added, 1)

        lag = RING - 1
        for g in range(lag):
            one_hot(g, g)
        with dve.Fori(0, GROUPS // RING - 1) as i:
            for b in range(RING):
                one_hot(i * RING + b + lag, (b + lag) % RING)
                add(i * RING + b, b)
        one_hot(GROUPS - 1, RING - 1)
        for b in range(RING):
            add(GROUPS - RING + b, b)

    def window_keys(w):
        flat = T.eT[:, :, :, :].rearrange("p a t g -> p a (t g)")
        d, t, chunk = flat[:, 0, :], flat[:, 1, :], flat[:, 3, :]
        rel, low, high, key = (T.kgen[:, n, :] for n in range(4))
        dve.wait_ge(S.added, w * GROUPS + RING)
        dve.wait_ge(S.w16_step, w + 1)
        V.tensor_scalar(rel, d, T.w16[:, 0:1], None, ALU.subtract).then_inc(S.key_step, 1)
        dve.wait_ge(S.key_step, w * 7 + 1)
        V.tensor_scalar(low, rel, 0.0, float(OUTSIDE), ALU.is_lt, ALU.mult).then_inc(S.key_step, 1)
        V.tensor_scalar(high, rel, float(WIN), float(OUTSIDE), ALU.is_ge, ALU.mult).then_inc(S.key_step, 1)
        V.scalar_tensor_tensor(key, t, float(WIN), rel, ALU.mult, ALU.add).then_inc(S.key_step, 1)
        dve.wait_ge(S.key_step, w * 7 + 4)
        V.tensor_tensor(key, key, low, ALU.add).then_inc(S.key_step, 1)
        dve.wait_ge(S.key_step, w * 7 + 5)
        V.tensor_tensor(low, chunk, high, ALU.add).then_inc(S.key_step, 1)
        dve.wait_ge(S.key_step, w * 7 + 6)
        V.tensor_tensor(key, key, low, ALU.add).then_inc(S.key_step, 1)
        dve.wait_ge(S.key_step, w * 7 + 7)
        V.tensor_scalar(T.w16[:, :], T.w16[:, :], float(WIN), None, ALU.add).then_inc(S.w16_step, 1)

    def layer(n):
        j0 = 2 * TYPES * n
        with dve.Fori(0, TYPES) as r:
            for k in range(KD):
                dve.wait_ge(S.yh_ready, r * 2 + (j0 + k + 1))
                dve.wait_ge(S.out_done, r * 2 + (j0 + k + 1))
                V.tensor_tensor(T.yl[:, k, :].rearrange("p (h n) -> p h n", h=2), R.banks[:, 2 * k:2 * k + 2, 0:HALF],
                                T.yh[:, k, :].rearrange("p (h n) -> p h n", h=2).bitcast(F32),
                                ALU.subtract).then_inc(S.yl_ready, 1)
        dve.wait_ge(S.out_done, 2 + 2 * TYPES * (n + 1))
        to = T.xn if n == 0 else T.xr
        dve.wait_ge(S.b_in, 32)
        for c in range(CH):
            V.tensor_tensor(to[:, c, :], R.flat[:, 2048 + c * DIM:2048 + (c + 1) * DIM], T.b_bc[:, n, :],
                            ALU.add).then_inc(S.acc_read, 1)
        dve.wait_ge(S.acc_read, CH * (n + 1))
        if n == 0:
            V.sem_inc(S.layer_step, 1)
            V.tensor_scalar(T.xn[:, :, :], T.xn[:, :, :], 0.0, None, ALU.max).then_inc(S.layer_step, 1)
        else:
            V.tensor_tensor(T.X[:, :, :], T.X[:, :, :], T.xr[:, :, :], ALU.add).then_inc(S.layer_step, 1)
            dve.wait_ge(S.layer_step, 3)

    V.memset(T.A[:, 0:A_BY_DVE, :, :].rearrange("p c r n -> p (c r n)"), 0.0).then_inc(S.a_zero, 1)
    edges()
    dve.wait_ge(S.x_in, 32)
    ln(0)
    edge_columns()
    xT(0)
    split3(0)
    fits = dve.value_load(T.fits[0:1, 0:1], min_val=0, max_val=1)
    V.sem_inc(S.added, RING)
    dve.wait_ge(S.base_ready, 1)
    dve.wait_ge(S.const_ready, 4)
    dve.wait_ge(S.eT_ready, 2)
    dve.wait_ge(S.a_zero, 2)
    V.tensor_copy(T.src[:, :, :], T.eT[:, 2, :, :].rearrange("p t g -> p g t")).then_inc(S.src_ready, 1)
    dve.wait_ge(S.src_ready, 4)
    for g in range(0, GROUPS, BATCH):
        V.tensor_tensor(T.oh[:, g:g + BATCH, :, :],
                        T.iota[:, 0:P].unsqueeze(1).unsqueeze(1).to_broadcast([P, BATCH, TILES, P]),
                        T.src[:, g:g + BATCH, :].unsqueeze(3).to_broadcast([P, BATCH, TILES, P]),
                        ALU.is_equal).then_inc(S.oh_ready, BATCH)
    with dve.If(fits == 1):
        counts(T.eT[:, 4, :, :], 0,
               lambda g: dve.value_load(T.bases[0:1, bass.ds(g, 1)], min_val=0, max_val=NODES - 1))
        dve.wait_ge(S.added, GROUPS + RING)
    with dve.Else():
        V.memset(T.w16[:, :], 0.0).then_inc(S.w16_step, 1)
        with dve.Fori(0, WINDOWS) as w:
            window_keys(w)
            counts(T.kgen[:, 3, :].rearrange("p (t g) -> p t g", t=TILES), w * GROUPS, lambda g: w * WIN)
        dve.wait_ge(S.added, GROUPS * WINDOWS + RING)
    V.sem_inc(S.A_built, 1)
    dve.wait_ge(S.wh_ready, 1)
    V.tensor_tensor(T.wl0[:, :, :, :], T.raw[:, :, :, :], T.wh0[:, :, :, :].bitcast(F32),
                    ALU.subtract).then_inc(S.wl_ready, 1)
    V.sem_inc(S.yl_ready, 2)
    layer(0)
    xT(1)
    split3(1)
    layer(1)

    ln(1)
    xT(2)

    def low(e, piece, s):
        dve.wait_ge(S.ewh_ready, e * PIECES + piece + 1)
        w = slice(piece * PIECE, (piece + 1) * PIECE)
        V.tensor_tensor((T.ewl0, T.ewl1)[s][:, w], T.stg[:, s, w], (T.ewh0, T.ewh1)[s][:, w].bitcast(F32),
                        ALU.subtract).then_inc(S.ewl_ready, 1)

    for piece in range(PIECES):
        low(0, piece, 0)
    dve.wait_ge(S.gate_mm, 1)
    dve.wait_ge(S.gate_in, 32)
    dve.wait_ge(S.gate_const, 1)
    V.tensor_tensor(T.gate[:, :, :], R.flat[:, 2048:2048 + CH * EXPERTS].rearrange("p (c e) -> p c e", c=CH),
                    T.bg[:, :].unsqueeze(1).to_broadcast([P, CH, EXPERTS]), ALU.add).then_inc(S.gate_step, 1)
    dve.wait_ge(S.gate_step, 1)
    for c in range(CH):
        V.max(T.top[:, c, :], T.gate[:, c, :]).then_inc(S.gate_step, 1)
    dve.wait_ge(S.gate_step, CH + 1)
    V.tensor_tensor(T.gp[:, 0, :], T.top[:, :, 1], T.top[:, :, 0], ALU.subtract).then_inc(S.gate_step, 1)
    for c in range(CH):
        V.max_index(T.topi[:, c, :], T.top[:, c, :], T.gate[:, c, :]).then_inc(S.gate_step, 1)
    dve.wait_ge(S.gate_step, 2 * CH + 2)
    V.tensor_copy(T.topf[:, :, :], T.topi[:, :, :]).then_inc(S.gate_step, 1)
    dve.wait_ge(S.gate_exp, 1)
    V.tensor_scalar(T.gp[:, 2, :], T.gp[:, 1, :], 1.0, None, ALU.add).then_inc(S.gate_step, 1)
    dve.wait_ge(S.gate_step, 2 * CH + 4)
    V.reciprocal(T.gp[:, 3, :], T.gp[:, 2, :]).then_inc(S.gate_step, 1)
    dve.wait_ge(S.gate_step, 2 * CH + 5)
    V.tensor_tensor(T.gp[:, 4, :], T.gp[:, 1, :], T.gp[:, 3, :], ALU.mult).then_inc(S.gate_step, 1)
    dve.wait_ge(S.gate_step, 2 * CH + 6)
    for c in range(CH):
        for n, to in enumerate((T.comb, T.ctmp)):
            V.tensor_scalar(to[:, c, :], T.iota8[:, :], T.topf[:, c, n:n + 1], T.gp[:, 3 + n, c:c + 1],
                            ALU.is_equal, ALU.mult).then_inc(S.gate_step, 1)
    dve.wait_ge(S.gate_step, 4 * CH + 6)
    V.tensor_tensor(T.comb[:, :, :], T.comb[:, :, :], T.ctmp[:, :, :], ALU.add).then_inc(S.comb_ready, 1)
    dve.wait_ge(S.b2_done, 1)
    V.tensor_tensor(T.X[:, :, :].rearrange("p c d -> p (c d)"), T.X[:, :, :].rearrange("p c d -> p (c d)"),
                    R.flat[:, 2048:2048 + CH * DIM], ALU.add).then_inc(S.b2_added, 1)
    dve.wait_ge(S.b2_added, 1)
    dve.wait_ge(S.comb_ready, 1)
    V.sem_inc(S.yacc_added, CH)
    V.sem_inc(S.hl_ready, HRING)

    def take_sums(e):
        dve.wait_ge(S.h_used, e * HB + 2 * HB)
        for c in range(CH):
            V.scalar_tensor_tensor(T.X[:, c, :], R.flat[:, 2048 + c * DIM:2048 + (c + 1) * DIM],
                                   T.comb[:, c, bass.ds(e, 1)], T.X[:, c, :], ALU.mult, ALU.add).then_inc(S.yacc_added, 1)

    LAG = 2

    def experts(i, first=False, last=False):
        for s in range(2):
            e = i * 2 + s
            for hb in range(HB):
                j = e * HB + hb
                b = hb % HRING
                if hb == LAG and not (first and s == 0):
                    dve.wait_ge(S.yacc_added, e * CH)
                    take_sums(e - 1)
                dve.wait_ge(S.ht_ready, j + 3)
                dve.wait_ge(S.h_used, j + (HB - HRING + 1))
                V.tensor_copy(T.hh[:, b, :], T.ht[:, b, :]).then_inc(S.hh_ready, 1)
                dve.wait_ge(S.hh_ready, j + 1)
                V.tensor_tensor(T.hl[:, b, :], T.ht[:, b, :], T.hh[:, b, :].bitcast(F32),
                                ALU.subtract).then_inc(S.hl_ready, 1)
                if FIRST_PIECE <= hb < FIRST_PIECE + PIECES and not (last and s == 1):
                    low(e + 1, hb - FIRST_PIECE, 1 - s)

    experts(0, first=True)
    with dve.Fori(1, EXPERTS // 2 - 1) as i:
        experts(i)
    experts(EXPERTS // 2 - 1, last=True)
    dve.wait_ge(S.yacc_added, EXPERTS * CH)
    take_sums(EXPERTS - 1)
    dve.wait_ge(S.yacc_added, (EXPERTS + 1) * CH)
    V.sem_inc(S.experts_done, 1)

    ln(2)
    xT(3)
    dve.wait_ge(S.w3_in, 48)
    dve.wait_ge(S.w3_ready, 1)
    for k in range(KD):
        ins = V.tensor_scalar(T.asrc_bc[:, k, :], T.ident[:, :], 0.0, T.asrc[:, k:k + 1], ALU.mult, ALU.add)
    ins.then_inc(S.asrc_ready, 1)
    dve.wait_ge(S.hp_done, 1)
    for c in range(CH):
        ins = V.tensor_copy(T.hp[:, c, :, 0:HD1],
                            R.flat[:, 2048 + c * DIM:2048 + (c + 1) * DIM].rearrange("p (h d) -> p h d", h=HEADS1))
    ins.then_inc(S.hp_ready, 1)
    dve.wait_ge(S.hp_ready, 1)
    for c in range(CH):
        V.tensor_tensor(T.edm[:, c, :].rearrange("p (h d) -> p h d", h=HEADS1), T.hp[:, c, :, 0:HD1],
                        T.adst[:, :].rearrange("p (h d) -> p h d", h=HEADS1), ALU.mult).then_inc(S.ed_step, 1)
    dve.wait_ge(S.ed_step, CH)
    V.tensor_reduce(T.ed[:, :, :].rearrange("p c h -> p (c h)"),
                    T.edm[:, :, :].rearrange("p c (h d) -> p (c h) d", h=HEADS1), AX.X, ALU.add).then_inc(S.ed_step, 1)
    for c in range(CH):
        dve.wait_ge(S.ct_ready, c + 1)
        V.tensor_scalar(T.negm[:, c, :], T.CT[:, c, :], 0.0, NEG,
                        ALU.is_equal, ALU.mult).then_inc(S.negm_ready, 1)
    n = 0
    for h in range(HEADS1):
        dve.wait_ge(S.es_ready, h + 1)
        for c in range(CH):
            dve.wait_ge(S.negm_ready, c + 1)
            if n >= 2:
                dve.wait_ge(S.mes_step, n - 1)
            V.tensor_tensor_reduce(T.mtmp[:, n % 2, :], T.es[:, h, :], T.negm[:, c, :], 1.0, NEG, ALU.add, ALU.max,
                                   T.mes[:, c, h:h + 1]).then_inc(S.mes_step, 1)
            n += 1
    dve.wait_ge(S.mes_step, n)
    dve.wait_ge(S.ed_step, CH + 1)
    V.tensor_tensor(T.tm[:, :, :], T.mes[:, :, :], T.ed[:, :, :], ALU.add).then_inc(S.mes_step, 1)
    dve.wait_ge(S.mes_step, n + 1)
    V.scalar_tensor_tensor(T.nm[:, :, :], T.tm[:, :, :], 0.2, T.tm[:, :, :], ALU.mult, ALU.max).then_inc(S.mes_step, 1)
    dve.wait_ge(S.mes_step, n + 2)
    V.tensor_scalar(T.nm[:, :, :], T.nm[:, :, :], -1.0, None, ALU.mult).then_inc(S.m_ready, 1)

    def scores(j):
        h, c = divmod(j, CH)
        b = j % 2
        if j >= 2:
            dve.wait_ge(S.lk_ready, j - 1)
        V.tensor_scalar(T.t[:, b, :], T.es[:, h, :], T.mes[:, c, h:h + 1], T.ed[:, c, h:h + 1],
                        ALU.min, ALU.add).then_inc(S.t_ready, 1)
        dve.wait_ge(S.t_ready, j + 1)
        if j >= 2:
            dve.wait_ge(S.ex_ready, j - 1)
        V.scalar_tensor_tensor(T.lk[:, b, :], T.t[:, b, :], 0.2, T.t[:, b, :], ALU.mult, ALU.max).then_inc(S.lk_ready, 1)

    def weights(j):
        h, c = divmod(j, CH)
        dve.wait_ge(S.ex_ready, j + 1)
        if j >= 2:
            dve.wait_ge(S.pT_done, j - 1)
        V.tensor_tensor(T.pr[:, j % 2, :], T.ex[:, j % 2, :], T.CT[:, c, :], ALU.mult).then_inc(S.pr_ready, 1)

    def normalise(h):
        o = 2048 + 512 * (h % 2)
        sums = R.flat[:, o:o + CH * (HD1 + 1)].rearrange("p (c d) -> p c d", c=CH)
        dve.wait_ge(S.agg_done, CH * (h + 1))
        V.tensor_scalar(T.den[:, 0, :], sums[:, :, HD1], 1e-16, None, ALU.add).then_inc(S.o3_step, 1)
        dve.wait_ge(S.o3_step, 3 * h + 1)
        V.reciprocal(T.den[:, 1, :], T.den[:, 0, :]).then_inc(S.o3_step, 1)
        dve.wait_ge(S.o3_step, 3 * h + 2)
        V.tensor_tensor(T.o3[:, :, :], sums[:, :, 0:HD1], T.den[:, 1, :].unsqueeze(2).to_broadcast([P, CH, HD1]),
                        ALU.mult).then_inc(S.o3_step, 1)
        dve.wait_ge(S.o3_step, 3 * h + 3)
        V.tensor_tensor(T.X[:, :, h * HD1:(h + 1) * HD1], T.X[:, :, h * HD1:(h + 1) * HD1], T.o3[:, :, :],
                        ALU.add).then_inc(S.x3_ready, 1)

    dve.wait_ge(S.m_ready, 1)
    dve.wait_ge(S.ct_ready, CH)
    for j in range(HEADS1 * CH):
        scores(j)
        if j >= 1:
            weights(j - 1)
        if j >= 2 * CH and j % CH == 2:
            normalise(j // CH - 2)
    weights(HEADS1 * CH - 1)
    for h in range(2, HEADS1):
        normalise(h)
    dve.wait_ge(S.x3_ready, HEADS1)

    ln(3)
    xT(4)
    dve.wait_ge(S.w4_in, W4_LOADS)
    V.tensor_scalar(T.temp[:, 1, :], T.temp[:, 0, :], 0.1, 5.0, ALU.max, ALU.min).then_inc(S.temp_step, 1)
    dve.wait_ge(S.temp_step, 1)
    V.reciprocal(T.temp[:, 0, :], T.temp[:, 1, :]).then_inc(S.temp_step, 1)
    dve.wait_ge(S.temp_step, 2)
    for c in range(CH):
        dve.wait_ge(S.fx_done, c + 1)
        V.tensor_tensor(T.fx[:, c, :], R.banks[:, 4 + c % 2, :], T.bfx[:, :], ALU.add).then_inc(S.fx_ready, 1)

    def per_head(t):
        return t.rearrange("p (h g) -> p h g", h=HEADS2)

    def over_slices(t, rows=P):
        return t.unsqueeze(2).to_broadcast([rows, HEADS2, SLICES])

    for c in range(CH):
        lg = per_head(T.lg[:, c, :])
        hs = slice(c * HEADS2, (c + 1) * HEADS2)
        dve.wait_ge(S.lg_done, c + 1)
        V.tensor_tensor(lg, per_head(R.banks[:, 6 + c % 2, :]),
                        T.bsl[:, :].unsqueeze(1).to_broadcast([P, HEADS2, SLICES]), ALU.add).then_inc(S.lg_step, 1)
        dve.wait_ge(S.lg_step, 4 * c + 1)
        V.tensor_tensor(lg, lg, over_slices(T.temp[:, 0, :]), ALU.mult).then_inc(S.lg_step, 1)
        dve.wait_ge(S.lg_step, 4 * c + 2)
        V.tensor_reduce(T.sm[:, 0, hs], lg, AX.X, ALU.max).then_inc(S.lg_step, 1)
        dve.wait_ge(S.lg_step, 4 * c + 3)
        V.tensor_tensor(lg, lg, over_slices(T.sm[:, 0, hs]), ALU.subtract).then_inc(S.lg_step, 1)
    for c in range(CH):
        sw = per_head(T.sw[:, c, :])
        hs = slice(c * HEADS2, (c + 1) * HEADS2)
        dve.wait_ge(S.sm_exp, c + 1)
        V.tensor_reduce(T.sm[:, 1, hs], sw, AX.X, ALU.add).then_inc(S.tok_step, 1)
        dve.wait_ge(S.tok_step, 2 * c + 1)
        V.reciprocal(T.sm[:, 2, hs], T.sm[:, 1, hs]).then_inc(S.tok_step, 1)
        dve.wait_ge(S.tok_step, 2 * c + 2)
        V.tensor_tensor(sw, sw, over_slices(T.sm[:, 2, hs]), ALU.mult).then_inc(S.sw_ready, 1)
    n = 2 * CH
    dve.wait_ge(S.tok_done, 1)
    V.tensor_scalar(T.nrm[:, 0, :], R.flat[0:HD2, 512:1024], 1e-5, None, ALU.add).then_inc(S.tok_step, 1)
    dve.wait_ge(S.tok_step, n + 1)
    V.reciprocal(T.nrm[:, 1, :], T.nrm[:, 0, :]).then_inc(S.tok_step, 1)
    dve.wait_ge(S.tok_step, n + 2)
    V.tensor_tensor(T.tok[:, :], R.flat[0:HD2, 0:512], T.nrm[:, 1, :], ALU.mult).then_inc(S.tok_ready, 1)
    dve.wait_ge(S.al_done, 1)
    al = per_head(R.flat[0:SLICES, 2560:2560 + INNER])
    V.tensor_reduce(T.ats[:, 0, :], al, AX.X, ALU.max).then_inc(S.al_step, 1)
    dve.wait_ge(S.al_step, 1)
    V.tensor_tensor(per_head(T.at[:, 0, :]), al, over_slices(T.ats[:, 0, :], SLICES), ALU.subtract).then_inc(S.al_step, 1)
    dve.wait_ge(S.al_exp, 1)
    V.tensor_reduce(T.ats[:, 1, :], per_head(T.at[:, 1, :]), AX.X, ALU.add).then_inc(S.al_step, 1)
    dve.wait_ge(S.al_step, 3)
    V.reciprocal(T.ats[:, 2, :], T.ats[:, 1, :]).then_inc(S.al_step, 1)
    dve.wait_ge(S.al_step, 4)
    V.tensor_tensor(per_head(T.at[:, 2, :]), per_head(T.at[:, 1, :]), over_slices(T.ats[:, 2, :], SLICES),
                    ALU.mult).then_inc(S.at_ready, 1)
    for c in range(CH):
        V.tensor_tensor(T.X[:, c, :], T.X[:, c, :], T.bout[:, :], ALU.add).then_inc(S.o3_step, 1)
    dve.wait_ge(S.o3_step, 3 * HEADS1 + CH)
    for c in range(CH):
        dve.wait_ge(S.out4_done, c + 1)
        V.tensor_tensor(T.X[:, c, :], T.X[:, c, :], R.banks[:, 2 + c, 0:DIM],
                        ALU.add).then_inc(S.y_ready, 1)


FIT_BELOW = WIN


NAMES = ["x", "src", "dst", "edge_type_8", "L0_gnn_W1", "L0_gnn_self_w1", "L0_gnn_b1", "L0_gnn_W2", "L0_gnn_self_w2",
         "L0_gnn_b2", "L0_ffn_bg", "L0_ffn_b2", "L1_gnn_W", "L1_ffn_W_fx", "L1_ffn_b_fx", "L1_ffn_W_x",
         "L1_ffn_W_slice", "L1_ffn_b_slice", "L1_ffn_W_q", "L1_ffn_W_k", "L1_ffn_W_v", "L1_ffn_W_out", "L1_ffn_b_out"]


def laid_out(inputs):
    import numpy as np

    a = {n: np.asarray(inputs[n]) for n in NAMES}
    a["wgT"] = np.asarray(inputs["L0_ffn_Wg"]).T
    a["w1T"] = np.asarray(inputs["L0_ffn_W1"]).transpose(0, 2, 1)
    a["w2T"] = np.asarray(inputs["L0_ffn_W2"]).transpose(0, 2, 1)
    a["b1T"] = np.asarray(inputs["L0_ffn_b1"]).reshape(EXPERTS * HB, P).T
    a["asrcT"] = np.asarray(inputs["L1_gnn_a_src"]).reshape(KD, P).T
    a["adst"] = np.asarray(inputs["L1_gnn_a_dst"]).reshape(-1)
    a["bxT"] = np.asarray(inputs["L1_ffn_b_x"]).reshape(IB, P).T
    a["temp"] = np.asarray(inputs["L1_ffn_temperature"]).reshape(-1)
    return {n: np.ascontiguousarray(v) for n, v in a.items()}


def kernel(**inputs):
    import concourse.bacc as bacc
    from concourse.bass_utils import run_bass_kernel_spmd

    arrays = laid_out(inputs)
    nc = bacc.Bacc("TRN2", target_bir_lowering=False, num_devices=1)
    D = namedtuple("Inputs", arrays)(*[
        nc.dram_tensor(f"in_{n}", v.shape, mybir.dt.from_np(v.dtype), kind="ExternalInput").ap()
        for n, v in arrays.items()])
    out = nc.dram_tensor("out_0", (NODES, DIM), F32, kind="ExternalOutput").ap()
    program(nc, D, out)
    r = run_bass_kernel_spmd(nc, [{f"in_{n}": v for n, v in arrays.items()}], core_ids=[0])
    return r.results[0]["out_0"]
```

```python
from collections import namedtuple
from contextlib import ExitStack

import concourse.bass as bass
from concourse import mybir

P = 128
F32 = mybir.dt.float32
F32R = mybir.dt.float32r
F16 = mybir.dt.float16
I16 = mybir.dt.int16
I32 = mybir.dt.int32
U32 = mybir.dt.uint32
ALU = mybir.AluOpType
ACT = mybir.ActivationFunctionType
AX = mybir.AxisListType

NODES, DIM, EDGES, TYPES = 625, 256, 20625, 8
CH = -(-NODES // P)
NP = CH * P
LAST = NODES - (CH - 1) * P
KD = DIM // P
HALF = NP // 2

TILES = 3
GE = TILES * P
GROUPS = -(-EDGES // GE)
FULL_ROWS = EDGES // GE
REST = EDGES - FULL_ROWS * GE
RING = 3
UNROLLED = 2 * RING
ACT_TILES = 2
WIN = 16
KEYS = TYPES * WIN
WINDOWS = NP // WIN
OUTSIDE = 5000

UNITS = ((0, 3), (3, CH))

EXPERTS, HID = 8, 1024
HB = HID // P
HRING = 4
PIECES = 4
FIRST_PIECE = HB - PIECES - 1
PIECE = (2 * HID + HB * DIM) // PIECES
HEADS1, HD1 = 4, 64
EX_RING, EM_RING = 3, 3
TURN_LAG = 3
WARM = dict(relu=8, relu_split=8, second_norm=20, third_norm=18, last_norm=24,
            token_norm=6, token_copy=6, query_copy=5, attention_copy=6, projection_copy=5)
GATHER_LAG = 1
SUMS_LAG = 3
TOK_LAG = 2
HEADS2, HD2, SLICES = 8, 64, 64
INNER = HEADS2 * HD2
IB = INNER // P
LN_EPS = 1e-5
NEG = -1e30


class Place:
    pass


def layout(nc):
    at = Place()
    at.pos = -(-nc.sbuf_base // 64) * 64
    size = {F32: 4, F32R: 4, F16: 2, I16: 2, I32: 4, U32: 4}

    def put(name, shape, dt):
        n = size[dt]
        for s in shape[1:]:
            n *= s
        t = nc.alloc_sbuf_tensor_at(name, shape, dt, offset=at.pos)
        at.pos += -(-n // 64) * 64
        return t

    T = Place()
    T.X = put("X", [P, CH, DIM], F32)
    xn_pos = at.pos
    T.xn = put("xn", [P, CH, DIM], F32)
    after_xn = at.pos
    T.xTh = put("xTh", [P, KD, NP], F32R)
    T.xTl = put("xTl", [P, KD, NP], F32R)
    T.stats = put("stats", [P, CH, 6], F32)
    T.mv = put("mv", [P, CH, 2], F32)
    T.std = put("std", [P, CH], F32)
    T.rstd = put("rstd", [P, CH], F32)
    T.eps = put("eps", [P, 1], F32)
    T.early = put("early", [P, 1], F32)
    T.ident = put("ident", [P, P], F32)
    shared = at.pos

    T.A = put("A", [P, CH, TYPES, NP], I16)
    T.wh0 = put("wh0", [P, TYPES + 1, KD, DIM], F32R)
    T.wl0 = put("wl0", [P, TYPES + 1, KD, DIM], F32R)
    after_w0 = at.pos
    T.wh1 = put("wh1", [P, TYPES + 1, KD, DIM], F32R)
    T.wl1 = put("wl1", [P, TYPES + 1, KD, DIM], F32R)
    T.raw = put("raw", [P, TYPES + 1, KD, DIM], F32)
    T.xh = put("xh", [P, CH, DIM], F32R)
    T.xl = put("xl", [P, CH, DIM], F32R)
    T.b_bc = put("b_bc", [P, 2, DIM], F32)
    over = at.pos
    T.ei = put("ei", [GROUPS, 4, GE], I32)
    T.ef = put("ef", [GROUPS, 5, GE], F32)
    behind = at.pos
    at.pos = over
    T.ko = put("ko", [P, RING, TILES, CH * KEYS], F16)
    T.oh = put("oh", [P, RING, TILES, P], F16)
    T.off = put("off", [P, 2, ACT_TILES, P], F16)
    at.pos = max(at.pos, behind)
    T.dlim = put("dlim", [GROUPS, 4], F32)
    T.eT = put("eT", [P, 5, TILES, GROUPS], F32)
    T.iota = put("iota", [P, CH * KEYS], F16)
    T.add = put("add", [P, RING, CH * KEYS], I16)
    T.kgen = put("kgen", [P, 4, TILES * GROUPS], F32)
    T.w16 = put("w16", [P, 1], F32)
    T.spanmax = put("spanmax", [1, 2], F32)
    T.bases = put("bases", [1, 64], I32)
    T.fits = put("fits", [1, 1], I32)
    end1 = at.pos
    at.pos = over
    T.yh = put("yh", [P, KD, NP], F32R)
    T.yl = put("yl", [P, KD, NP], F32R)
    first, second = ((c1 - c0) * P for c0, c1 in UNITS)
    T.Ar = [put("Ar0", [P, CH, first], F32R)]
    at.pos = max(at.pos, over + CH * NP * 4)
    c_pos = at.pos
    T.C = put("C", [P, CH, NP], F32)
    end1 = max(end1, at.pos)
    assert end1 <= nc.sbuf_usable_end, end1
    at.pos = xn_pos
    T.Ar.append(put("Ar1", [P, CH, second], F32R))
    assert at.pos <= after_xn
    at.pos = over
    T.CT = put("CT", [P, CH, NP], F32)
    assert at.pos <= c_pos
    at.pos = c_pos
    T.negm = put("negm", [P, CH, NP], F32)

    at.pos = shared
    T.ewh0 = put("ewh0", [P, 2 * HID + HB * DIM], F32R)
    assert at.pos <= after_w0
    at.pos = shared + 2 * CH * TYPES * NP
    T.stg = put("stg", [P, 2, 2 * HID + HB * DIM], F32)
    assert at.pos <= after_w0
    T.ewl0 = put("ewl0", [P, 2 * HID + HB * DIM], F32R)
    T.ewh1 = put("ewh1", [P, 2 * HID + HB * DIM], F32R)
    T.ewl1 = put("ewl1", [P, 2 * HID + HB * DIM], F32R)
    assert at.pos <= over
    at.pos = shared + 16384
    T.ht = put("ht", [P, HRING, NP], F32)
    T.hh = put("hh", [P, HRING, NP], F32R)
    T.hl = put("hl", [P, HRING, NP], F32R)
    T.b1 = put("b1", [P, EXPERTS * HB], F32)
    T.b2 = put("b2", [EXPERTS, DIM], F32)
    assert at.pos <= shared + 2 * CH * TYPES * NP
    at.pos = c_pos + CH * NP * 4
    T.wgh = put("wgh", [P, KD, EXPERTS], F32R)
    T.wgl = put("wgl", [P, KD, EXPERTS], F32R)
    T.wg = put("wg", [P, 1, KD, EXPERTS], F32)
    T.bg = put("bg", [P, EXPERTS], F32)
    T.gate = put("gate", [P, CH, EXPERTS], F32)
    T.top = put("top", [P, CH, 8], F32)
    T.topi = put("topi", [P, CH, 8], U32)
    T.topf = put("topf", [P, CH, 8], F32)
    T.gp = put("gp", [P, 5, CH], F32)
    T.ctmp = put("ctmp", [P, CH, EXPERTS], F32)
    T.comb = put("comb", [P, CH, EXPERTS], F32)
    T.iota8 = put("iota8", [P, EXPERTS], F32)
    T.combT = put("combT", [EXPERTS, NP], F32)
    assert at.pos <= nc.sbuf_usable_end, at.pos

    at.pos = shared
    T.w3 = put("w3", [P, KD, DIM], F32)
    T.w3h = put("w3h", [P, KD, DIM], F32R)
    T.w3l = put("w3l", [P, KD, DIM], F32R)
    T.hp = put("hp", [P, CH, HEADS1, HD1 + 1], F32)
    T.hpT = put("hpT", [P, KD, NP], F32)
    T.asrc = put("asrc", [P, KD], F32)
    T.asrc_bc = put("asrc_bc", [P, KD, P], F32)
    T.adst = put("adst", [P, KD], F32)
    T.adst_bd = put("adst_bd", [P, KD, HEADS1], F32)
    T.ed = put("ed", [P, CH, HEADS1], F32)
    T.es = put("es", [P, HEADS1, NP], F32)
    T.mt = put("mt", [P, 2 * CH, NP], F32)
    T.mes = put("mes", [P, CH, HEADS1], F32)
    T.tm = put("tm", [P, CH, HEADS1], F32)
    T.nm = put("nm", [P, CH, HEADS1], F32)
    T.ed2 = put("ed2", [P, 2, CH, HEADS1], F32)
    T.ex = put("ex", [P, EX_RING, 2, NP], F32)
    T.em = put("em", [P, EM_RING, NP], F32)
    T.pr = put("pr", [P, EM_RING, NP], F32)
    T.pT = put("pT", [P, 2, CH, NP], F32)
    T.oT = put("oT", [HD1 + 1, NP], F32)
    T.den = put("den", [P, 2, CH], F32)
    T.o3 = put("o3", [P, CH, HD1], F32)
    assert at.pos <= over, (at.pos, over)

    T.wfx = put("wfx", [P, KD, INNER], F32)
    T.wfxh = put("wfxh", [P, KD, INNER], F32R)
    T.wfxl = put("wfxl", [P, KD, INNER], F32R)
    T.wx = put("wx", [P, KD, INNER], F32)
    T.wxh = put("wxh", [P, KD, INNER], F32R)
    T.wxl = put("wxl", [P, KD, INNER], F32R)
    T.wo = put("wo", [HD2, HEADS2, DIM], F32)
    T.wsl = put("wsl", [P, P], F32)
    T.wqkv = put("wqkv", [HD2, 3, HD2], F32)
    T.bfx = put("bfx", [P, INNER], F32)
    T.bx = put("bx", [P, IB], F32)
    T.bsl = put("bsl", [P, SLICES], F32)
    T.bout = put("bout", [P, DIM], F32)
    T.bst = put("bst", [P, INNER], F32)
    T.temp = put("temp", [P, 2, HEADS2], F32)
    T.tcol = put("tcol", [P, 3, IB], F32)
    T.bxt = put("bxt", [P, IB], F32)
    assert at.pos <= over, (at.pos, over)
    at.pos = shared
    T.fx = put("fx", [P, CH, HEADS2, HD2 + 1], F32)
    T.xm = put("xm", [P, IB, NP], F32)
    T.lg = put("lg", [P, CH, INNER], F32)
    T.sm = put("sm", [P, 4, CH * HEADS2], F32)
    T.sw = put("sw", [P, CH, INNER], F32)
    T.swT = put("swT", [P, IB, NP], F32)
    T.nrm = put("nrm", [SLICES, 2, HEADS2], F32)
    T.tokT = put("tokT", [SLICES, INNER], F32)
    T.tok = put("tok", [HD2, INNER], F32)
    T.qk = put("qk", [HD2, 2, INNER], F32)
    T.vT = put("vT", [HD2, INNER], F32)
    T.vo = put("vo", [SLICES, HEADS2, DIM], F32)
    T.at = put("at", [SLICES, 3, INNER], F32)
    T.ats = put("ats", [SLICES, 3, HEADS2], F32)
    T.atT = put("atT", [SLICES, INNER], F32)
    T.M = put("M", [P, IB, DIM], F32)
    T.bounds = (at.pos,)
    return T


SEMAPHORES = """
x_zero x_in ei_set e_in b_in raw_in wh_ready wl_ready const_ready a_zero
early ln_stats ln_aggr ln_std ln_rstd ln_out
tr_done xTh_ready xTl_ready
ef_ready ef_step eT_done eT_ready base_done base_step base_ready
src_ready off_ready oh_ready ko_ready counts_done staged added key_step w16_step A_built
xh_ready xl_ready a_ready y_done yh_ready yl_ready out_done acc_read layer_step relu_ready c_zero c_step C_built
stg0_in stg1_in ewh_ready ewl_ready experts_done
gate_in gate_const wg_step wg_ready gate_mm gate_step gate_exp comb_ready combT_done combT_ready b2_done b2_added eb_in
h_done ht_ready hh_ready hl_ready h_used yacc_done yacc_added
w3_in w3_ready asrc_ready hp_done hp_ready adst_ready ed_done hpT_done hpT_ready es_done es_ready ed_ready
ct_done ct_ready negm_ready mt_ready bound_step bounds_ready ex_ready em_ready pr_ready pT_done pT_ready agg_done oT_ready turned_done
o3_step x3_ready
w4_in wfx_ready wx_ready w4_const fx_done fx_ready fx_ones xm_done xm_ready temp_step temp_ready lg_done lg_step sm_exp sm_ready sw_ready
swT_done swT_ready tok_done tok_step tokT_ready tok_turned tok_ready qkv_done qkv_ready al_done al_step al_exp at_ready
atT_done atT_ready vo_done vo_ready M_done M_ready out4_done y_ready stored
""".split()


def program(nc, D, out):
    T = layout(nc)
    with ExitStack() as ctx:
        S = namedtuple("Semaphores", SEMAPHORES)(*[ctx.enter_context(nc.semaphore(n)) for n in SEMAPHORES])
        PS = ctx.enter_context(nc.psum_tensor("PS", [P, 8, 512], F32))
        block = ctx.enter_context(nc.Block())
        R = Place()
        R.banks = PS
        R.flat = PS[:, :, :].rearrange("p b n -> p (b n)")

        @block.sync
        def _(sp):
            load_everything(sp, nc, S, T, D, out)

        @block.gpsimd
        def _(pool):
            pool_program(pool, nc, S, T)

        @block.scalar
        def _(act):
            act_program(act, nc, S, T, R)

        @block.tensor
        def _(pe):
            pe_program(pe, nc, S, T, R)

        @block.vector
        def _(dve):
            dve_program(dve, nc, S, T, R)


def chunks(t, c):
    return P if c < CH - 1 else LAST


def load_everything(sp, nc, S, T, D, out):
    full = (CH - 1) * P
    sp.wait_ge(S.ei_set, 1)
    for n, e in enumerate((D.dst, D.edge_type_8, D.src)):
        sp.dma_start(T.ei[0:FULL_ROWS, n, :], e[0:FULL_ROWS * GE].rearrange("(g e) -> g e", e=GE)).then_inc(S.e_in, 16)
        sp.dma_start(T.ei[FULL_ROWS:FULL_ROWS + 1, n, 0:REST],
                     e[FULL_ROWS * GE:EDGES].rearrange("(g e) -> g e", g=1)).then_inc(S.e_in, 16)
    sp.wait_ge(S.x_zero, 1)
    sp.dma_start(T.X[:, 0:CH - 1, :], D.x[0:full, :].rearrange("(c p) d -> p c d", p=P)).then_inc(S.x_in, 16)
    sp.dma_start(T.X[0:LAST, CH - 1, :], D.x[full:NODES, :]).then_inc(S.x_in, 16)
    for n, (w, self_w, b) in enumerate(((D.L0_gnn_W1, D.L0_gnn_self_w1, D.L0_gnn_b1),
                                        (D.L0_gnn_W2, D.L0_gnn_self_w2, D.L0_gnn_b2))):
        if n:
            sp.wait_ge(S.wl_ready, 1)
        for k in range(KD):
            sp.dma_start(T.raw[:, 0:TYPES, k, :],
                         w[:, k * P:(k + 1) * P, :].rearrange("r p o -> p r o")).then_inc(S.raw_in, 16)
        sp.dma_start(T.raw[:, TYPES, :, :], self_w.rearrange("(k p) o -> p k o", p=P)).then_inc(S.raw_in, 16)
        sp.dma_start(T.b_bc[:, n, :], b.partition_broadcast(P)).then_inc(S.b_in, 16)
    sp.wait_ge(S.A_built, 1)
    sp.dma_start(T.wg[:, 0, :, :], D.wgT.rearrange("(k p) e -> p k e", p=P)).then_inc(S.gate_in, 16)
    sp.dma_start(T.bg[:, :], D.L0_ffn_bg.partition_broadcast(P)).then_inc(S.gate_in, 16)

    def expert(e):
        s = e % 2
        arrived = (S.stg0_in, S.stg1_in)[s]
        sp.dma_start(T.stg[:, s, 0:2 * HID].rearrange("p (k h) -> p k h", k=KD),
                     D.w1T[e].rearrange("(k p) h -> p k h", p=P)).then_inc(arrived, 16)
        sp.dma_start(T.stg[:, s, 2 * HID:].rearrange("p (b o) -> p b o", b=HB),
                     D.w2T[e].rearrange("(b p) o -> p b o", p=P)).then_inc(arrived, 16)

    sp.wait_ge(S.out_done, 2 + 2 * TYPES)
    expert(0)
    expert(1)
    sp.wait_ge(S.y_done, 2 + 4 * TYPES)
    sp.wait_ge(S.C_built, 1)
    sp.dma_start(T.b1[:, :], D.b1T).then_inc(S.eb_in, 16)
    sp.dma_start(T.b2[:, :], D.L0_ffn_b2).then_inc(S.eb_in, 16)
    for e in range(2, EXPERTS):
        sp.wait_ge(S.ewl_ready, (e - 1) * PIECES)
        expert(e)
    sp.wait_ge(S.experts_done, 1)
    sp.dma_start(T.w3[:, :, :], D.L1_gnn_W.rearrange("(k p) o -> p k o", p=P)).then_inc(S.w3_in, 16)
    sp.dma_start(T.adst[:, :], D.adstT).then_inc(S.w3_in, 16)
    sp.dma_start(T.asrc[:, :], D.asrcT).then_inc(S.w3_in, 16)
    sp.dma_start(T.wfx[:, :, :], D.L1_ffn_W_fx.rearrange("(k p) o -> p k o", p=P)).then_inc(S.w4_in, 16)
    sp.dma_start(T.wx[:, :, :], D.L1_ffn_W_x.rearrange("(k p) o -> p k o", p=P)).then_inc(S.w4_in, 16)
    sp.dma_start(T.wo[:, :, :], D.L1_ffn_W_out.rearrange("(h c) o -> c h o", c=HD2)).then_inc(S.w4_in, 16)
    for n, w in enumerate((D.L1_ffn_W_q, D.L1_ffn_W_k, D.L1_ffn_W_v)):
        sp.dma_start(T.wqkv[:, n, :], w).then_inc(S.w4_in, 16)
    sp.dma_start(T.bfx[:, :], D.L1_ffn_b_fx.partition_broadcast(P)).then_inc(S.w4_in, 16)
    sp.dma_start(T.bx[:, :], D.bxT).then_inc(S.w4_in, 16)
    sp.dma_start(T.bsl[:, :], D.L1_ffn_b_slice.partition_broadcast(P)).then_inc(S.w4_in, 16)
    sp.dma_start(T.bout[:, :], D.L1_ffn_b_out.partition_broadcast(P)).then_inc(S.w4_in, 16)
    sp.dma_start(T.temp[:, 0, :], D.temp.partition_broadcast(P)).then_inc(S.w4_in, 16)
    sp.dma_start(T.tcol[:, 0, :], D.tcolT).then_inc(S.w4_in, 16)
    sp.wait_ge(S.w4_const, 1)
    for n in range(2):
        sp.dma_start(T.wsl[n * HD2:(n + 1) * HD2, n * HD2:(n + 1) * HD2], D.L1_ffn_W_slice).then_inc(S.w4_in, 16)
    sp.wait_ge(S.y_ready, CH - 1)
    sp.dma_start(out[0:full, :].rearrange("(c p) d -> p c d", p=P), T.X[:, 0:CH - 1, :]).then_inc(S.stored, 16)
    sp.wait_ge(S.y_ready, CH)
    sp.dma_start(out[full:NODES, :], T.X[0:LAST, CH - 1, :]).then_inc(S.stored, 16)
    sp.wait_ge(S.stored, 32)


W4_LOADS = 16 * 14
A_BY_DVE = 2


def pool_program(pool, nc, S, T):
    nc.gpsimd.memset(T.ei[:, 1:3, :], 0)
    nc.gpsimd.memset(T.ei[:, 0, :], OUTSIDE).then_inc(S.ei_set, 1)
    nc.gpsimd.memset(T.X[:, CH - 1, :], 0.0).then_inc(S.x_zero, 1)
    nc.gpsimd.memset(T.eps[:, :], LN_EPS).then_inc(S.const_ready, 1)
    nc.gpsimd.memset(T.ident[:, :], 0.0).then_inc(S.const_ready, 1)
    nc.gpsimd.iota(T.iota[:, :], pattern=[[1, CH * KEYS]], base=0, channel_multiplier=0,
                   allow_small_or_imprecise_dtypes=True).then_inc(S.const_ready, 1)
    pool.wait_ge(S.const_ready, 3)
    nc.gpsimd.affine_select(out=T.ident[:, :], in_=T.ident[:, :], compare_op=ALU.not_equal, fill=1.0,
                            base=0, pattern=[[-1, P]], channel_multiplier=1).then_inc(S.const_ready, 1)
    nc.gpsimd.memset(T.A[:, A_BY_DVE:CH, :, :].rearrange("p c r n -> p (c r n)").bitcast(F32), 0.0).then_inc(S.a_zero, 1)

    pool.wait_ge(S.ln_out, CH)
    nc.gpsimd.tensor_copy(T.xh[:, :, :], T.xn[:, :, :]).then_inc(S.xh_ready, 1)
    pool.wait_ge(S.xh_ready, 1)
    nc.gpsimd.tensor_tensor(T.xl[:, :, :], T.xn[:, :, :], T.xh[:, :, :].bitcast(F32), ALU.subtract).then_inc(S.xl_ready, 1)
    pool.wait_ge(S.raw_in, 48)
    nc.gpsimd.tensor_copy(T.wh0[:, :, :, :], T.raw[:, :, :, :]).then_inc(S.wh_ready, 1)
    pool.wait_ge(S.wh_ready, 1)
    nc.gpsimd.tensor_tensor(T.wl0[:, :, :, :], T.raw[:, :, :, :], T.wh0[:, :, :, :].bitcast(F32),
                            ALU.subtract).then_inc(S.wl_ready, 1)
    pool.wait_ge(S.raw_in, 96)
    nc.gpsimd.tensor_copy(T.wh1[:, :, :, :], T.raw[:, :, :, :]).then_inc(S.wh_ready, 1)
    pool.wait_ge(S.wh_ready, 2)
    nc.gpsimd.tensor_tensor(T.wl1[:, :, :, :], T.raw[:, :, :, :], T.wh1[:, :, :, :].bitcast(F32),
                            ALU.subtract).then_inc(S.wl_ready, 1)
    pool.wait_ge(S.gate_in, 32)
    nc.gpsimd.tensor_copy(T.wgh[:, :, :], T.wg[:, 0, :, :]).then_inc(S.wg_step, 1)
    pool.wait_ge(S.wg_step, 1)
    nc.gpsimd.tensor_tensor(T.wgl[:, :, :], T.wg[:, 0, :, :], T.wgh[:, :, :].bitcast(F32), ALU.subtract).then_inc(S.wg_ready, 1)
    pool.wait_ge(S.A_built, 1)
    nc.gpsimd.iota(T.iota8[:, :], pattern=[[1, EXPERTS]], base=0, channel_multiplier=0,
                   allow_small_or_imprecise_dtypes=True).then_inc(S.gate_const, 1)
    nc.gpsimd.memset(T.C[:, :, :], 0.0).then_inc(S.c_zero, 1)
    nc.gpsimd.sem_inc(S.c_step, 2)
    pool.wait_ge(S.c_zero, 1)
    with pool.Fori(0, TYPES) as r:
        for u, (c0, c1) in enumerate(UNITS):
            pool.wait_ge(S.a_ready, r * 2 + (2 * TYPES + u + 1))
            pool.wait_ge(S.c_step, r * 2 + (u + 1))
            unit = T.C[:, :, c0 * P:c1 * P]
            nc.gpsimd.tensor_tensor(unit, unit, T.Ar[u][:, :, :].bitcast(F32), ALU.add).then_inc(S.c_step, 1)
    pool.wait_ge(S.c_step, 2 + 2 * TYPES)
    nc.gpsimd.engine_nop().then_inc(S.C_built, 1)
    pool.wait_ge(S.experts_done, 1)
    nc.gpsimd.memset(T.hp[:, :, :, HD1:HD1 + 1], 1.0).then_inc(S.w3_ready, 1)
    nc.gpsimd.memset(T.adst_bd[:, :, :], 0.0).then_inc(S.adst_ready, 1)
    nc.gpsimd.memset(T.wsl[:, :], 0.0).then_inc(S.w4_const, 1)
    pool.wait_ge(S.w3_in, 48)
    nc.gpsimd.tensor_copy(T.w3h[:, :, :], T.w3[:, :, :]).then_inc(S.w3_ready, 1)
    pool.wait_ge(S.w3_ready, 2)
    nc.gpsimd.tensor_tensor(T.w3l[:, :, :], T.w3[:, :, :], T.w3h[:, :, :].bitcast(F32),
                            ALU.subtract).then_inc(S.w3_ready, 1)
    for j in range(HEADS1 * CH):
        pool.wait_ge(S.em_ready, j + 1)
        if j >= EM_RING:
            pool.wait_ge(S.pT_done, j - EM_RING + 1)
        if j == 0:
            pool.wait_ge(S.ct_ready, CH)
        nc.gpsimd.tensor_tensor(T.pr[:, j % EM_RING, :], T.em[:, j % EM_RING, :], T.CT[:, j % CH, :], ALU.mult).then_inc(S.pr_ready, 1)
    pool.wait_ge(S.w4_in, W4_LOADS)
    for raw, hi, lo, ready in ((T.wx, T.wxh, T.wxl, S.wx_ready), (T.wfx, T.wfxh, T.wfxl, S.wfx_ready)):
        nc.gpsimd.tensor_copy(hi[:, :, :], raw[:, :, :]).then_inc(ready, 1)
        pool.wait_ge(ready, 1)
        nc.gpsimd.tensor_tensor(lo[:, :, :], raw[:, :, :], hi[:, :, :].bitcast(F32),
                                ALU.subtract).then_inc(ready, 1)
    pool.wait_ge(S.x3_ready, HEADS1)
    nc.gpsimd.memset(T.fx[:, :, :, HD2:HD2 + 1], 1.0).then_inc(S.fx_ones, 1)
    for c in range(CH):
        pool.wait_ge(S.sm_ready, 2 * c + 2)
        sw = T.sw[:, c, :].rearrange("p (h g) -> p h g", h=HEADS2)
        nc.gpsimd.tensor_tensor(sw, sw, T.sm[:, 2, c * HEADS2:(c + 1) * HEADS2].unsqueeze(2)
                                .to_broadcast([P, HEADS2, SLICES]), ALU.mult).then_inc(S.sw_ready, 1)


def act_program(act, nc, S, T, R):
    A = nc.scalar

    def ln(n):
        if n == 0:
            act.wait_ge(S.const_ready, 1)
        else:
            act.wait_ge(S.ln_std, n)
        A.activation(T.early[:, :], T.eps[:, :], ACT.Sqrt).then_inc(S.early, 1)
        act.wait_ge(S.ln_aggr, CH * (n + 1))
        A.activation(T.std[:, :], T.mv[:, :, 1], ACT.Sqrt, bias=T.eps[:, 0:1]).then_inc(S.ln_std, 1)

    def xT(n):
        for c in range(CH):
            act.wait_ge(S.tr_done, CH * n + c + 1)
            A.activation(T.xTh[:, :, c * P:(c + 1) * P], R.banks[:, c, 0:DIM].rearrange("p (k n) -> p k n", k=KD),
                         ACT.Copy).then_inc(S.xTh_ready, 1)

    def split():
        act.wait_ge(S.relu_ready, CH)
        A.activation(T.xh[:, :, :], T.xn[:, :, :], ACT.Copy).then_inc(S.xh_ready, 1)

    def count(g0):
        def offsets(g, b):
            act.wait_ge(S.oh_ready, g + (g0 + 1))
            for j in range(ACT_TILES):
                ins = A.activation(T.off[:, b % 2, j, :], T.iota[:, 0:P], ACT.Abs, bias=T.eT[:, 2, j, bass.ds(g, 1)], scale=-1.0)
            ins.then_inc(S.off_ready, 1)

        def sources(g, b):
            act.wait_ge(S.off_ready, g + (g0 + 1))
            act.wait_ge(S.counts_done, g + (g0 + 1))
            A.activation(T.oh[:, b % RING, 0:ACT_TILES, :], T.off[:, b % 2, :, :], ACT.Relu, bias=1.0, scale=-1.0).then_inc(S.oh_ready, 1)

        def stage(g, b):
            act.wait_ge(S.counts_done, g + (g0 + RING + 1))
            act.wait_ge(S.added, g + (g0 + 1))
            A.activation(T.add[:, b, :], R.flat[:, 1024 * b:1024 * b + CH * KEYS], ACT.Copy).then_inc(S.staged, 1)

        def both(g, b):
            offsets(g + lag, b + lag)
            stage(g, b % RING)
            sources(g + lag, b + lag)

        lag = RING - 1
        for g in range(lag):
            offsets(g, g)
            sources(g, g)
        with act.Fori(0, GROUPS // UNROLLED - 1) as i:
            for b in range(UNROLLED):
                both(i * UNROLLED + b, b)
        for b in range(UNROLLED - lag):
            both(GROUPS - UNROLLED + b, b)
        for g in range(GROUPS - lag, GROUPS):
            stage(g, g % RING)

    def layer(n):
        j0 = 2 * TYPES * n

        def counts_for_pe(r, u, j):
            act.wait_ge(S.y_done, j + 1)
            if n:
                act.wait_ge(S.c_step, j - (j0 - 1))
            c0, c1 = UNITS[u]
            A.activation(T.Ar[u][:, :, :], (T.A[:, :, r, c0 * P:c1 * P] if type(r) is int else
                                            T.A[:, :, bass.ds(r, 1), c0 * P:c1 * P].rearrange("p c a n -> p c (a n)")),
                         ACT.Copy).then_inc(S.a_ready, 1)

        def high(u, j):
            act.wait_ge(S.y_done, j + 3)
            act.wait_ge(S.out_done, j + 1)
            c0, c1 = UNITS[u]
            A.activation(T.yh[:, :, c0 * P:c1 * P], R.banks[:, 2 * u:2 * u + 2, 0:(c1 - c0) * P],
                         ACT.Copy).then_inc(S.yh_ready, 1)

        act.wait_ge(S.A_built, 1)
        counts_for_pe(0, 0, j0)
        act.wait_ge(S.xl_ready, n + 1)
        act.wait_ge(S.tr_done, CH * (n + 1))
        counts_for_pe(0, 1, j0 + 1)
        with act.Fori(0, TYPES - 1) as r:
            for u in range(2):
                high(u, r * 2 + (j0 + u))
                counts_for_pe(r + 1, u, r * 2 + (j0 + 2 + u))
        for u in range(2):
            high(u, j0 + 2 * TYPES - 2 + u)

    ln(0)
    xT(0)
    act.wait_ge(S.base_ready, 1)
    fits = act.value_load(T.fits[0:1, 0:1], min_val=0, max_val=1)
    A.sem_inc(S.staged, RING)
    A.sem_inc(S.oh_ready, 2)
    act.wait_ge(S.const_ready, 4)
    act.wait_ge(S.eT_ready, 2)
    with act.If(fits == 1):
        count(0)
    with act.Else():
        with act.Fori(0, WINDOWS) as w:
            count(w * GROUPS)
    layer(0)
    for c in range(CH):
        act.wait_ge(S.acc_read, c + 1)
        A.activation(T.xn[:, c, :], T.xn[:, c, :], ACT.Relu).then_inc(S.relu_ready, 1)
    xT(1)
    split()
    layer(1)

    ln(1)
    xT(2)
    act.wait_ge(S.y_done, 2 + 4 * TYPES)
    act.wait_ge(S.out_done, 2 + 4 * TYPES)

    def high(piece, s, n):
        act.wait_ge((S.stg0_in, S.stg1_in)[s], n * 32 + 32)
        w = slice(piece * PIECE, (piece + 1) * PIECE)
        A.activation((T.ewh0, T.ewh1)[s][:, w], T.stg[:, s, w], ACT.Copy).then_inc(S.ewh_ready, 1)

    for piece in range(PIECES):
        high(piece, 0, 0)
    act.wait_ge(S.eb_in, 32)
    A.sem_inc(S.ht_ready, 2)

    def experts(i, first=False, last=False):
        for s in range(2):
            for hb in range(HB):
                b = hb % 2
                if first and s == 0 and hb == 2:
                    act.wait_ge(S.gate_step, CH + 2)
                    A.activation(T.gp[:, 1, :], T.gp[:, 0, :], ACT.Exp).then_inc(S.gate_exp, 1)
                act.wait_ge(S.h_done, (i * 2 + s) * HB + hb + 1)
                act.wait_ge(S.hl_ready, (i * 2 + s) * HB + hb + 1)
                A.activation(T.ht[:, hb % HRING, :].rearrange("p (h n) -> p h n", h=2),
                             R.banks[:, 2 * b:2 * b + 2, 0:HALF], ACT.Relu,
                             bias=T.b1[:, bass.ds((i * 2 + s) * HB + hb, 1)]).then_inc(S.ht_ready, 1)
                if FIRST_PIECE <= hb < FIRST_PIECE + PIECES and not (last and s == 1):
                    act.wait_ge(S.h_used, (i * 2 + s) * HB + HB)
                    high(hb - FIRST_PIECE, 1 - s, i + s)

    experts(0, first=True)
    with act.Fori(1, EXPERTS // 2 - 1) as i:
        experts(i)
    experts(EXPERTS // 2 - 1, last=True)
    act.wait_ge(S.combT_done, 1)
    A.activation(T.combT[:, 0:4 * P], R.flat[0:EXPERTS, 1536:1536 + 4 * P], ACT.Copy)
    A.activation(T.combT[:, 4 * P:], R.flat[0:EXPERTS, 3584:3584 + P], ACT.Copy).then_inc(S.combT_ready, 1)

    for c in range(CH):
        act.wait_ge(S.ct_done, c + 1)
        A.activation(T.CT[:, c, :], R.flat[:, 1024 * (c % 2):1024 * (c % 2) + NP], ACT.Copy).then_inc(S.ct_ready, 1)
    ln(2)
    xT(3)
    act.wait_ge(S.w3_in, 48)
    act.wait_ge(S.adst_ready, 1)
    for h in range(HEADS1):
        k, o = divmod(h * HD1, P)
        A.activation(T.adst_bd[o:o + HD1, k, h:h + 1], T.adst[o:o + HD1, k:k + 1], ACT.Copy).then_inc(S.adst_ready, 1)
    A.activation(T.early[:, :], T.eps[:, :], ACT.Exp).then_inc(S.early, 1)
    act.wait_ge(S.hpT_done, 1)
    for k in range(KD):
        A.activation(T.hpT[:, k, :].rearrange("p (h n) -> p h n", h=2),
                     R.banks[:, 2 * k:2 * k + 2, 0:HALF], ACT.Copy).then_inc(S.hpT_ready, 1)

    def source_scores(h):
        b = h % 2
        act.wait_ge(S.es_done, h + 1)
        A.activation(T.es[:, h, :].rearrange("p (h n) -> p h n", h=2),
                     R.banks[:, 2 * b:2 * b + 2, 0:HALF], ACT.Copy).then_inc(S.es_ready, 1)

    def probs_T(j):
        act.wait_ge(S.pT_done, j + 1)
        h, c = divmod(j, CH)
        if c == 0 and h >= 2:
            act.wait_ge(S.agg_done, 2 * (h - 1))
        A.activation(T.pT[:, h % 2, :, c * P:(c + 1) * P],
                     R.flat[:, 1024 * (j % 2):1024 * (j % 2) + NP].rearrange("p (s n) -> p s n", s=CH),
                     ACT.Copy).then_inc(S.pT_ready, 1)

    def sums_T(h):
        act.wait_ge(S.agg_done, 2 * (h + 1))
        if h:
            act.wait_ge(S.turned_done, h)
        A.activation(T.oT[:, :].rearrange("p (h n) -> p h n", h=2), R.banks[0:HD1 + 1, 4:6, 0:HALF],
                     ACT.Copy).then_inc(S.oT_ready, 1)

    source_scores(0)
    source_scores(1)
    for j in range(HEADS1 * CH):
        h, c = divmod(j, CH)
        act.wait_ge(S.bounds_ready, h + 1)
        act.wait_ge(S.mt_ready, j + 1)
        if j >= EX_RING:
            act.wait_ge(S.em_ready, j - EX_RING + 1)
        for n, slope in enumerate((1.0, 0.2)):
            ins = A.activation(T.ex[:, j % EX_RING, n, :], T.mt[:, j % (2 * CH), :], ACT.Exp,
                               bias=T.ed2[:, n, c, h:h + 1], scale=slope)
        ins.then_inc(S.ex_ready, 1)
        if j + 2 < HEADS1:
            source_scores(j + 2)
        if j >= TURN_LAG:
            probs_T(j - TURN_LAG)
        if j - TURN_LAG >= CH and (j - TURN_LAG) % CH == SUMS_LAG:
            sums_T((j - TURN_LAG) // CH - 1)
    for j in range(HEADS1 * CH - TURN_LAG, HEADS1 * CH):
        probs_T(j)
        if j % CH == SUMS_LAG:
            sums_T(j // CH - 1)
    sums_T(HEADS1 - 1)

    ln(3)
    xT(4)
    act.wait_ge(S.temp_ready, 2)
    for b in range(IB):
        act.wait_ge(S.xm_done, b + 1)
        A.activation(T.xm[:, b, :].rearrange("p (h n) -> p h n", h=2),
                     R.banks[:, 2 * (b % 2):2 * (b % 2) + 2, 0:HALF], ACT.Identity,
                     bias=T.bxt[:, b:b + 1], scale=T.tcol[:, 2, b:b + 1]).then_inc(S.xm_ready, 1)

    def weights_T(c):
        act.wait_ge(S.swT_done, c + 1)
        A.activation(T.swT[:, :, c * P:(c + 1) * P], R.banks[:, 2 + c % 2, :].rearrange("p (b n) -> p b n", b=IB),
                     ACT.Copy).then_inc(S.swT_ready, 1)

    for c in range(CH):
        act.wait_ge(S.lg_step, 3 * c + 3)
        A.activation(T.sw[:, c, :], T.lg[:, c, :], ACT.Exp).then_inc(S.sm_exp, 1)
        if c >= 3:
            weights_T(c - 3)
    for c in range(CH - 3, CH):
        weights_T(c)
    act.wait_ge(S.tok_turned, 1)
    A.activation(T.tok[:, :], R.banks[0:HD2, 2, :], ACT.Copy).then_inc(S.tok_ready, 1)
    act.wait_ge(S.qkv_done, 2)
    A.activation(T.qk[:, :, :].rearrange("p a n -> p (a n)"), R.flat[0:HD2, 1024:2048], ACT.Copy).then_inc(S.qkv_ready, 1)
    act.wait_ge(S.qkv_done, 3)
    A.activation(T.vT[:, :], R.flat[0:HD2, 2048:2560], ACT.Copy).then_inc(S.qkv_ready, 1)
    act.wait_ge(S.al_step, 2)
    A.activation(T.at[:, 1, :], T.at[:, 0, :], ACT.Exp, scale=float(HD2) ** -0.5).then_inc(S.al_exp, 1)
    act.wait_ge(S.vo_done, 1)
    A.activation(T.vo[:, 0:4, :].rearrange("p h n -> p (h n)"), R.flat[0:SLICES, 1024:2048], ACT.Copy).then_inc(S.vo_ready, 1)
    act.wait_ge(S.atT_done, 1)
    A.activation(T.atT[:, :], R.flat[0:SLICES, 0:INNER], ACT.Copy).then_inc(S.atT_ready, 1)
    act.wait_ge(S.M_done, 1)
    A.activation(T.M[:, 0:2, :].rearrange("p b n -> p (b n)"), R.flat[:, 3072:3584], ACT.Copy).then_inc(S.M_ready, 1)


def pe_program(pe, nc, S, T, R):
    def mm3(o, lh, ll, rh, rl, start, stop, **kw):
        nc.tensor.matmul(o, lh, rh, start=start, stop=False, **kw)
        nc.tensor.matmul(o, lh, rl, start=False, stop=False, **kw)
        return nc.tensor.matmul(o, ll, rh, start=False, stop=stop, **kw)

    def keep_clock(products, bank):
        for _ in range(products):
            nc.tensor.matmul(R.banks[:, bank, 0:P], T.ident[:, :], T.ident[:, :], start=True, stop=True)

    def transpose_x(n):
        for c in range(CH):
            if n == 1:
                pe.wait_ge(S.relu_ready, c + 1)
            else:
                pe.wait_ge(S.ln_out, CH * max(n - 1, 0) + c + 1)
            if n == 0 and c == CH - 1:
                pe.wait_ge(S.eT_ready, 2)
            for k in range(KD):
                mm = nc.tensor.transpose(R.banks[:, c, k * P:(k + 1) * P], T.xn[:, c, k * P:(k + 1) * P], T.ident[:, :])
            mm.then_inc(S.tr_done, 1)

    def edges():
        pe.wait_ge(S.const_ready, 4)
        pe.wait_ge(S.ef_ready, 1)
        for n in range(5):
            for j in range(TILES):
                o = 2048 + (0 if n < 3 else 512) + ((n % 3) * TILES + j) * GROUPS
                mm = nc.tensor.transpose(R.flat[:, o:o + GROUPS], T.ef[:, n, j * P:(j + 1) * P],
                                         T.ident[0:GROUPS, 0:GROUPS])
        mm.then_inc(S.eT_done, 1)
        for n in range(2):
            o = 3072 + n * GROUPS
            mm = nc.tensor.transpose(R.flat[0:1, o:o + GROUPS], T.dlim[:, n:n + 1], T.ident[0:GROUPS, 0:GROUPS])
        mm.then_inc(S.base_done, 1)

    def counts(g0):
        with pe.Fori(0, GROUPS // RING) as i:
            for b in range(RING):
                pe.wait_ge(S.oh_ready, g0 + i * RING + b + 3)
                pe.wait_ge(S.ko_ready, g0 + i * RING + b + 1)
                pe.wait_ge(S.staged, g0 + i * RING + b + 1)
                for o, end in ((0, 512), (512, CH * KEYS)):
                    for j in range(TILES):
                        mm = nc.tensor.matmul(R.flat[:, 1024 * b + o:1024 * b + end], T.oh[:, b, j, :],
                                              T.ko[:, b, j, o:end], start=(j == 0), stop=(j == TILES - 1))
                mm.then_inc(S.counts_done, 1)

    def layer(n):
        wh, wl = ((T.wh0, T.wl0), (T.wh1, T.wl1))[n]
        j0 = 2 * TYPES * n

        def acc(c):
            return R.flat[:, 2048 + c * DIM:2048 + (c + 1) * DIM]

        def own_rows():
            pe.wait_ge(S.wh_ready, n + 1)
            pe.wait_ge(S.wl_ready, n + 1)
            pe.wait_ge(S.xTl_ready, CH * (n + 1))
            pe.wait_ge(S.xTh_ready, CH * (n + 1))
            for c in range(CH):
                for k in range(KD):
                    x = slice(c * P, (c + 1) * P)
                    mm3(acc(c), T.xTh[:, k, x], T.xTl[:, k, x], wh[:, TYPES, k, :], wl[:, TYPES, k, :],
                        start=(k == 0 and c % 2 == 0), stop=False, skip_group_check=True)

        def aggregate(u, j):
            pe.wait_ge(S.a_ready, j + 1)
            pe.wait_ge(S.yl_ready, j + 1)
            cols = (UNITS[u][1] - UNITS[u][0]) * P
            for k in range(KD):
                for x in (T.xh, T.xl):
                    for c in range(CH):
                        mm = nc.tensor.matmul(R.banks[:, 2 * u + k, 0:cols], x[:, c, k * P:(k + 1) * P], T.Ar[u][:, c, :],
                                              start=(c == 0 and x is T.xh), stop=(c == CH - 1 and x is T.xl))
            mm.then_inc(S.y_done, 1)

        def product(r, u, j, last=False):
            pe.wait_ge(S.yl_ready, j + 3)
            for c in range(*UNITS[u]):
                for k in range(KD):
                    x = slice(c * P, (c + 1) * P)
                    if type(r) is int:
                        h, l = wh[:, r, k, :], wl[:, r, k, :]
                    else:
                        h = wh[:, bass.ds(r, 1), k, :].rearrange("p a n -> p (a n)")
                        l = wl[:, bass.ds(r, 1), k, :].rearrange("p a n -> p (a n)")
                    mm = mm3(acc(c), T.yh[:, k, x], T.yl[:, k, x], h, l,
                             start=False, stop=(last and k == KD - 1), skip_group_check=True)
            mm.then_inc(S.out_done, 1)

        own_rows()
        pe.wait_ge(S.xh_ready, n + 1)
        pe.wait_ge(S.xl_ready, n + 1)
        aggregate(0, j0)
        with pe.Fori(0, TYPES - 1) as r:
            aggregate(1, r * 2 + (j0 + 1))
            product(r, 0, r * 2 + j0)
            aggregate(0, r * 2 + (j0 + 2))
            product(r, 1, r * 2 + (j0 + 1))
        j = j0 + 2 * TYPES - 2
        aggregate(1, j + 1)
        product(TYPES - 1, 0, j, last=True)
        product(TYPES - 1, 1, j + 1, last=True)

    edges()
    transpose_x(0)
    pe.wait_ge(S.base_ready, 1)
    fits = pe.value_load(T.fits[0:1, 0:1], min_val=0, max_val=1)
    nc.tensor.sem_inc(S.counts_done, RING)
    with pe.If(fits == 1):
        counts(0)
    with pe.Else():
        with pe.Fori(0, WINDOWS) as w:
            counts(w * GROUPS)
    nc.tensor.sem_inc(S.out_done, 2)
    nc.tensor.sem_inc(S.y_done, 2)
    pe.wait_ge(S.A_built, 1)
    layer(0)
    keep_clock(WARM["relu"], 7)
    transpose_x(1)
    keep_clock(WARM["relu_split"], 7)
    layer(1)

    keep_clock(WARM["second_norm"], 7)
    transpose_x(2)
    pe.wait_ge(S.xTh_ready, 3 * CH)
    pe.wait_ge(S.xTl_ready, 3 * CH)
    pe.wait_ge(S.wg_ready, 1)
    pe.wait_ge(S.acc_read, 2 * CH)
    for c in range(CH):
        for k in range(KD):
            x = slice(c * P, (c + 1) * P)
            mm = mm3(R.flat[:, 3584 + c * EXPERTS:3584 + (c + 1) * EXPERTS], T.xTh[:, k, x], T.xTl[:, k, x],
                     T.wgh[:, k, :], T.wgl[:, k, :], start=(k == 0), stop=(k == KD - 1))
    mm.then_inc(S.gate_mm, 1)

    def yacc(c):
        return R.flat[:, 2048 + c * DIM:2048 + (c + 1) * DIM]

    nc.tensor.sem_inc(S.h_used, HB)

    def hidden(wh, wl, hb, j):
        b = hb % 2
        pe.wait_ge(S.ht_ready, j + 1)
        for half in range(2):
            for k in range(KD):
                w = slice(k * HID + hb * P, k * HID + (hb + 1) * P)
                n = slice(half * HALF, (half + 1) * HALF)
                mm = mm3(R.banks[:, 2 * b + half, 0:HALF], wh[:, w], wl[:, w], T.xTh[:, k, n], T.xTl[:, k, n],
                         start=(k == 0), stop=(k == KD - 1))
        mm.then_inc(S.h_done, 1)

    def outputs(wh, wl, hb, j, e):
        pe.wait_ge(S.hl_ready, j + HRING + 1)
        w = slice(2 * HID + hb * DIM, 2 * HID + (hb + 1) * DIM)
        for c in range(CH):
            if hb == 0 and c % 2 == 0:
                pe.wait_ge(S.yacc_added, e * CH + min(c + 2, CH))
            x = slice(c * P, (c + 1) * P)
            mm = mm3(yacc(c), T.hh[:, hb % HRING, x], T.hl[:, hb % HRING, x], wh[:, w], wl[:, w],
                     start=(hb == 0 and c % 2 == 0), stop=(hb == HB - 1), skip_group_check=True)
        mm.then_inc(S.h_used, 1)

    LAG = 2
    sets = ((T.ewh0, T.ewl0), (T.ewh1, T.ewl1))

    def experts(i, first):
        for n in range(2 * HB):
            s, hb = divmod(n, HB)
            if hb == 0:
                pe.wait_ge(S.ewl_ready, (i * 2 + s + 1) * PIECES)
            hidden(*sets[s], hb, i * (2 * HB) + n)
            if n >= LAG or not first:
                m = n - LAG
                s2, hb2 = divmod(m % (2 * HB), HB)
                outputs(*sets[s2], hb2, i * (2 * HB) + m, i * 2 + (s2 if m >= 0 else s2 - 2))

    pe.wait_ge(S.xTl_ready, 3 * CH)
    experts(0, True)
    with pe.Fori(1, EXPERTS // 2) as i:
        experts(i, False)
    pe.wait_ge(S.comb_ready, 1)
    pe.wait_ge(S.ht_ready, EXPERTS * HB + 2)
    for c in range(CH):
        o = 1536 + c * P if c < 4 else 3584
        mm = nc.tensor.transpose(R.flat[0:EXPERTS, o:o + P], T.comb[:, c, :], T.ident[:, :])
    mm.then_inc(S.combT_done, 1)
    outputs(*sets[1], HB - 2, EXPERTS * HB - 2, EXPERTS - 1)
    pe.wait_ge(S.combT_ready, 1)
    pe.wait_ge(S.eb_in, 32)
    for c in range(CH):
        mm = nc.tensor.matmul(R.flat[:, c * DIM:(c + 1) * DIM], T.combT[:, c * P:(c + 1) * P], T.b2[:, :],
                              start=True, stop=True)
    mm.then_inc(S.b2_done, 1)
    outputs(*sets[1], HB - 1, EXPERTS * HB - 1, EXPERTS - 1)
    pe.wait_ge(S.b2_added, 1)

    pe.wait_ge(S.C_built, 1)
    for c in range(CH):
        if c >= 2:
            pe.wait_ge(S.ct_ready, c - 1)
        for s in range(CH):
            o = 1024 * (c % 2) + s * P
            mm = nc.tensor.transpose(R.flat[:, o:o + P], T.C[:, s, c * P:(c + 1) * P], T.ident[:, :])
        mm.then_inc(S.ct_done, 1)
    keep_clock(WARM["third_norm"], 7)
    pe.wait_ge(S.ct_ready, CH)
    transpose_x(3)
    pe.wait_ge(S.xTh_ready, 4 * CH)
    pe.wait_ge(S.xTl_ready, 4 * CH)
    pe.wait_ge(S.w3_ready, 3)
    for f in range(KD):
        for half in range(2):
            n = slice(half * HALF, (half + 1) * HALF)
            for k in range(KD):
                w = slice(f * P, (f + 1) * P)
                mm = mm3(R.banks[:, 2 * f + half, 0:HALF], T.w3h[:, k, w], T.w3l[:, k, w],
                         T.xTh[:, k, n], T.xTl[:, k, n], start=(k == 0), stop=(k == KD - 1))
    mm.then_inc(S.hpT_done, 1)
    pe.wait_ge(S.asrc_ready, 1)
    pe.wait_ge(S.hpT_ready, 2)

    def source_scores(h):
        k, o = divmod(h * HD1, P)
        b = h % 2
        if h >= 2:
            pe.wait_ge(S.es_ready, h - 1)
        for half in range(2):
            mm = nc.tensor.matmul(R.banks[:, 2 * b + half, 0:HALF], T.asrc_bc[o:o + HD1, k, :],
                                  T.hpT[o:o + HD1, k, half * HALF:(half + 1) * HALF], start=True, stop=True)
        mm.then_inc(S.es_done, 1)

    source_scores(0)
    source_scores(1)
    pe.wait_ge(S.adst_ready, 1 + HEADS1)
    for c in range(CH):
        for k in range(KD):
            mm = nc.tensor.matmul(R.flat[:, 3584 + c * HEADS1:3584 + (c + 1) * HEADS1], T.hpT[:, k, c * P:(c + 1) * P],
                                  T.adst_bd[:, k, :], start=(k == 0), stop=(k == KD - 1))
    mm.then_inc(S.ed_done, 1)
    for h in range(2, HEADS1):
        source_scores(h)

    def hp(c):
        x = slice(c * P, (c + 1) * P)
        for k in range(KD):
            mm = mm3(R.flat[:, 2048 + c * DIM:2048 + (c + 1) * DIM], T.xTh[:, k, x], T.xTl[:, k, x],
                     T.w3h[:, k, :], T.w3l[:, k, :], start=(k == 0), stop=(k == KD - 1))
        mm.then_inc(S.hp_done, 1)

    def turn(j):
        pe.wait_ge(S.pr_ready, j + 1)
        if j < 2:
            pe.wait_ge(S.es_ready, j + 3)
        else:
            pe.wait_ge(S.pT_ready, j - 1)
        for s in range(CH):
            o = 1024 * (j % 2) + s * P
            mm = nc.tensor.transpose(R.flat[:, o:o + P], T.pr[:, j % EM_RING, s * P:(s + 1) * P], T.ident[:, :])
        mm.then_inc(S.pT_done, 1)

    def gather(h, half):
        pe.wait_ge(S.hp_ready, 1)
        pe.wait_ge(S.pT_ready, CH * (h + 1))
        if h:
            pe.wait_ge(S.oT_ready, h)
        for s in range(CH):
            mm = nc.tensor.matmul(R.banks[0:HD1 + 1, 4 + half, 0:HALF], T.hp[:, s, h, :],
                                  T.pT[:, h % 2, s, half * HALF:(half + 1) * HALF],
                                  start=(s == 0), stop=(s == CH - 1))
        mm.then_inc(S.agg_done, 1)

    def turn_sums(h):
        pe.wait_ge(S.oT_ready, h + 1)
        pe.wait_ge(S.ed_ready, 1)
        if h >= 2:
            pe.wait_ge(S.x3_ready, h - 1)
        for c in range(CH):
            mm = nc.tensor.transpose(R.banks[:, 6 + h % 2, c * (HD1 + 1):(c + 1) * (HD1 + 1)], T.oT[:, c * P:(c + 1) * P],
                                     T.ident[0:HD1 + 1, 0:HD1 + 1])
        mm.then_inc(S.turned_done, 1)

    for j in range(HEADS1 * CH):
        h, c = divmod(j, CH)
        if j < CH:
            hp(j)
        turn(j)
        if h and GATHER_LAG <= c < GATHER_LAG + 2:
            gather(h - 1, c - GATHER_LAG)
        if h and c == CH - 1:
            turn_sums(h - 1)
    for half in range(2):
        gather(HEADS1 - 1, half)
    turn_sums(HEADS1 - 1)

    keep_clock(WARM["last_norm"], 5)
    transpose_x(4)
    pe.wait_ge(S.xTh_ready, 5 * CH)
    pe.wait_ge(S.xTl_ready, 5 * CH)
    pe.wait_ge(S.wx_ready, 2)
    pe.wait_ge(S.w4_in, W4_LOADS)
    for b in range(IB):
        if b >= 2:
            pe.wait_ge(S.xm_ready, b - 1)
        for half in range(2):
            n = slice(half * HALF, (half + 1) * HALF)
            for k in range(KD):
                w = slice(b * P, (b + 1) * P)
                mm = mm3(R.banks[:, 2 * (b % 2) + half, 0:HALF], T.wxh[:, k, w], T.wxl[:, k, w],
                         T.xTh[:, k, n], T.xTl[:, k, n], start=(k == 0), stop=(k == KD - 1))
        mm.then_inc(S.xm_done, 1)
    pe.wait_ge(S.xm_ready, IB)

    def slice_scores(c):
        if c >= 2:
            pe.wait_ge(S.lg_step, 3 * (c - 2) + 1)
        for b in range(IB):
            mm = nc.tensor.matmul(R.banks[:, 6 + c % 2, b * P:(b + 1) * P], T.xm[:, b, c * P:(c + 1) * P],
                                  T.wsl[:, :], start=True, stop=True)
        mm.then_inc(S.lg_done, 1)

    def fx_mid(c):
        if c >= 2:
            pe.wait_ge(S.fx_ready, c - 1)
        x = slice(c * P, (c + 1) * P)
        for k in range(KD):
            mm = mm3(R.banks[:, 4 + c % 2, :], T.xTh[:, k, x], T.xTl[:, k, x], T.wfxh[:, k, :], T.wfxl[:, k, :],
                     start=(k == 0), stop=(k == KD - 1))
        mm.then_inc(S.fx_done, 1)

    def tokens(c):
        pe.wait_ge(S.sw_ready, c + 1)
        if c >= 2:
            pe.wait_ge(S.swT_ready, c - 1)
        for b in range(IB):
            mm = nc.tensor.transpose(R.banks[:, 2 + c % 2, b * P:(b + 1) * P], T.sw[:, c, b * P:(b + 1) * P],
                                     T.ident[:, :])
        mm.then_inc(S.swT_done, 1)
        k = chunks(T, c)
        pe.wait_ge(S.fx_ready, c + 1)
        for h in range(HEADS2):
            b, o = divmod(h, 4)
            mm = nc.tensor.matmul(R.banks[0:SLICES, b, o * (HD2 + 1):(o + 1) * (HD2 + 1)],
                                  T.sw[0:k, c, h * SLICES:(h + 1) * SLICES], T.fx[0:k, c, h, :],
                                  start=(c == 0 and o == 0), stop=(c == CH - 1), skip_group_check=True)
        return mm

    slice_scores(0)
    slice_scores(1)
    pe.wait_ge(S.wfx_ready, 2)
    pe.wait_ge(S.fx_ones, 1)
    for c in range(CH):
        fx_mid(c)
        if c + 2 < CH:
            slice_scores(c + 2)
        if c >= TOK_LAG:
            tokens(c - TOK_LAG)
    for c in range(CH - TOK_LAG, CH):
        mm = tokens(c)
    mm.then_inc(S.tok_done, 1)
    keep_clock(WARM["token_norm"], 7)
    pe.wait_ge(S.tokT_ready, 1)
    pe.wait_ge(S.swT_ready, CH)
    for h in range(HEADS2):
        w = slice(h * HD2, (h + 1) * HD2)
        mm = nc.tensor.transpose(R.banks[0:HD2, 2, w], T.tokT[:, w], T.ident[0:SLICES, 0:SLICES])
    mm.then_inc(S.tok_turned, 1)
    keep_clock(WARM["token_copy"], 7)
    pe.wait_ge(S.tok_ready, 1)
    for n in range(3):
        mm = nc.tensor.matmul(R.flat[0:HD2, 1024 + 512 * n:1536 + 512 * n], T.wqkv[:, n, :], T.tok[:, :],
                              start=True, stop=True)
        mm.then_inc(S.qkv_done, 1)
    keep_clock(WARM["query_copy"], 7)
    pe.wait_ge(S.qkv_ready, 1)
    for h in range(HEADS2):
        w = slice(h * SLICES, (h + 1) * SLICES)
        mm = nc.tensor.matmul(R.flat[0:SLICES, 512 + h * SLICES:512 + (h + 1) * SLICES], T.qk[:, 0, w], T.qk[:, 1, w],
                              start=True, stop=True)
    mm.then_inc(S.al_done, 1)
    pe.wait_ge(S.qkv_ready, 2)
    for h in range(HEADS2):
        mm = nc.tensor.matmul(R.flat[0:SLICES, 1024 + h * DIM:1024 + (h + 1) * DIM], T.vT[:, h * HD2:(h + 1) * HD2],
                              T.wo[:, h, :], start=True, stop=True)
        if h % 4 == 3:
            mm.then_inc(S.vo_done, 1)
    pe.wait_ge(S.at_ready, 1)
    for h in range(HEADS2):
        w = slice(h * SLICES, (h + 1) * SLICES)
        mm = nc.tensor.transpose(R.flat[0:SLICES, w], T.at[:, 2, w], T.ident[0:SLICES, 0:SLICES])
    mm.then_inc(S.atT_done, 1)
    keep_clock(WARM["attention_copy"], 7)
    pe.wait_ge(S.atT_ready, 1)
    pe.wait_ge(S.vo_ready, 2)
    for h in range(HEADS2):
        b, o = divmod(h * SLICES, P)
        mm = nc.tensor.matmul(R.flat[o:o + SLICES, 3072 + b * DIM:3072 + (b + 1) * DIM], T.atT[:, h * SLICES:(h + 1) * SLICES],
                              T.vo[:, h, :], start=True, stop=True)
        if h % 4 == 3:
            mm.then_inc(S.M_done, 1)
    keep_clock(WARM["projection_copy"], 0)
    pe.wait_ge(S.M_ready, 2)
    for c in range(CH):
        for b in range(IB):
            mm = nc.tensor.matmul(R.banks[:, 1 + c, 0:DIM], T.swT[:, b, c * P:(c + 1) * P],
                                  T.M[:, b, :], start=(b == 0), stop=(b == IB - 1))
        mm.then_inc(S.out4_done, 1)


def dve_program(dve, nc, S, T, R):
    V = nc.vector

    def ln(n):
        for c in range(CH):
            V.bn_stats(T.stats[:, c, :], T.X[:, c, :]).then_inc(S.ln_stats, 1)
        for c in range(CH):
            dve.wait_ge(S.ln_stats, CH * n + c + 1)
            V.bn_aggr(T.mv[:, c, :], T.stats[:, c, :]).then_inc(S.ln_aggr, 1)
        dve.wait_ge(S.ln_std, n + 1)
        V.reciprocal(T.rstd[:, :], T.std[:, :]).then_inc(S.ln_rstd, 1)
        dve.wait_ge(S.ln_rstd, n + 1)
        for c in range(CH):
            V.tensor_scalar(T.xn[:, c, :], T.X[:, c, :], T.mv[:, c, 0:1], T.rstd[:, c:c + 1],
                            ALU.subtract, ALU.mult).then_inc(S.ln_out, 1)

    def xT(n):
        for c in range(CH):
            dve.wait_ge(S.xTh_ready, CH * n + c + 1)
            x = slice(c * P, (c + 1) * P)
            V.tensor_tensor(T.xTl[:, :, x], R.banks[:, c, 0:DIM].rearrange("p (k n) -> p k n", k=KD),
                            T.xTh[:, :, x].bitcast(F32), ALU.subtract).then_inc(S.xTl_ready, 1)

    def split():
        dve.wait_ge(S.xh_ready, 2)
        V.tensor_tensor(T.xl[:, :, :], T.xn[:, :, :], T.xh[:, :, :].bitcast(F32), ALU.subtract).then_inc(S.xl_ready, 1)

    def edges():
        dve.wait_ge(S.e_in, 96)
        V.tensor_scalar(T.ei[:, 3, :], T.ei[:, 2, :], -P, None, ALU.bitwise_and).then_inc(S.src_ready, 1)
        V.tensor_copy(T.ef[:, 0:2, :], T.ei[:, 0:2, :]).then_inc(S.ef_step, 1)
        dve.wait_ge(S.src_ready, 1)
        V.tensor_copy(T.ef[:, 3, :], T.ei[:, 3, :]).then_inc(S.src_ready, 1)
        V.tensor_tensor(T.ef[:, 2, :], T.ei[:, 2, :], T.ei[:, 3, :], ALU.subtract).then_inc(S.src_ready, 1)
        dve.wait_ge(S.ef_step, 1)
        V.tensor_reduce(T.dlim[:, 0:1], T.ef[:, 0, :], AX.X, ALU.min).then_inc(S.ef_step, 1)
        V.scalar_tensor_tensor(T.ef[:, 4, :], T.ef[:, 0, :], float(OUTSIDE), T.ef[:, 0, :],
                               ALU.is_lt, ALU.mult).then_inc(S.ef_step, 1)
        dve.wait_ge(S.ef_step, 3)
        V.tensor_reduce(T.dlim[:, 2:3], T.ef[:, 4, :], AX.X, ALU.max).then_inc(S.ef_step, 1)
        dve.wait_ge(S.ef_step, 4)
        V.tensor_tensor(T.dlim[:, 1:2], T.dlim[:, 2:3], T.dlim[:, 0:1], ALU.subtract).then_inc(S.ef_step, 1)
        V.scalar_tensor_tensor(T.ef[:, 4, :], T.ef[:, 1, :], float(WIN), T.ef[:, 0, :],
                               ALU.mult, ALU.add).then_inc(S.ef_step, 1)
        dve.wait_ge(S.ef_step, 6)
        dve.wait_ge(S.src_ready, 3)
        V.scalar_tensor_tensor(T.ef[:, 4, :], T.ef[:, 4, :], T.dlim[:, 0:1], T.ef[:, 3, :],
                               ALU.subtract, ALU.add).then_inc(S.ef_ready, 1)

    def edge_columns():
        n = 3 * TILES * GROUPS
        flat = T.eT[:, :, :, :].rearrange("p a t g -> p (a t g)")
        dve.wait_ge(S.eT_done, 1)
        V.tensor_copy(flat[:, 0:n], R.flat[:, 2048:2048 + n]).then_inc(S.eT_ready, 1)
        V.tensor_copy(flat[:, n:n + 2 * TILES * GROUPS], R.flat[:, 2560:2560 + 2 * TILES * GROUPS]).then_inc(S.eT_ready, 1)
        dve.wait_ge(S.base_done, 1)
        V.tensor_copy(T.bases[:, 0:GROUPS], R.flat[0:1, 3072:3072 + GROUPS]).then_inc(S.base_step, 1)
        V.tensor_reduce(T.spanmax[:, 0:1], R.flat[0:1, 3072 + GROUPS:3072 + 2 * GROUPS], AX.X, ALU.max).then_inc(S.base_step, 1)
        dve.wait_ge(S.base_step, 2)
        V.tensor_scalar(T.spanmax[:, 1:2], T.spanmax[:, 0:1], float(FIT_BELOW), None, ALU.is_lt).then_inc(S.base_step, 1)
        dve.wait_ge(S.base_step, 3)
        V.tensor_copy(T.fits[:, :], T.spanmax[:, 1:2]).then_inc(S.base_ready, 1)

    def counts(key, g0, bases_from):
        def one_hot(g, b):
            dve.wait_ge(S.counts_done, g + g0 + 1)
            for j in range(ACT_TILES, TILES):
                V.tensor_scalar(T.oh[:, b, j, :], T.iota[:, 0:P], T.eT[:, 2, j, bass.ds(g, 1)], None, ALU.is_equal)
            for j in range(TILES):
                ins = V.tensor_scalar(T.ko[:, b, j, :], T.iota[:, :], key[:, j, bass.ds(g, 1)], None, ALU.is_equal)
            ins.then_inc(S.ko_ready, 1)

        def add(g, b, base):
            dve.wait_ge(S.staged, g + g0 + RING + 1)
            dve.wait_ge(S.added, g + g0 + RING)
            at = T.A[:, :, :, bass.ds(base, WIN)]
            V.tensor_tensor(at, at, T.add[:, b, :].rearrange("p (c r d) -> p c r d", c=CH, r=TYPES),
                            ALU.add).then_inc(S.added, 1)

        def both(g, b, base):
            one_hot(g + lag, (b + lag) % RING)
            add(g, b % RING, base)

        lag = RING - 1
        for g in range(lag):
            one_hot(g, g)
        with dve.Fori(0, GROUPS // UNROLLED - 1) as i:
            bases = bases_from(i * UNROLLED)
            for b in range(UNROLLED):
                both(i * UNROLLED + b, b, bases[b])
        bases = bases_from(GROUPS - UNROLLED)
        for b in range(UNROLLED - lag):
            both(GROUPS - UNROLLED + b, b, bases[b])
        for b in range(UNROLLED - lag, UNROLLED):
            add(GROUPS - UNROLLED + b, b % RING, bases[b])

    def window_keys(w):
        flat = T.eT[:, :, :, :].rearrange("p a t g -> p a (t g)")
        d, t, chunk = flat[:, 0, :], flat[:, 1, :], flat[:, 3, :]
        rel, low, high, key = (T.kgen[:, n, :] for n in range(4))
        dve.wait_ge(S.added, w * GROUPS + RING)
        dve.wait_ge(S.w16_step, w + 1)
        V.tensor_scalar(rel, d, T.w16[:, 0:1], None, ALU.subtract).then_inc(S.key_step, 1)
        dve.wait_ge(S.key_step, w * 7 + 1)
        V.tensor_scalar(low, rel, 0.0, float(OUTSIDE), ALU.is_lt, ALU.mult).then_inc(S.key_step, 1)
        V.tensor_scalar(high, rel, float(WIN), float(OUTSIDE), ALU.is_ge, ALU.mult).then_inc(S.key_step, 1)
        V.scalar_tensor_tensor(key, t, float(WIN), rel, ALU.mult, ALU.add).then_inc(S.key_step, 1)
        dve.wait_ge(S.key_step, w * 7 + 4)
        V.tensor_tensor(key, key, low, ALU.add).then_inc(S.key_step, 1)
        dve.wait_ge(S.key_step, w * 7 + 5)
        V.tensor_tensor(low, chunk, high, ALU.add).then_inc(S.key_step, 1)
        dve.wait_ge(S.key_step, w * 7 + 6)
        V.tensor_tensor(key, key, low, ALU.add).then_inc(S.key_step, 1)
        dve.wait_ge(S.key_step, w * 7 + 7)
        V.tensor_scalar(T.w16[:, :], T.w16[:, :], float(WIN), None, ALU.add).then_inc(S.w16_step, 1)

    def layer(n):
        j0 = 2 * TYPES * n
        if n:
            V.tensor_tensor(T.X[:, :, :], T.X[:, :, :], T.b_bc[:, n, :].unsqueeze(1).to_broadcast([P, CH, DIM]),
                            ALU.add).then_inc(S.layer_step, 1)
        with dve.Fori(0, TYPES) as r:
            for u, (c0, c1) in enumerate(UNITS):
                dve.wait_ge(S.yh_ready, r * 2 + (j0 + u + 1))
                dve.wait_ge(S.out_done, r * 2 + (j0 + u + 1))
                V.tensor_tensor(T.yl[:, :, c0 * P:c1 * P], R.banks[:, 2 * u:2 * u + 2, 0:(c1 - c0) * P],
                                T.yh[:, :, c0 * P:c1 * P].bitcast(F32), ALU.subtract).then_inc(S.yl_ready, 1)
        dve.wait_ge(S.out_done, 2 + 2 * TYPES * (n + 1))
        if n == 0:
            dve.wait_ge(S.b_in, 32)
            for c in range(CH):
                V.tensor_tensor(T.xn[:, c, :], R.flat[:, 2048 + c * DIM:2048 + (c + 1) * DIM], T.b_bc[:, n, :],
                                ALU.add).then_inc(S.acc_read, 1)
        else:
            dve.wait_ge(S.layer_step, 1)
            for c in range(CH):
                V.tensor_tensor(T.X[:, c, :], T.X[:, c, :], R.flat[:, 2048 + c * DIM:2048 + (c + 1) * DIM],
                                ALU.add).then_inc(S.acc_read, 1)
            dve.wait_ge(S.acc_read, 2 * CH)
            dve.wait_ge(S.C_built, 1)

    V.memset(T.A[:, 0:A_BY_DVE, :, :].rearrange("p c r n -> p (c r n)"), 0.0).then_inc(S.a_zero, 1)
    edges()
    dve.wait_ge(S.x_in, 32)
    ln(0)
    edge_columns()
    xT(0)
    V.sem_inc(S.added, RING)
    dve.wait_ge(S.base_ready, 1)
    fits = dve.value_load(T.fits[0:1, 0:1], min_val=0, max_val=1)
    dve.wait_ge(S.const_ready, 4)
    dve.wait_ge(S.eT_ready, 2)
    dve.wait_ge(S.a_zero, 2)
    with dve.If(fits == 1):
        counts(T.eT[:, 4, :, :], 0,
               lambda g: nc.values_load_multi_w_load_instructions(
                   T.bases[0:1, bass.ds(g, UNROLLED)], engines=(mybir.EngineType.DVE,), min_val=0, max_val=NODES - 1,
                   skip_runtime_bounds_check_because="a group's first destination is a node")[1])
        dve.wait_ge(S.added, GROUPS + RING)
    with dve.Else():
        V.memset(T.w16[:, :], 0.0).then_inc(S.w16_step, 1)
        with dve.Fori(0, WINDOWS) as w:
            window_keys(w)
            counts(T.kgen[:, 3, :].rearrange("p (t g) -> p t g", t=TILES), w * GROUPS, lambda g: [w * WIN] * UNROLLED)
        dve.wait_ge(S.added, GROUPS * WINDOWS + RING)
    V.sem_inc(S.A_built, 1)
    V.sem_inc(S.yl_ready, 2)
    layer(0)
    xT(1)
    split()
    layer(1)

    ln(1)
    xT(2)

    def low(e, piece, s):
        dve.wait_ge(S.ewh_ready, e * PIECES + piece + 1)
        w = slice(piece * PIECE, (piece + 1) * PIECE)
        V.tensor_tensor((T.ewl0, T.ewl1)[s][:, w], T.stg[:, s, w], (T.ewh0, T.ewh1)[s][:, w].bitcast(F32),
                        ALU.subtract).then_inc(S.ewl_ready, 1)

    for piece in range(PIECES):
        low(0, piece, 0)

    def gate_scores():
        dve.wait_ge(S.gate_mm, 1)
        dve.wait_ge(S.gate_in, 32)
        dve.wait_ge(S.gate_const, 1)
        V.tensor_tensor(T.gate[:, :, :], R.flat[:, 3584:3584 + CH * EXPERTS].rearrange("p (c e) -> p c e", c=CH),
                        T.bg[:, :].unsqueeze(1).to_broadcast([P, CH, EXPERTS]), ALU.add).then_inc(S.gate_step, 1)
        dve.wait_ge(S.gate_step, 1)
        for c in range(CH):
            V.max(T.top[:, c, :], T.gate[:, c, :]).then_inc(S.gate_step, 1)
        dve.wait_ge(S.gate_step, CH + 1)
        V.tensor_tensor(T.gp[:, 0, :], T.top[:, :, 1], T.top[:, :, 0], ALU.subtract).then_inc(S.gate_step, 1)

    def gate_ranks():
        for c in range(CH):
            V.max_index(T.topi[:, c, :], T.top[:, c, :], T.gate[:, c, :]).then_inc(S.gate_step, 1)
        dve.wait_ge(S.gate_step, 2 * CH + 2)
        V.tensor_copy(T.topf[:, :, :], T.topi[:, :, :]).then_inc(S.gate_step, 1)

    def gate_shares():
        dve.wait_ge(S.gate_exp, 1)
        V.tensor_scalar(T.gp[:, 2, :], T.gp[:, 1, :], 1.0, None, ALU.add).then_inc(S.gate_step, 1)
        dve.wait_ge(S.gate_step, 2 * CH + 4)
        V.reciprocal(T.gp[:, 3, :], T.gp[:, 2, :]).then_inc(S.gate_step, 1)
        dve.wait_ge(S.gate_step, 2 * CH + 5)
        V.tensor_tensor(T.gp[:, 4, :], T.gp[:, 1, :], T.gp[:, 3, :], ALU.mult).then_inc(S.gate_step, 1)
        dve.wait_ge(S.gate_step, 2 * CH + 6)

    def gate_of(n, to):
        for c in range(CH):
            V.tensor_scalar(to[:, c, :], T.iota8[:, :], T.topf[:, c, n:n + 1], T.gp[:, 3 + n, c:c + 1],
                            ALU.is_equal, ALU.mult).then_inc(S.gate_step, 1)

    def gate_together():
        dve.wait_ge(S.gate_step, 4 * CH + 6)
        V.tensor_tensor(T.comb[:, :, :], T.comb[:, :, :], T.ctmp[:, :, :], ALU.add).then_inc(S.comb_ready, 1)
        dve.wait_ge(S.comb_ready, 1)

    def no_edges(c):
        dve.wait_ge(S.ct_ready, CH)
        V.tensor_scalar(T.negm[:, c, :], T.CT[:, c, :], 0.0, NEG, ALU.is_equal, ALU.mult).then_inc(S.negm_ready, 1)

    V.sem_inc(S.yacc_added, CH)
    V.sem_inc(S.hl_ready, HRING)

    def take_sums(e):
        dve.wait_ge(S.h_used, e * HB + 2 * HB)
        for c in range(CH):
            V.scalar_tensor_tensor(T.X[:, c, :], R.flat[:, 2048 + c * DIM:2048 + (c + 1) * DIM],
                                   T.comb[:, c, bass.ds(e, 1)], T.X[:, c, :], ALU.mult, ALU.add).then_inc(S.yacc_added, 1)

    LAG = 2

    def experts(i, first=False, last=False):
        for s in range(2):
            e = i * 2 + s
            for hb in range(HB):
                j = e * HB + hb
                b = hb % HRING
                if hb == LAG and not (first and s == 0):
                    dve.wait_ge(S.yacc_added, e * CH)
                    take_sums(e - 1)
                dve.wait_ge(S.ht_ready, j + 3)
                dve.wait_ge(S.h_used, j + (HB - HRING + 1))
                V.tensor_copy(T.hh[:, b, :], T.ht[:, b, :]).then_inc(S.hh_ready, 1)
                dve.wait_ge(S.hh_ready, j + 1)
                V.tensor_tensor(T.hl[:, b, :], T.ht[:, b, :], T.hh[:, b, :].bitcast(F32),
                                ALU.subtract).then_inc(S.hl_ready, 1)
                if FIRST_PIECE <= hb < FIRST_PIECE + PIECES and not (last and s == 1):
                    low(e + 1, hb - FIRST_PIECE, 1 - s)
                if first and s == 0:
                    if hb == 0:
                        gate_scores()
                    if hb == 1:
                        gate_ranks()
                    if hb == 3:
                        gate_shares()
                    if hb == 4:
                        gate_of(0, T.comb)
                    if hb == 5:
                        gate_of(1, T.ctmp)
                    if hb == 6:
                        gate_together()

    experts(0, first=True)
    with dve.Fori(1, EXPERTS // 2 - 1) as i:
        experts(i)
    experts(EXPERTS // 2 - 1, last=True)
    dve.wait_ge(S.yacc_added, EXPERTS * CH)
    dve.wait_ge(S.b2_done, 1)
    V.tensor_tensor(T.X[:, :, :].rearrange("p c d -> p (c d)"), T.X[:, :, :].rearrange("p c d -> p (c d)"),
                    R.flat[:, 0:CH * DIM], ALU.add).then_inc(S.b2_added, 1)
    dve.wait_ge(S.b2_added, 1)
    take_sums(EXPERTS - 1)
    dve.wait_ge(S.yacc_added, (EXPERTS + 1) * CH)
    V.sem_inc(S.experts_done, 1)

    ln(2)
    xT(3)
    dve.wait_ge(S.w3_in, 48)
    dve.wait_ge(S.w3_ready, 1)
    for c in range(CH):
        no_edges(c)
    for k in range(KD):
        ins = V.tensor_scalar(T.asrc_bc[:, k, :], T.ident[:, :], 0.0, T.asrc[:, k:k + 1], ALU.mult, ALU.add)
    ins.then_inc(S.asrc_ready, 1)

    def masked(n):
        h, c = divmod(n, CH)
        dve.wait_ge(S.es_ready, h + 1)
        dve.wait_ge(S.negm_ready, c + 1)
        if n >= 2 * CH:
            dve.wait_ge(S.ex_ready, n - 2 * CH + 1)
        V.tensor_tensor_reduce(T.mt[:, n % (2 * CH), :], T.es[:, h, :], T.negm[:, c, :], 1.0, NEG, ALU.add, ALU.max,
                               T.mes[:, c, h:h + 1]).then_inc(S.mt_ready, 1)

    def bounds(h):
        dve.wait_ge(S.mt_ready, (h + 1) * CH)
        dve.wait_ge(S.ed_ready, 1)
        V.tensor_tensor(T.tm[:, :, h], T.mes[:, :, h], T.ed[:, :, h], ALU.add).then_inc(S.bound_step, 1)
        dve.wait_ge(S.bound_step, 3 * h + 1)
        V.scalar_tensor_tensor(T.nm[:, :, h], T.tm[:, :, h], 0.2, T.tm[:, :, h], ALU.mult, ALU.max).then_inc(S.bound_step, 1)
        dve.wait_ge(S.bound_step, 3 * h + 2)
        V.tensor_tensor(T.ed2[:, 0, :, h], T.ed[:, :, h], T.nm[:, :, h], ALU.subtract).then_inc(S.bound_step, 1)
        V.scalar_tensor_tensor(T.ed2[:, 1, :, h], T.ed[:, :, h], 0.2, T.nm[:, :, h],
                               ALU.mult, ALU.subtract).then_inc(S.bounds_ready, 1)

    def larger(j):
        dve.wait_ge(S.ex_ready, j + 1)
        if j >= EM_RING:
            dve.wait_ge(S.pr_ready, j - EM_RING + 1)
        V.tensor_tensor(T.em[:, j % EM_RING, :], T.ex[:, j % EX_RING, 0, :], T.ex[:, j % EX_RING, 1, :], ALU.max).then_inc(S.em_ready, 1)

    def normalise(h):
        o = 3072 + 512 * (h % 2)
        sums = R.flat[:, o:o + CH * (HD1 + 1)].rearrange("p (c d) -> p c d", c=CH)
        dve.wait_ge(S.turned_done, h + 1)
        V.tensor_scalar(T.den[:, 0, :], sums[:, :, HD1], 1e-16, None, ALU.add).then_inc(S.o3_step, 1)
        dve.wait_ge(S.o3_step, 3 * h + 1)
        V.reciprocal(T.den[:, 1, :], T.den[:, 0, :]).then_inc(S.o3_step, 1)
        dve.wait_ge(S.o3_step, 3 * h + 2)
        V.tensor_tensor(T.o3[:, :, :], sums[:, :, 0:HD1], T.den[:, 1, :].unsqueeze(2).to_broadcast([P, CH, HD1]),
                        ALU.mult).then_inc(S.o3_step, 1)
        dve.wait_ge(S.o3_step, 3 * h + 3)
        V.tensor_tensor(T.X[:, :, h * HD1:(h + 1) * HD1], T.X[:, :, h * HD1:(h + 1) * HD1], T.o3[:, :, :],
                        ALU.add).then_inc(S.x3_ready, 1)

    def take_hp():
        dve.wait_ge(S.hp_done, CH)
        for c in range(CH):
            ins = V.tensor_copy(T.hp[:, c, :, 0:HD1],
                                R.flat[:, 2048 + c * DIM:2048 + (c + 1) * DIM].rearrange("p (h d) -> p h d", h=HEADS1))
        ins.then_inc(S.hp_ready, 1)

    for n in range(CH):
        masked(n)
    dve.wait_ge(S.ed_done, 1)
    V.tensor_copy(T.ed[:, :, :].rearrange("p c h -> p (c h)"), R.flat[:, 3584:3584 + CH * HEADS1]).then_inc(S.ed_ready, 1)
    bounds(0)
    for j in range(HEADS1 * CH):
        if j + CH < HEADS1 * CH:
            masked(j + CH)
            if j % CH == CH - 1:
                bounds(j // CH + 1)
        if j >= 1:
            larger(j - 1)
        if j == CH + GATHER_LAG:
            take_hp()
        if j >= 2 * CH and j % CH == CH - 1:
            normalise(j // CH - 2)
    larger(HEADS1 * CH - 1)
    for h in range(2, HEADS1):
        normalise(h)
    dve.wait_ge(S.x3_ready, HEADS1)

    ln(3)
    xT(4)
    dve.wait_ge(S.w4_in, W4_LOADS)
    V.tensor_scalar(T.temp[:, 1, :], T.temp[:, 0, :], 0.1, 5.0, ALU.max, ALU.min).then_inc(S.temp_step, 1)
    V.tensor_scalar(T.tcol[:, 1, :], T.tcol[:, 0, :], 0.1, 5.0, ALU.max, ALU.min).then_inc(S.temp_step, 1)
    dve.wait_ge(S.temp_step, 1)
    V.reciprocal(T.temp[:, 0, :], T.temp[:, 1, :]).then_inc(S.temp_step, 1)
    dve.wait_ge(S.temp_step, 2)
    V.reciprocal(T.tcol[:, 2, :], T.tcol[:, 1, :]).then_inc(S.temp_ready, 1)

    def per_head(t):
        return t.rearrange("p (h g) -> p h g", h=HEADS2)

    def over_slices(t, rows=P):
        return t.unsqueeze(2).to_broadcast([rows, HEADS2, SLICES])

    dve.wait_ge(S.temp_ready, 1)
    V.tensor_tensor(T.bxt[:, :], T.bx[:, :], T.tcol[:, 2, :], ALU.mult).then_inc(S.temp_ready, 1)
    dve.wait_ge(S.temp_step, 3)
    V.tensor_tensor(per_head(T.bst[:, :]), T.bsl[:, :].unsqueeze(1).to_broadcast([P, HEADS2, SLICES]),
                    over_slices(T.temp[:, 0, :]), ALU.mult).then_inc(S.temp_step, 1)
    dve.wait_ge(S.temp_step, 4)

    def off_maximum(c):
        lg = per_head(T.lg[:, c, :])
        hs = slice(c * HEADS2, (c + 1) * HEADS2)
        dve.wait_ge(S.lg_done, c + 1)
        V.tensor_tensor(T.lg[:, c, :], R.banks[:, 6 + c % 2, :], T.bst[:, :], ALU.add).then_inc(S.lg_step, 1)
        dve.wait_ge(S.lg_step, 3 * c + 1)
        V.tensor_reduce(T.sm[:, 0, hs], lg, AX.X, ALU.max).then_inc(S.lg_step, 1)
        dve.wait_ge(S.lg_step, 3 * c + 2)
        V.tensor_tensor(lg, lg, over_slices(T.sm[:, 0, hs]), ALU.subtract).then_inc(S.lg_step, 1)

    def sums(c):
        hs = slice(c * HEADS2, (c + 1) * HEADS2)
        dve.wait_ge(S.sm_exp, c + 1)
        V.tensor_reduce(T.sm[:, 1, hs], per_head(T.sw[:, c, :]), AX.X, ALU.add).then_inc(S.sm_ready, 1)
        dve.wait_ge(S.sm_ready, 2 * c + 1)
        V.reciprocal(T.sm[:, 2, hs], T.sm[:, 1, hs]).then_inc(S.sm_ready, 1)
        dve.wait_ge(S.fx_done, c + 1)
        V.tensor_tensor(T.fx[:, c, :, 0:HD2], per_head(R.banks[:, 4 + c % 2, :]), per_head(T.bfx[:, :]), ALU.add).then_inc(S.fx_ready, 1)

    for c in range(CH):
        off_maximum(c)
        if c:
            sums(c - 1)
    sums(CH - 1)
    dve.wait_ge(S.tok_done, 1)
    toks = R.banks[0:SLICES, 0:2, 0:4 * (HD2 + 1)].rearrange("p b (h d) -> p b h d", h=4)

    def by_four(t):
        return t.rearrange("p (b h) -> p b h", b=2)

    V.tensor_scalar(by_four(T.nrm[:, 0, :]), toks[:, :, :, HD2], 1e-5, None, ALU.add).then_inc(S.tok_step, 1)
    dve.wait_ge(S.tok_step, 1)
    V.reciprocal(T.nrm[:, 1, :], T.nrm[:, 0, :]).then_inc(S.tok_step, 1)
    dve.wait_ge(S.tok_step, 2)
    for b in range(2):
        ins = V.tensor_tensor(T.tokT[:, b * 4 * HD2:(b + 1) * 4 * HD2].rearrange("p (h d) -> p h d", h=4),
                              toks[:, b, :, 0:HD2],
                              T.nrm[:, 1, b * 4:(b + 1) * 4].unsqueeze(2).to_broadcast([SLICES, 4, HD2]), ALU.mult)
    ins.then_inc(S.tokT_ready, 1)
    dve.wait_ge(S.al_done, 1)
    al = per_head(R.flat[0:SLICES, 512:512 + INNER])
    V.tensor_reduce(T.ats[:, 0, :], al, AX.X, ALU.max).then_inc(S.al_step, 1)
    dve.wait_ge(S.al_step, 1)
    V.tensor_tensor(per_head(T.at[:, 0, :]), al, over_slices(T.ats[:, 0, :], SLICES), ALU.subtract).then_inc(S.al_step, 1)
    dve.wait_ge(S.al_exp, 1)
    V.tensor_reduce(T.ats[:, 1, :], per_head(T.at[:, 1, :]), AX.X, ALU.add).then_inc(S.al_step, 1)
    dve.wait_ge(S.al_step, 3)
    V.reciprocal(T.ats[:, 2, :], T.ats[:, 1, :]).then_inc(S.al_step, 1)
    dve.wait_ge(S.al_step, 4)
    V.tensor_tensor(per_head(T.at[:, 2, :]), per_head(T.at[:, 1, :]), over_slices(T.ats[:, 2, :], SLICES),
                    ALU.mult).then_inc(S.at_ready, 1)
    for c in range(CH):
        V.tensor_tensor(T.X[:, c, :], T.X[:, c, :], T.bout[:, :], ALU.add).then_inc(S.o3_step, 1)
    dve.wait_ge(S.vo_done, 2)
    V.tensor_copy(T.vo[:, 4:8, :].rearrange("p h n -> p (h n)"), R.flat[0:SLICES, 2048:3072]).then_inc(S.vo_ready, 1)
    dve.wait_ge(S.M_done, 2)
    V.tensor_copy(T.M[:, 2:4, :].rearrange("p b n -> p (b n)"), R.flat[:, 3584:4096]).then_inc(S.M_ready, 1)
    dve.wait_ge(S.o3_step, 3 * HEADS1 + CH)
    for c in range(CH):
        dve.wait_ge(S.out4_done, c + 1)
        V.tensor_tensor(T.X[:, c, :], T.X[:, c, :], R.banks[:, 1 + c, 0:DIM],
                        ALU.add).then_inc(S.y_ready, 1)


FIT_BELOW = WIN


NAMES = ["x", "src", "dst", "edge_type_8", "L0_gnn_W1", "L0_gnn_self_w1", "L0_gnn_b1", "L0_gnn_W2", "L0_gnn_self_w2",
         "L0_gnn_b2", "L0_ffn_bg", "L0_ffn_b2", "L1_gnn_W", "L1_ffn_W_fx", "L1_ffn_b_fx", "L1_ffn_W_x",
         "L1_ffn_W_slice", "L1_ffn_b_slice", "L1_ffn_W_q", "L1_ffn_W_k", "L1_ffn_W_v", "L1_ffn_W_out", "L1_ffn_b_out"]


def laid_out(inputs):
    import numpy as np

    a = {n: np.asarray(inputs[n]) for n in NAMES}
    a["wgT"] = np.asarray(inputs["L0_ffn_Wg"]).T
    a["w1T"] = np.asarray(inputs["L0_ffn_W1"]).transpose(0, 2, 1)
    a["w2T"] = np.asarray(inputs["L0_ffn_W2"]).transpose(0, 2, 1)
    a["b1T"] = np.asarray(inputs["L0_ffn_b1"]).reshape(EXPERTS * HB, P).T
    a["asrcT"] = np.asarray(inputs["L1_gnn_a_src"]).reshape(KD, P).T
    a["adstT"] = np.asarray(inputs["L1_gnn_a_dst"]).reshape(KD, P).T
    a["bxT"] = np.asarray(inputs["L1_ffn_b_x"]).reshape(IB, P).T
    a["tcolT"] = np.repeat(np.asarray(inputs["L1_ffn_temperature"]).reshape(-1), HD2).reshape(IB, P).T
    a["temp"] = np.asarray(inputs["L1_ffn_temperature"]).reshape(-1)
    return {n: np.ascontiguousarray(v) for n, v in a.items()}


def kernel(**inputs):
    import concourse.bacc as bacc
    from concourse.bass_utils import run_bass_kernel_spmd

    arrays = laid_out(inputs)
    nc = bacc.Bacc("TRN2", target_bir_lowering=False, num_devices=1)
    D = namedtuple("Inputs", arrays)(*[
        nc.dram_tensor(f"in_{n}", v.shape, mybir.dt.from_np(v.dtype), kind="ExternalInput").ap()
        for n, v in arrays.items()])
    out = nc.dram_tensor("out_0", (NODES, DIM), F32, kind="ExternalOutput").ap()
    program(nc, D, out)
    r = run_bass_kernel_spmd(nc, [{f"in_{n}": v for n, v in arrays.items()}], core_ids=[0])
    return r.results[0]["out_0"]
```
